# Optimizing a Trainium2 kernel written in Bass

```python
import numpy as np
import jax
import jax.numpy as jnp

def _softmax(x, axis=-1):
    return jax.nn.softmax(x, axis=axis)

def _gelu(x):
    return jax.nn.gelu(x, approximate=True)

def _silu(x):
    return jax.nn.silu(x)

def _sigmoid(x):
    return jax.nn.sigmoid(x)

def _layernorm(x, axis=-1, eps=1e-05):
    m = jnp.mean(x, axis=axis, keepdims=True)
    v = jnp.var(x, axis=axis, keepdims=True)
    return (x - m) / jnp.sqrt(v + eps)

def _scatter_add(tgt, idx, src, axis=0):
    return tgt.at[idx].add(src)

def _segment_sum(src, seg, n):
    return jax.ops.segment_sum(src, seg, n)
kernel_name = 'mk_conv_attn_hybrid_d2_conv_nchw384_r4_64b4a9'

def setup_inputs(seed: int=0):
    np.random.seed(seed)
    _w = jnp.asarray

    def _rec_inputs():
        import jax
        import jax.numpy as jnp
        _gk = jax.random.key(seed)
        x = 7.572e-06 + 1 * jax.random.normal(jax.random.fold_in(_gk, 1), (32, 96, 28, 28), jnp.float32)
        return x
    x = _rec_inputs()

    def _L0_conv_setup():
        import jax, jax.numpy as jnp
        import numpy as np
        B, C, H, W = (32, 96, 28, 28)
        E, HID, K = (4, 96, 2)
        key = jax.random.key(seed)
        ks = jax.random.split(key, 5)
        x = jax.random.normal(ks[0], (B, C, H, W), jnp.float32)
        gate_w = jax.random.normal(ks[1], (C, E), jnp.float32) * 0.02
        gate_b = jnp.zeros((E,), jnp.float32)
        w1 = jax.random.normal(ks[2], (E, HID, C), jnp.float32) * 0.02
        b1 = jnp.zeros((E, HID), jnp.float32)
        w2 = jax.random.normal(ks[3], (E, C, HID), jnp.float32) * 0.02
        b2 = jnp.zeros((E, C), jnp.float32)
        return {'x': x, 'gate_w': gate_w, 'gate_b': gate_b, 'w1': w1, 'b1': b1, 'w2': w2, 'b2': b2}
    _L0_conv_all = _L0_conv_setup()
    _L0_conv_in = {k: v for k, v in _L0_conv_all.items() if k in ('gate_w', 'gate_b', 'w1', 'b1', 'w2', 'b2')}
    del _L0_conv_all

    def _L1_attn_setup():
        import jax, jax.numpy as jnp
        import numpy as np
        import math
        NUM_HEADS = 12
        LAMBDA_INIT = 0.8 - 0.6 * math.exp(-0.3 * (2 - 1))
        SIGMA = 0.5

        def _feature_map(t):
            return jnp.where(t >= 0, t + 1.0, jnp.exp(t))
        key = jax.random.key(seed)
        ks = jax.random.split(key, 9)
        B_, N, C, H = (512, 16, 96, NUM_HEADS)
        d = C // H
        s = 0.02
        return {'x': jax.random.normal(ks[0], (B_, N, C), dtype=jnp.float32), 'qkv_w': jax.random.normal(ks[1], (C, 3 * C), dtype=jnp.float32) * s, 'qkv_b': jax.random.normal(ks[2], (3 * C,), dtype=jnp.float32) * s, 'proj_w': jax.random.normal(ks[3], (C, C), dtype=jnp.float32) * s, 'proj_b': jax.random.normal(ks[4], (C,), dtype=jnp.float32) * s, 'lambda_k1': jax.random.normal(ks[5], (H, d), dtype=jnp.float32) * 0.1, 'lambda_v1': jax.random.normal(ks[6], (H, d), dtype=jnp.float32) * 0.1, 'lambda_k2': jax.random.normal(ks[7], (H, d), dtype=jnp.float32) * 0.1, 'lambda_v2': jax.random.normal(ks[8], (H, d), dtype=jnp.float32) * 0.1}
    _L1_attn_all = _L1_attn_setup()
    _L1_attn_in = {k: v for k, v in _L1_attn_all.items() if k in ('qkv_w', 'qkv_b', 'proj_w', 'proj_b', 'lambda_k1', 'lambda_v1', 'lambda_k2', 'lambda_v2')}
    del _L1_attn_all

    def _L1_ffn_setup():
        import jax, jax.numpy as jnp
        import numpy as np
        NUM_GROUPS = 5
        EPS = 1e-05
        QB = 128.0

        def _binarize_weights_groupwise(W):
            n_out = W.shape[0]
            gs = n_out // NUM_GROUPS
            Wb = jnp.zeros_like(W)
            for g in range(NUM_GROUPS):
                wg = W[g * gs:(g + 1) * gs]
                z = wg - wg.mean()
                ste = z + jax.lax.stop_gradient(jnp.sign(z) - z)
                Wb = Wb.at[g * gs:(g + 1) * gs].set(ste)
            return Wb

        def _quantize_activations_groupwise(x):
            n = x.shape[0]
            gs = n // NUM_GROUPS
            xq = jnp.zeros_like(x)
            for g in range(NUM_GROUPS):
                ag = x[g * gs:(g + 1) * gs]
                gamma = jnp.max(jnp.abs(ag))
                xq = xq.at[g * gs:(g + 1) * gs].set(jnp.clip(ag * QB / (gamma + EPS), -QB + EPS, QB - EPS))
            return xq

        def _bitlinear(x, W, b):
            Wb = _binarize_weights_groupwise(W)
            y = jnp.einsum('btc,oc->bto', x, Wb) + b
            return _quantize_activations_groupwise(y)
        key = jax.random.key(seed)
        k1, k2, k3, k4, k5 = jax.random.split(key, 5)
        B, T, C = (10, 512, 96)
        H = 4 * C
        lim1 = 1.0 / np.sqrt(C)
        lim2 = 1.0 / np.sqrt(H)
        x = jax.random.normal(k1, (B, T, C), dtype=jnp.float32)
        W1 = jax.random.uniform(k2, (H, C), minval=-lim1, maxval=lim1, dtype=jnp.float32)
        b1 = jax.random.uniform(k3, (H,), minval=-lim1, maxval=lim1, dtype=jnp.float32)
        W2 = jax.random.uniform(k4, (C, H), minval=-lim2, maxval=lim2, dtype=jnp.float32)
        b2 = jax.random.uniform(k5, (C,), minval=-lim2, maxval=lim2, dtype=jnp.float32)
        return {'x': x, 'W1': W1, 'b1': b1, 'W2': W2, 'b2': b2}
    _L1_ffn_all = _L1_ffn_setup()
    _L1_ffn_in = {k: v for k, v in _L1_ffn_all.items() if k in ('W1', 'b1', 'W2', 'b2')}
    del _L1_ffn_all
    return {'x': x, 'L0_conv_gate_w': _L0_conv_in['gate_w'], 'L0_conv_gate_b': _L0_conv_in['gate_b'], 'L0_conv_w1': _L0_conv_in['w1'], 'L0_conv_b1': _L0_conv_in['b1'], 'L0_conv_w2': _L0_conv_in['w2'], 'L0_conv_b2': _L0_conv_in['b2'], 'L1_attn_qkv_w': _L1_attn_in['qkv_w'], 'L1_attn_qkv_b': _L1_attn_in['qkv_b'], 'L1_attn_proj_w': _L1_attn_in['proj_w'], 'L1_attn_proj_b': _L1_attn_in['proj_b'], 'L1_attn_lambda_k1': _L1_attn_in['lambda_k1'], 'L1_attn_lambda_v1': _L1_attn_in['lambda_v1'], 'L1_attn_lambda_k2': _L1_attn_in['lambda_k2'], 'L1_attn_lambda_v2': _L1_attn_in['lambda_v2'], 'L1_ffn_W1': _L1_ffn_in['W1'], 'L1_ffn_b1': _L1_ffn_in['b1'], 'L1_ffn_W2': _L1_ffn_in['W2'], 'L1_ffn_b2': _L1_ffn_in['b2']}

def reference(x, L0_conv_gate_w, L0_conv_gate_b, L0_conv_w1, L0_conv_b1, L0_conv_w2, L0_conv_b2, L1_attn_qkv_w, L1_attn_qkv_b, L1_attn_proj_w, L1_attn_proj_b, L1_attn_lambda_k1, L1_attn_lambda_v1, L1_attn_lambda_k2, L1_attn_lambda_v2, L1_ffn_W1, L1_ffn_b1, L1_ffn_W2, L1_ffn_b2):
    import jax
    import jax.numpy as jnp

    def _L0_conv_ref(x, gate_w, gate_b, w1, b1, w2, b2):
        import jax, jax.numpy as jnp
        import numpy as np
        B, C, H, W = (32, 96, 28, 28)
        E, HID, K = (4, 96, 2)
        b, c, h, w = x.shape
        e = gate_b.shape[0]
        x_flat = x.transpose(0, 2, 3, 1).reshape(-1, c)
        scores = jax.nn.softmax(x_flat @ gate_w + gate_b, -1)
        top_v, top_i = jax.lax.top_k(scores, K)
        top_w = jax.nn.softmax(top_v, -1)
        wmap = top_w.T.reshape(K, b, h, w)
        present = (top_i[:, :, None] == jnp.arange(e)[None, None, :]).any(0)
        coef = jnp.einsum('ke,kbhw->ebhw', present.astype(x.dtype), wmap)
        hdn = jax.nn.relu(jnp.einsum('bchw,edc->ebdhw', x, w1) + b1[:, None, :, None, None])
        y = jnp.einsum('ebdhw,eod->ebohw', hdn, w2) + b2[:, None, :, None, None]
        out = jnp.einsum('ebohw,ebhw->bohw', y, coef)
        return out

    def _L1_attn_ref(x, qkv_w, qkv_b, proj_w, proj_b, lambda_k1, lambda_v1, lambda_k2, lambda_v2):
        import jax, jax.numpy as jnp
        import numpy as np
        import math
        NUM_HEADS = 12
        LAMBDA_INIT = 0.8 - 0.6 * math.exp(-0.3 * (2 - 1))
        SIGMA = 0.5

        def _feature_map(t):
            return jnp.where(t >= 0, t + 1.0, jnp.exp(t))
        B_, N, C = x.shape
        H = NUM_HEADS
        d = C // H
        scale = d ** (-0.5)
        qkv = (x @ qkv_w + qkv_b).reshape(B_, N, 3, H, d).transpose(2, 0, 3, 1, 4)
        q, k, v = (qkv[0], qkv[1], qkv[2])
        q = q * scale
        lam1 = jnp.exp(jnp.sum(lambda_k1 * lambda_v1, axis=-1))
        lam2 = jnp.exp(jnp.sum(lambda_k2 * lambda_v2, axis=-1))
        lambda_full = lam1 - lam2 + LAMBDA_INIT
        fk = _feature_map(jnp.swapaxes(k, -1, -2))
        fv = _feature_map(v)
        idx = jnp.arange(d, dtype=jnp.float32)
        gauss = jnp.exp(-(idx[:, None] - idx[None, :]) ** 2 / (2.0 * SIGMA ** 2))
        A = jnp.einsum('bhdn,bhne->bhde', fk, fv) * gauss
        attn = A - lambda_full[None, :, None, None] * A
        out = jnp.einsum('bhnd,bhde->bhne', q, attn)
        out = jnp.swapaxes(out, 1, 2).reshape(B_, N, C)
        return out @ proj_w + proj_b

    def _L1_ffn_ref(x, W1, b1, W2, b2):
        import jax, jax.numpy as jnp
        import numpy as np
        NUM_GROUPS = 5
        EPS = 1e-05
        QB = 128.0

        def _binarize_weights_groupwise(W):
            n_out = W.shape[0]
            gs = n_out // NUM_GROUPS
            Wb = jnp.zeros_like(W)
            for g in range(NUM_GROUPS):
                wg = W[g * gs:(g + 1) * gs]
                z = wg - wg.mean()
                ste = z + jax.lax.stop_gradient(jnp.sign(z) - z)
                Wb = Wb.at[g * gs:(g + 1) * gs].set(ste)
            return Wb

        def _quantize_activations_groupwise(x):
            n = x.shape[0]
            gs = n // NUM_GROUPS
            xq = jnp.zeros_like(x)
            for g in range(NUM_GROUPS):
                ag = x[g * gs:(g + 1) * gs]
                gamma = jnp.max(jnp.abs(ag))
                xq = xq.at[g * gs:(g + 1) * gs].set(jnp.clip(ag * QB / (gamma + EPS), -QB + EPS, QB - EPS))
            return xq

        def _bitlinear(x, W, b):
            Wb = _binarize_weights_groupwise(W)
            y = jnp.einsum('btc,oc->bto', x, Wb) + b
            return _quantize_activations_groupwise(y)
        h = _bitlinear(x, W1, b1)
        h = jax.nn.gelu(h, approximate=False)
        out = _bitlinear(h, W2, b2)
        return out

    def _gn(v, G=32, eps=1e-05):
        B_, C_, H_, W_ = v.shape
        g = v.reshape(B_, G, C_ // G, H_, W_)
        m = jnp.mean(g, axis=(2, 3, 4), keepdims=True)
        s = jnp.var(g, axis=(2, 3, 4), keepdims=True)
        return ((g - m) / jnp.sqrt(s + eps)).reshape(v.shape)

    def _ln_c(v, eps=1e-06):
        m = jnp.mean(v, axis=1, keepdims=True)
        s = jnp.var(v, axis=1, keepdims=True)
        return (v - m) / jnp.sqrt(s + eps)

    def _ln_t(v, eps=1e-05):
        m = jnp.mean(v, axis=-1, keepdims=True)
        s = jnp.var(v, axis=-1, keepdims=True)
        return (v - m) / jnp.sqrt(s + eps)

    def _to_tokens(v):
        B_, C_, H_, W_ = v.shape
        return v.reshape(B_, C_, H_ * W_).transpose(0, 2, 1)

    def _from_tokens(t, like):
        B_, C_, H_, W_ = like.shape
        return t.transpose(0, 2, 1).reshape(B_, C_, H_, W_)
    x = x + _L0_conv_ref(_gn(x), L0_conv_gate_w, L0_conv_gate_b, L0_conv_w1, L0_conv_b1, L0_conv_w2, L0_conv_b2)
    t = _to_tokens(x)
    t = t + _L1_attn_ref(_ln_t(t), L1_attn_qkv_w, L1_attn_qkv_b, L1_attn_proj_w, L1_attn_proj_b, L1_attn_lambda_k1, L1_attn_lambda_v1, L1_attn_lambda_k2, L1_attn_lambda_v2)
    t = t + _L1_ffn_ref(_ln_t(t), L1_ffn_W1, L1_ffn_b1, L1_ffn_W2, L1_ffn_b2)
    x = _from_tokens(t, x)
    return x

_drawn_inputs = setup_inputs


def setup_inputs(seed=0):
    import zlib

    import numpy as np

    out = dict(_drawn_inputs(seed))
    spreads = {'L0_conv_gate_b': (0.0, 0.8), 'L0_conv_b1': (0.0, 0.297), 'L0_conv_b2': (0.0, 0.1)}
    factors = {'L0_conv_gate_w': 8.0, 'L1_attn_proj_b': 8.0, 'L1_ffn_b1': 8.0, 'L1_ffn_b2': 8.0}
    for name, (base, spread) in spreads.items():
        noise = np.random.default_rng([zlib.crc32(name.encode()), seed]).standard_normal(out[name].shape)
        drawn = base * np.exp(spread * noise) if base else spread * noise
        out[name] = jnp.asarray(drawn.astype(out[name].dtype))
    for name, factor in factors.items():
        out[name] = (out[name] * factor).astype(out[name].dtype)
    return out
```

```python
from contextlib import ExitStack

import numpy as np

import concourse.bass as bass
from concourse import mybir

ALU = mybir.AluOpType
ACT = mybir.ActivationFunctionType
AX = mybir.AxisListType
F32 = mybir.dt.float32
F16 = mybir.dt.float16
BF16 = mybir.dt.bfloat16

P = 128
BATCH, C, HW = 32, 96, 784
HALF = HW // 2
TOK = 112
CHUNKS = HW // TOK
CH_A = 4
E = 4
HID = E * C
TILES = HID // P
HEADS, HD = 12, 8
GN_GROUPS = 32
GN_C = C // GN_GROUPS
SLAB = 8
SLABS = BATCH // SLAB
QGROUPS = 5
QB = BATCH // QGROUPS
QIMAGES = QGROUPS * QB
W1_GS = HID // QGROUPS
W2_GS = C // QGROUPS
QMAX = 128.0
Q_EPS = 1e-5
Q_CLIP = float(np.float32(QMAX - Q_EPS))
GN_EPS = 1e-5
LN_EPS = 1e-5
LAMBDA_INIT = 0.8 - 0.6 * float(np.exp(-0.3))
SIGMA = 0.5
PARTS = 3

K_ID, K_GAUSS, K_HEAD, K_GROUP, K_EXPERT, K_PART, K_PART96, K_END = np.cumsum(
    [0, P, C, C, C, TILES * E, PARTS, PARTS]).tolist()


def shape_constants():
    k = np.zeros((P, K_END), np.float32)
    k[:, K_ID:K_ID + P] = np.eye(P)
    row = np.arange(C)
    same_head = row[:, None] // HD == row[None, :] // HD
    dist = (row[:, None] % HD - row[None, :] % HD).astype(np.float32)
    k[:C, K_GAUSS:K_GAUSS + C] = np.exp(-dist ** 2 / (2.0 * SIGMA ** 2)) * same_head
    k[:C, K_HEAD:K_HEAD + C] = same_head
    k[:C, K_GROUP:K_GROUP + C] = (row[:, None] // GN_C == row[None, :] // GN_C) / np.float32(GN_C)
    for t in range(TILES):
        for e in range(E):
            k[:, K_EXPERT + t * E + e] = (np.arange(P) + t * P) // C == e
    for n in range(PARTS):
        k[n, K_PART + n] = 1.0
        k[C + n, K_PART96 + n] = 1.0
    return k


def wait_count(eng, sem, count):
    if isinstance(count, int) and count <= 0:
        return
    eng.wait_ge(sem, count)


def wait_apart(eng, sem, count, passed):
    eng.wait_ge(sem, count)
    eng.sem_inc(passed, 1)


def build(nc, x, gate_w, gate_b, w1, b1, w2, b2, qkv_w, qkv_b, proj_w, proj_b,
          lk1, lv1, lk2, lv2, W1, fb1, W2, fb2, consts, out):
    with ExitStack() as ctx:
        def sb(name, shape, dt=F32):
            return ctx.enter_context(nc.sbuf_tensor(name, shape, dt))

        def sem(name):
            return ctx.enter_context(nc.semaphore(name))

        ctx.enter_context(nc.allow_non_contiguous_dma(reason="small parameter columns"))
        ctx.enter_context(nc.allow_low_precision(reason="float32 carried as exact parts"))

        S = [ctx.enter_context(nc.psum_tensor(f"slot{k}", [P, 2, 512], F32)) for k in range(4)]

        def halves(k, rows):
            return S[k][0:rows, :, 0:HALF]

        def flat(k):
            return S[k][:, :, :].rearrange("p a b -> p (a b)")

        def chunks(k, n, width, used):
            return flat(k)[0:TOK, 0:n * width].rearrange("p (j c) -> p j c", c=width)[:, :, 0:used]

        con = sb("con", [P, K_END])
        ident = con[:, K_ID:K_ID + P]
        w1_raw = sb("w1_raw", [C, E, C])
        w2_raw = sb("w2_raw", [C, E, C])
        w1T = sb("w1T", [C, HID])
        b1c = sb("b1c", [P, TILES])
        w2T = sb("w2T", [P, TILES, C])
        w2s = sb("w2s", [P, TILES, 2 * C])
        b2all = sb("b2all", [P, E, C])
        bias2 = sb("bias2", [P, 2, C])
        bias2_parts = sb("bias2_parts", [P, 2, 2, C], BF16)
        ones_b = sb("ones_b", [P, TOK], BF16)
        ones_f = sb("ones_f", [P, P])
        gw = sb("gw", [C, E])
        gb = sb("gb", [TOK, E])
        qkvw = sb("qkvw", [C + 1, 3 * C])
        wqT = sb("wqT", [C, C + 1])
        projw = sb("projw", [C, C])
        projb = sb("projb", [C + 1, C])
        lam = sb("lam", [C, 4])
        lam_e = sb("lam_e", [C, 4])
        gauss = sb("gauss", [C, C])
        W1_raw = sb("W1_raw", [P, TILES, C])
        W1f = sb("W1f", [C, HID])
        W1b = sb("W1b", [C + PARTS, HID], BF16)
        fb1r = sb("fb1r", [C + PARTS, HID])
        W2_raw = sb("W2_raw", [C, HID])
        W2f = sb("W2f", [P, TILES, C])
        W2b = sb("W2b", [P, TILES, C], BF16)
        fb2c = sb("fb2c", [C, 1])
        wsum = sb("wsum", [P, 2, QGROUPS])
        wmean = sb("wmean", [P, 2, QGROUPS])
        part_a = sb("part_a", [P, HID])
        part_b = sb("part_b", [P, HID])
        part_h = sb("part_h", [P, HID], BF16)
        minus_one = sb("minus_one", [TOK, 1])
        ln_eps = sb("ln_eps", [TOK, CHUNKS])
        pow_half = sb("pow_half", [P, 2 * SLAB])

        big = sb("big", [C + PARTS, BATCH, 2, HW], F16)
        x_all = big[0:C, :, :, :].rearrange("p b s n -> p (b s n)").bitcast(F32).rearrange(
            "p (b n) -> p b n", n=HW)
        y2_all = x_all
        stage = sb("stage", [P, SLAB * HW])
        gn_scale = sb("gn_scale", [C, BATCH])
        gn_shift = sb("gn_shift", [C, BATCH])
        w0 = sb("w0", [TOK, BATCH * CHUNKS])
        ymax = sb("ymax", [P, QIMAGES * TILES])
        y2max = sb("y2max", [C, QIMAGES])

        xn_slab = stage[0:C, :].rearrange("p (j n) -> p j n", n=HW)
        gn_st = sb("gn_st", [C, SLAB, 2, 6])
        gn_mv = sb("gn_mv", [C, SLAB, 2])
        gn_avg = sb("gn_avg", [C, SLAB, 2])
        gn_dev = sb("gn_dev", [C, SLAB])
        gn_dev2 = sb("gn_dev2", [C, SLAB])
        gn_var = sb("gn_var", [C, SLAB])
        NT = BATCH * CHUNKS
        hT = sb("hT", [P, TILES, HW])
        logits = hT[0:TOK, :, :].rearrange("p t n -> p (t n)")[:, 0:NT * E].rearrange("p (n e) -> p n e", e=E)
        top = sb("top", [TOK, 4, NT])
        present = sb("present", [TOK, 2, E])
        flags = sb("flags", [P, 2, E])
        flag_tmp = sb("flag_tmp", [P, TILES, E])
        row_flag = sb("row_flag", [P, 2, TILES])
        prefer = sb("prefer", [TOK, E])

        xs = [sb(f"xs{r}", [C, HW]) for r in range(2)]
        xn = [sb(f"xn{r}", [C, HW]) for r in range(2)]
        tmp = stage[0:TOK, 4 * CHUNKS * C:5 * CHUNKS * C].rearrange("p (j c) -> p j c", c=C)
        t1 = [sb(f"t1_{r}", [TOK, CHUNKS, C]) for r in range(2)]
        t2 = sb("t2", [TOK, CHUNKS, C])
        ln_st = sb("ln_st", [TOK, CHUNKS, 6])
        ln_mv = [sb(f"ln_mv{n}", [TOK, CHUNKS, 2]) for n in range(2)]
        ln_ve = [sb(f"ln_ve{n}", [TOK, CHUNKS]) for n in range(2)]
        ln_rs = [sb(f"ln_rs{n}", [TOK, CHUNKS]) for n in range(2)]
        xh1 = sb("xh1", [TOK, CHUNKS, C])
        xh2 = sb("xh2", [TOK, CHUNKS, C])
        xh1T = sb("xh1T", [C + 1, HW])
        ekv = stage[0:TOK, 0:CHUNKS * 2 * C].rearrange("p (j c) -> p j c", c=2 * C)
        fkv = stage[0:TOK, CHUNKS * 2 * C:2 * CHUNKS * 2 * C].rearrange("p (j c) -> p j c", c=2 * C)
        Am = sb("Am", [C, C])
        St = sb("St", [C, C + 1])
        R = sb("R", [C + 1, C])
        t2T = [sb(f"t2T{r}", [C, HW]) for r in range(2)]

        def gel_buf(r, t):
            return hT[:, (3 * r + t) % 2, :]

        stage16 = stage[:, :].bitcast(F16)
        SPL = TILES * HW
        h_hi = [stage16[:, (2 * r) * SPL:(2 * r + 1) * SPL].rearrange("p (t n) -> p t n", t=TILES) for r in range(2)]
        h_lo = [stage16[:, (2 * r + 1) * SPL:(2 * r + 2) * SPL].rearrange("p (t n) -> p t n", t=TILES) for r in range(2)]
        tc_buf = xs
        qv = xn
        gmax1 = sb("gmax1", [P, QGROUPS])
        gcol = sb("gcol", [QGROUPS, 1])
        gdiag = sb("gdiag", [QGROUPS, QGROUPS])
        s1 = sb("s1", [P, QGROUPS])
        s1e = sb("s1e", [P, QGROUPS])
        gmax2 = sb("gmax2", [C, 1])
        g2one = sb("g2one", [1, 1])
        s2e = sb("s2e", [C, 1])
        s2 = sb("s2", [C, QGROUPS])

        act_passed = sem("act_passed")
        dve_passed = sem("dve_passed")
        params_loaded = sem("params_loaded")
        x_loaded = [sem(f"x_loaded{r}") for r in range(2)]
        ones_ready = sem("ones_ready")
        bigones_ready = sem("bigones_ready")
        setup_T = sem("setup_T")
        setup_dve = sem("setup_dve")
        fold_in = sem("fold_in")
        wsum_ready = sem("wsum_ready")
        lam_prod = sem("lam_prod")
        lam_sum = sem("lam_sum")
        lam_exp = sem("lam_exp")
        wmean_sum = sem("wmean_sum")
        gn_stats = sem("gn_stats")
        gn_mv_ready = sem("gn_mv_ready")
        gn_group = sem("gn_group")
        gn_avg_ready = sem("gn_avg_ready")
        gn_dev_ready = sem("gn_dev_ready")
        gn_dev2_ready = sem("gn_dev2_ready")
        gn_between = sem("gn_between")
        gn_var_ready = sem("gn_var_ready")
        gn_rstd = sem("gn_rstd")
        gn_coef = sem("gn_coef")
        xn_slab_ready = sem("xn_slab_ready")
        gates_done = sem("gates_done")
        logits_ready = sem("logits_ready")
        gate_exp_in = sem("gate_exp_in")
        gate_exp = sem("gate_exp")
        top_exp = sem("top_exp")
        present_ready = sem("present_ready")
        counts_ready = sem("counts_ready")
        conv_ready = sem("conv_ready")

        xs_loaded = [sem(f"xs_loaded{r}") for r in range(2)]
        xn_ready = sem("xn_ready")
        z_ready = sem("z_ready")
        h_ready = sem("h_ready")
        yx_ready = sem("yx_ready")
        tmp_ready = sem("tmp_ready")
        t1_ready = sem("t1_ready")
        ln_stats = sem("ln_stats")
        ln_mean = [sem("ln1_mean"), sem("ln2_mean")]
        ln_var = [sem("ln1_var"), sem("ln2_var")]
        ln_rstd = [sem("ln1_rstd"), sem("ln2_rstd")]
        xh1_ready = sem("xh1_ready")
        xh2_ready = sem("xh2_ready")
        x1T_ready = sem("x1T_ready")
        xh1T_ready = sem("xh1T_ready")
        kv_ready = sem("kv_ready")
        e_ready = sem("e_ready")
        f_ready = sem("f_ready")
        a_ready = sem("a_ready")
        am_ready = sem("am_ready")
        stp_ready = sem("stp_ready")
        st_ready = sem("st_ready")
        rp_ready = sem("rp_ready")
        r_ready = sem("r_ready")
        ao_ready = sem("ao_ready")
        t2_ready = sem("t2_ready")
        t2p_ready = sem("t2p_ready")
        t2T_evac = sem("t2T_evac")
        t2T_stored = [sem(f"t2T_stored{r}") for r in range(2)]
        x2p_ready = sem("x2p_ready")
        hi_ready = sem("hi_ready")
        lo_ready = sem("lo_ready")
        y_ready = sem("y_ready")
        ymax_done = sem("ymax_done")

        gmax_ready = sem("gmax_ready")
        gmaxT = sem("gmaxT")
        gdiag_ready = sem("gdiag_ready")
        gbc = sem("gbc")
        s1_ready = sem("s1_ready")
        y1_ready = sem("y1_ready")
        gelu_ready = sem("gelu_ready")
        hhi_ready = sem("hhi_ready")
        hlo_ready = sem("hlo_ready")
        y2_ready = sem("y2_ready")
        y2_evac = sem("y2_evac")
        y2max_done = sem("y2max_done")
        g2_ready = sem("g2_ready")
        g2T = sem("g2T")
        g2one_ready = sem("g2one_ready")
        g2bc = sem("g2bc")
        s2e_ready = sem("s2e_ready")
        s2_ready = sem("s2_ready")
        tc_loaded = [sem(f"tc_loaded{r}") for r in range(2)]
        qv_ready = sem("qv_ready")
        o_ready = sem("o_ready")
        o_stored = [sem(f"o_stored{r}") for r in range(2)]

        block = ctx.enter_context(nc.Block())

        x_bcn = x.rearrange("b c h w -> b c (h w)")
        out_bcn = out.rearrange("b c h w -> b c (h w)")

        FIRST, LAST = 4, BATCH
        N_PARAMS = 19
        CONSTS_SET = (ones_ready, 11)

        @block.sync
        def _(sp):
            for r in range(2):
                sp.dma_start(x_all[:, 4 * r:4 * r + 4, :],
                             x_bcn[4 * r:4 * r + 4].rearrange("b c n -> c b n")).then_inc(x_loaded[r], 16)
            with sp.Fori(1, SLABS) as s:
                for r in range(2):
                    sp.wait_ge(x_loaded[r], 16 * s)
                    b0 = s * SLAB + 4 * r
                    sp.dma_start(x_all[:, bass.ds(b0, 4), :],
                                 x_bcn[bass.ds(b0, 4)].rearrange("b c n -> c b n")).then_inc(x_loaded[r], 16)
            for r in range(2):
                sp.dma_start(xs[r][:, :], x_bcn[r]).then_inc(xs_loaded[r], 16)

            def step(m, r, load=True):
                i = 2 * m + r
                if load:
                    wait_count(sp, yx_ready, 2 * i + 2)
                    sp.dma_start(xs[r][:, :], x_bcn[i + 2]).then_inc(xs_loaded[r], 16)
                if not isinstance(i, int) or i >= 2:
                    sp.wait_ge(t2T_evac, i - 1)
                    sp.dma_start(out_bcn[i - 2], t2T[r][:, :]).then_inc(t2T_stored[r], 16)

            for m in range(FIRST // 2):
                for r in range(2):
                    step(m, r)
            with sp.Fori(FIRST // 2, LAST // 2 - 1) as m:
                for r in range(2):
                    step(m, r)
            for m in (LAST // 2 - 1, LAST // 2):
                for r in range(2):
                    step(m, r, load=False)
            for r in range(2):
                sp.wait_ge(t2T_stored[r], 16 * (BATCH // 2))

            def load_c(b, m, r):
                wait_count(sp, o_stored[r], 16 * m)
                sp.dma_start(tc_buf[r][:, :], out_bcn[b]).then_inc(tc_loaded[r], 16)

            def store_c(b, m, r):
                sp.wait_ge(o_ready, b + 1)
                sp.dma_start(out_bcn[b], tc_buf[r][:, :]).then_inc(o_stored[r], 16)

            for r in range(2):
                sp.dma_start(tc_buf[r][:, :], out_bcn[r]).then_inc(tc_loaded[r], 16)
            with sp.Fori(0, QIMAGES // 2 - 1) as m:
                for r in range(2):
                    store_c(2 * m + r, m, r)
                for r in range(2):
                    load_c(2 * m + 2 + r, m + 1, r)
            for r in range(2):
                store_c(QIMAGES - 2 + r, QIMAGES // 2 - 1, r)
            for r in range(2):
                sp.wait_ge(o_stored[r], 16 * (QIMAGES // 2))

        @block.gpsimd
        def _(pool):
            nc.gpsimd.memset(ones_b[:, :], 1.0).then_inc(ones_ready, 1)
            nc.gpsimd.memset(ones_f[:, :], 1.0).then_inc(ones_ready, 1)
            nc.gpsimd.memset(minus_one[:, :], -1.0).then_inc(ones_ready, 1)
            nc.gpsimd.memset(ln_eps[:, :], LN_EPS).then_inc(ones_ready, 1)
            nc.gpsimd.memset(pow_half[:, :], -0.5).then_inc(ones_ready, 1)
            nc.gpsimd.memset(projb[:, :], 0.0).then_inc(ones_ready, 1)
            for e in range(E):
                nc.gpsimd.memset(prefer[:, e:e + 1], float(E - e)).then_inc(ones_ready, 1)
            pool.wait_ge(ones_ready, CONSTS_SET[1] - 1)
            nc.gpsimd.memset(xh1T[C:C + 1, :], 1.0).then_inc(ones_ready, 1)
            pool.wait_ge(*CONSTS_SET)
            nc.gpsimd.memset(big[C:C + PARTS, 0:QIMAGES, 0, :], 1.0).then_inc(bigones_ready, 1)
            pool.wait_ge(bigones_ready, 1)
            with pool.Fori(0, SLABS) as s:
                pool.wait_ge(gn_var_ready, s + 1)
                nc.gpsimd.tensor_tensor(gn_scale[:, bass.ds(s * SLAB, SLAB)], gn_var[:, :],
                                        pow_half[0:C, 0:SLAB], ALU.pow).then_inc(gn_rstd, 1)

            def rstd(n, b):
                pool.wait_ge(ln_mean[n], b + 1)
                nc.gpsimd.tensor_tensor(ln_ve[n][:, :], ln_mv[n][:, :, 1], ln_eps[:, :],
                                        ALU.add).then_inc(ln_var[n], 1)
                pool.wait_ge(ln_var[n], b + 1)
                nc.gpsimd.tensor_tensor(ln_rs[n][:, :], ln_ve[n][:, :], pow_half[0:TOK, 0:CHUNKS],
                                        ALU.pow).then_inc(ln_rstd[n], 1)

            def step(i):
                rstd(0, i)
                rstd(1, i - 1)

            rstd(0, 0)
            with pool.Fori(1, LAST) as i:
                step(i)

        @block.scalar
        def _(act):
            def load(dst, src):
                act.dma_start(dst, src).then_inc(params_loaded, 16)

            load(con[:, :], consts)
            load(w1_raw[:, :, :], w1.rearrange("e d c -> d e c"))
            load(w2_raw[:, :, :], w2.rearrange("e o d -> o e d"))
            load(b1c[:, :], b1.rearrange("e d -> (e d)").rearrange("(t p) -> p t", p=P))
            load(b2all[:, :, :], b2.rearrange("(a e) o -> a e o", a=1).to_broadcast([P, E, C]))
            load(gw[:, :], gate_w)
            load(gb[:, :], gate_b.rearrange("(a e) -> a e", a=1).to_broadcast([TOK, E]))
            load(qkvw[0:C, :], qkv_w)
            load(qkvw[C:C + 1, :], qkv_b.rearrange("(a n) -> a n", a=1))
            load(projw[:, :], proj_w)
            for n, l in enumerate((lk1, lv1, lk2, lv2)):
                load(lam[:, n:n + 1], l.rearrange("h (d a) -> (h d) a", a=1))
            load(W1_raw[:, :, :], W1.rearrange("(t p) c -> p t c", p=P))
            load(fb1r[C:C + PARTS, :], fb1.rearrange("(a n) -> a n", a=1).to_broadcast([PARTS, HID]))
            load(W2_raw[:, :], W2)
            load(fb2c[:, :], fb2.rearrange("(c a) -> c a", a=1))
            act.wait_ge(*CONSTS_SET)
            load(projb[C:C + 1, :], proj_b.rearrange("(a n) -> a n", a=1))

            act.wait_ge(params_loaded, 16 * N_PARAMS)
            act.wait_ge(lam_sum, 1)
            nc.scalar.activation(lam_e[:, 0:2], S[2][0:C, 1, 0:2], ACT.Exp).then_inc(lam_exp, 1)

            with act.Fori(0, SLABS) as s:
                wait_apart(act, gn_coef, s + 1, act_passed)
                for j in range(SLAB):
                    b = s * SLAB + j
                    ins = nc.scalar.activation(xn_slab[:, j, :], x_all[:, b, :], ACT.Identity,
                                               scale=gn_scale[:, bass.ds(b, 1)], bias=gn_shift[:, bass.ds(b, 1)])
                ins.then_inc(xn_slab_ready, 1)
                act.wait_ge(gates_done, s + 1)
                nc.scalar.copy(logits[:, bass.ds(s * SLAB * CHUNKS, SLAB * CHUNKS), :],
                               flat(1)[0:TOK, 0:SLAB * CHUNKS * E].rearrange("p (n e) -> p n e", e=E)
                               ).then_inc(logits_ready, 1)
            act.wait_ge(gate_exp_in, 1)
            nc.scalar.activation(logits[:, :, :], logits[:, :, :], ACT.Exp).then_inc(gate_exp, 1)
            act.wait_ge(gate_exp_in, 2)
            nc.scalar.activation(top[:, 2, :], top[:, 2, :], ACT.Exp).then_inc(top_exp, 1)

            def norm_image(m, r, i):
                act.wait_ge(xs_loaded[r], 16 * (m + 1))
                if isinstance(i, int):
                    wait_count(act, z_ready, 3 * (i - 1))
                else:
                    wait_apart(act, z_ready, 3 * (i - 1), act_passed)
                nc.scalar.activation(xn[r][:, :], xs[r][:, :], ACT.Identity, scale=gn_scale[:, bass.ds(i, 1)],
                                     bias=gn_shift[:, bass.ds(i, 1)]).then_inc(xn_ready, 1)

            def step(m, r, s1_=True, s2_=True, s3=True, ffn=True, next_=True):
                i = 2 * m + r
                if s2_:
                    act.wait_ge(x1T_ready, i)
                    nc.scalar.copy(xh1T[0:C, :].rearrange("p (j t) -> p j t", t=TOK),
                                   flat(2)[0:C, 0:CHUNKS * P].rearrange("p (j t) -> p j t", t=P)[:, :, 0:TOK]
                                   ).then_inc(xh1T_ready, 1)
                if s1_:
                    for t in range(TILES):
                        act.wait_ge(z_ready, 3 * i + t + 1)
                        nc.scalar.activation(hT[:, t, :].rearrange("p (a n) -> p a n", a=2), halves(t % 2, P),
                                             ACT.Relu, bias=b1c[:, t:t + 1]).then_inc(h_ready, 1)
                if s2_:
                    for q, (k, j0, n) in enumerate(((3, 0, CH_A), (2, CH_A, CHUNKS - CH_A))):
                        act.wait_ge(kv_ready, 2 * (i - 1) + q + 1)
                        nc.scalar.activation(ekv[:, j0:j0 + n, :], chunks(k, n, 256, 2 * C), ACT.Exp,
                                             bias=minus_one[:, :]).then_inc(e_ready, 1)
                if s1_ and next_:
                    norm_image(m + r, 1 - r, i + 1)
                if s3:
                    act.wait_ge(t2p_ready, i - 1)
                    wait_count(act, t2T_stored[r], 16 * (m - 1))
                    nc.scalar.copy(t2T[r][:, :].rearrange("p (j t) -> p j t", t=TOK),
                                   flat(2)[0:C, 0:CHUNKS * P].rearrange("p (j t) -> p j t", t=P)[:, :, 0:TOK]
                                   ).then_inc(t2T_evac, 1)
                    if ffn:
                        wait_apart(act, x2p_ready, i - 1, act_passed)
                        nc.scalar.copy(big[0:C, i - 2, 0, :].rearrange("p (j t) -> p j t", t=TOK),
                                       flat(1)[0:C, 0:CHUNKS * P].rearrange("p (j t) -> p j t", t=P)[:, :, 0:TOK]
                                       ).then_inc(hi_ready, 1)
                if s2_:
                    act.wait_ge(stp_ready, i)
                    nc.scalar.copy(St[:, :], S[3][0:C, 0, 0:C + 1]).then_inc(st_ready, 1)

            norm_image(0, 0, 0)
            for i in range(FIRST):
                step(i // 2, i % 2, s2_=i >= 1, s3=i >= 2)
            with act.Fori(FIRST // 2, LAST // 2 - 1) as m:
                for r in range(2):
                    step(m, r)
            step(LAST // 2 - 1, 0)
            step(LAST // 2 - 1, 1, next_=False)
            step(LAST // 2, 0, s1_=False, ffn=False)
            step(LAST // 2, 1, s1_=False, s2_=False, ffn=False)

            act.wait_ge(s1_ready, 1)

            def ffn(g, m, r):
                b = 2 * m + r
                for t in range(TILES):
                    n = 3 * b + t
                    wait_count(act, hlo_ready, n - 1)
                    wait_apart(act, y1_ready, n + 1, act_passed)
                    nc.scalar.activation(gel_buf(r, t).rearrange("p (a n) -> p a n", a=2), halves((3 * r + t) % 2, P),
                                         ACT.Gelu, scale=s1[:, g:g + 1] if isinstance(g, int) else s1[:, bass.ds(g, 1)]).then_inc(gelu_ready, 1)
                wait_apart(act, y2_ready, b + 1, act_passed)
                nc.scalar.activation(y2_all[:, b, :].rearrange("p (a n) -> p a n", a=2), halves(2 + r, C),
                                     ACT.Identity, bias=fb2c[:, 0:1]).then_inc(y2_evac, 1)

            for r in range(2):
                ffn(0, 0, r)
            with act.Fori(1, QB // 2) as q:
                for r in range(2):
                    ffn(0, q, r)
            with act.Fori(1, QGROUPS) as g:
                with act.Fori(0, QB // 2) as q:
                    for r in range(2):
                        ffn(g, g * (QB // 2) + q, r)

        @block.tensor
        def _(pe):
            mm = nc.tensor.matmul

            def tr(o, i, start=True):
                rows = i.shape[0]
                return mm(o, i, ident[0:rows, 0:rows], start=start, stop=True, is_transpose=True,
                          skip_group_check=True)

            pe.wait_ge(params_loaded, 16 * N_PARAMS)
            pe.wait_ge(*CONSTS_SET)
            for e in range(E):
                tr(S[0][0:C, 0, e * C:(e + 1) * C], w1_raw[:, e, :])
            for t in range(TILES):
                tr(S[0][:, 1, t * C:(t + 1) * C],
                   w2_raw[:, :, :].rearrange("p e d -> p (e d)")[:, t * P:(t + 1) * P])
            tr(S[1][0:C, 0, 0:C + 1], qkvw[:, 0:C])
            for t in range(TILES):
                tr(S[1][0:C, 1, t * P:(t + 1) * P], W1_raw[:, t, :])
            for t in range(TILES):
                ins = tr(S[2][:, 0, t * C:(t + 1) * C], W2_raw[:, t * P:(t + 1) * P])
            ins.then_inc(setup_T, 1)
            pe.wait_ge(lam_prod, 1)
            mm(S[2][0:C, 1, 0:2], con[0:C, K_HEAD:K_HEAD + C], lam_e[:, 2:4],
               start=True, stop=True).then_inc(lam_sum, 1)
            pe.wait_ge(wsum_ready, 1)
            mm(S[3][0:C, 0, 0:QGROUPS], ones_f[0:C, 0:C], wsum[0:C, 0, :], start=True, stop=True)
            mm(S[3][:, 1, 0:QGROUPS], ones_f[:, :], wsum[:, 1, :], start=True, stop=True).then_inc(wmean_sum, 1)
            pe.wait_ge(fold_in, 1)

            with pe.Fori(0, SLABS) as s:
                pe.wait_ge(gn_mv_ready, 2 * s + 2)
                mm(S[0][0:C, 0, 0:2 * SLAB], con[0:C, K_GROUP:K_GROUP + C],
                   gn_mv[:, :, :].rearrange("p j k -> p (j k)"), start=True, stop=True).then_inc(gn_group, 1)
                pe.wait_ge(gn_dev2_ready, s + 1)
                mm(S[0][0:C, 1, 0:SLAB], con[0:C, K_GROUP:K_GROUP + C], gn_dev2[:, :],
                   start=True, stop=True).then_inc(gn_between, 1)
                pe.wait_ge(xn_slab_ready, s + 1)
                for j in range(SLAB):
                    for c in range(CHUNKS):
                        n = (j * CHUNKS + c) * E
                        ins = mm(flat(1)[0:TOK, n:n + E], xn_slab[:, j, c * TOK:(c + 1) * TOK], gw[:, :],
                                 start=True, stop=True, skip_group_check=True)
                ins.then_inc(gates_done, 1)
                pe.wait_ge(logits_ready, s + 1)
            pe.wait_ge(present_ready, 1)
            mm(S[0][:, 0, 0:2 * E], ones_f[0:TOK, :], present[:, :, :].rearrange("p k e -> p (k e)"),
               start=True, stop=True).then_inc(counts_ready, 1)

            pe.wait_ge(conv_ready, 1)
            pe.wait_ge(bigones_ready, 1)

            def step(m, r, s1_=True, s2_=True, s3=True, ffn=True):
                i = 2 * m + r
                a = i - 1
                f = i - 2
                if s2_:
                    pe.wait_ge(xh1_ready, i)
                    wait_count(pe, ymax_done, 3 * (i - 3) + 2)
                    for j in range(CHUNKS):
                        ins = tr(flat(2)[0:C, j * P:j * P + TOK], xh1[:, j, :], start=j % CH_A == 0)
                    ins.then_inc(x1T_ready, 1)
                if s1_:
                    pe.wait_ge(xn_ready, i + 1)
                    wait_count(pe, t1_ready, 2 * i)
                    for t in range(TILES):
                        if t == 0:
                            wait_count(pe, ymax_done, 3 * (i - 3) + 1)
                        elif t == 1:
                            wait_count(pe, ymax_done, 3 * (i - 3) + 3)
                        else:
                            pe.wait_ge(h_ready, 3 * i + 1)
                        for h in range(2):
                            ins = mm(S[t % 2][:, h, 0:HALF], w1T[:, t * P:(t + 1) * P],
                                     xn[r][:, h * HALF:(h + 1) * HALF], start=True, stop=True)
                        ins.then_inc(z_ready, 1)
                if s2_:
                    pe.wait_ge(xh1T_ready, i)
                    wait_count(pe, t2_ready, i - 1)
                    for k, j0, n in ((3, 0, CH_A), (2, CH_A, CHUNKS - CH_A)):
                        for j in range(n):
                            ins = mm(chunks(k, n, 256, 2 * C)[:, j, :], xh1T[:, (j0 + j) * TOK:(j0 + j + 1) * TOK],
                                     qkvw[:, C:3 * C], start=True, stop=True, skip_group_check=True)
                        ins.then_inc(kv_ready, 1)
                if s1_:
                    pe.wait_ge(h_ready, 3 * i + 3)
                    for k, j0, n in ((1, 0, CH_A), (0, CH_A, CHUNKS - CH_A)):
                        o = chunks(k, n, 256, 2 * C)
                        for j in range(n):
                            tr(o[:, j, C:2 * C], xs[r][:, (j0 + j) * TOK:(j0 + j + 1) * TOK], start=j % 2 == 0)
                        for j in range(0, n, 2):
                            w = min(2, n - j)
                            mm(o[:, j:j + w, :], ones_b[:, :],
                               bias2_parts[:, 0:w, :, :].rearrange("p w v c -> p w (v c)"),
                               start=False, stop=False, skip_group_check=True)
                        for j in range(n):
                            for t in range(TILES):
                                ins = mm(o[:, j, :], hT[:, t, (j0 + j) * TOK:(j0 + j + 1) * TOK], w2s[:, t, :],
                                         start=False, stop=t == TILES - 1, skip_group_check=True)
                        ins.then_inc(yx_ready, 1)
                if s2_:
                    pe.wait_ge(f_ready, 2 * i)
                    for j in range(CHUNKS):
                        ins = mm(S[3][0:C, 0, 0:C], fkv[:, j, 0:C], fkv[:, j, C:2 * C],
                                 start=j == 0, stop=j == CHUNKS - 1)
                    ins.then_inc(a_ready, 1)
                if s3:
                    wait_count(pe, t2T_evac, i - 2)
                    pe.wait_ge(t2_ready, i - 1)
                    for j in range(CHUNKS):
                        ins = tr(flat(2)[0:C, j * P:j * P + TOK], t2[:, j, :], start=j % CH_A == 0)
                    ins.then_inc(t2p_ready, 1)
                    if ffn:
                        pe.wait_ge(xh2_ready, i - 1)
                        pe.wait_ge(t1_ready, 2 * i + 1)
                        for j in range(CHUNKS):
                            ins = tr(flat(1)[0:C, j * P:j * P + TOK], xh2[:, j, :], start=j % CH_A == 0)
                        ins.then_inc(x2p_ready, 1)

                def ffn_tile(t, k):
                    w = W1b[:, t * P:(t + 1) * P]
                    for h in range(2):
                        mm(S[k][:, h, 0:HALF], w, big[:, f, 0, h * HALF:(h + 1) * HALF],
                           start=True, stop=False, skip_group_check=True)
                    for h in range(2):
                        ins = mm(S[k][:, h, 0:HALF], w[0:C, :], big[0:C, f, 1, h * HALF:(h + 1) * HALF],
                                 start=False, stop=True, skip_group_check=True)
                    ins.then_inc(y_ready, 1)

                if s2_:
                    pe.wait_ge(am_ready, i)
                    mm(S[3][0:C, 0, 0:C + 1], Am[:, :], wqT[:, :], start=True, stop=True).then_inc(stp_ready, 1)
                if s3 and ffn:
                    pe.wait_ge(hi_ready, i - 1)
                    pe.wait_ge(lo_ready, i - 1)
                    pe.wait_ge(t1_ready, 2 * i + 2)
                    ffn_tile(0, 0)
                if s2_:
                    pe.wait_ge(st_ready, i)
                    mm(S[3][0:C + 1, 0, 0:C], St[:, :], projw[:, :], start=True, stop=True).then_inc(rp_ready, 1)
                if s3 and ffn:
                    pe.wait_ge(t2T_evac, i - 1)
                    ffn_tile(1, 2)
                    ffn_tile(2, 1)
                if s2_:
                    pe.wait_ge(r_ready, i)
                    for j in range(CHUNKS):
                        ins = mm(flat(3)[0:TOK, j * P:j * P + C], xh1T[:, j * TOK:(j + 1) * TOK], R[:, :],
                                 start=True, stop=True, skip_group_check=True)
                    ins.then_inc(ao_ready, 1)

            for i in range(FIRST):
                step(i // 2, i % 2, s2_=i >= 1, s3=i >= 2)
            with pe.Fori(FIRST // 2, LAST // 2) as m:
                for r in range(2):
                    step(m, r)
            step(LAST // 2, 0, s1_=False, ffn=False)
            step(LAST // 2, 1, s1_=False, s2_=False, ffn=False)

            pe.wait_ge(gmax_ready, 1)
            pe.wait_ge(t2T_evac, BATCH)
            tr(S[0][0:QGROUPS, 0, 0:P], gmax1[:, :]).then_inc(gmaxT, 1)
            pe.wait_ge(gdiag_ready, 1)
            mm(S[0][:, 1, 0:QGROUPS], ones_f[0:QGROUPS, :], gdiag[:, :], start=True, stop=True).then_inc(gbc, 1)
            pe.wait_ge(s1_ready, 1)

            def ffn_up(b, r):
                for t in range(TILES):
                    n = 3 * b + t
                    k = (3 * r + t) % 2
                    wait_count(pe, gelu_ready, n - 1)
                    w = W1b[:, t * P:(t + 1) * P]
                    for h in range(2):
                        mm(S[k][:, h, 0:HALF], w, big[:, b, 0, h * HALF:(h + 1) * HALF],
                           start=True, stop=False, skip_group_check=True)
                    for h in range(2):
                        ins = mm(S[k][:, h, 0:HALF], w[0:C, :], big[0:C, b, 1, h * HALF:(h + 1) * HALF],
                                 start=False, stop=True, skip_group_check=True)
                    ins.then_inc(y1_ready, 1)

            def ffn_down(b, r):
                k = 2 + r
                wait_count(pe, y2_evac, b - 1)
                for t in range(TILES):
                    pe.wait_ge(hlo_ready, 3 * b + t + 1)
                    for part, src in enumerate((h_hi[r], h_lo[r])):
                        for h in range(2):
                            ins = mm(S[k][0:C, h, 0:HALF], W2b[:, t, :], src[:, t, h * HALF:(h + 1) * HALF],
                                     start=t == 0 and part == 0, stop=t == TILES - 1 and part == 1,
                                     skip_group_check=True)
                ins.then_inc(y2_ready, 1)

            def group_scale(g):
                pe.wait_ge(g2_ready, g + 1)
                tr(S[3][0:1, 0, 400:400 + C], gmax2[:, :]).then_inc(g2T, 1)
                pe.wait_ge(g2one_ready, g + 1)
                mm(S[3][0:C, 1, 400:401], ones_f[0:1, 0:C], g2one[:, :], start=True, stop=True,
                   skip_group_check=True).then_inc(g2bc, 1)

            def ffn_pair(m):
                for r in range(2):
                    ffn_up(2 * m + r, r)
                    ffn_down(2 * m + r, r)

            ffn_pair(0)
            with pe.Fori(1, QB // 2) as q:
                ffn_pair(q)
            group_scale(0)
            with pe.Fori(1, QGROUPS) as g:
                with pe.Fori(0, QB // 2) as q:
                    ffn_pair(g * (QB // 2) + q)
                group_scale(g)

        @block.vector
        def _(dve):
            V = nc.vector
            links = [0]

            def link(ins):
                links[0] += 1
                ins.then_inc(setup_dve, 1)
                dve.wait_ge(setup_dve, links[0])

            dve.wait_ge(params_loaded, 16 * N_PARAMS)
            dve.wait_ge(*CONSTS_SET)
            V.tensor_tensor(lam_e[:, 2:4], lam[:, 0:4:2], lam[:, 1:4:2], ALU.mult).then_inc(lam_prod, 1)
            dve.wait_ge(setup_T, 1)
            V.tensor_copy(w1T[:, :], S[0][0:C, 0, 0:HID])
            V.tensor_copy(w2T[:, :, :], S[0][:, 1, 0:TILES * C].rearrange("p (t c) -> p t c", c=C))
            V.tensor_scalar(wqT[:, :], S[1][0:C, 0, 0:C + 1], float(HD) ** -0.5, None, ALU.mult)
            V.tensor_copy(W1f[:, :], S[1][0:C, 1, 0:HID])
            link(V.tensor_copy(W2f[:, :, :], S[2][:, 0, 0:TILES * C].rearrange("p (t c) -> p t c", c=C)))
            V.tensor_scalar(qkvw[C:C + 1, C:3 * C], qkvw[C:C + 1, C:3 * C], 1.0, None, ALU.add)
            W1v = W1f[:, 0:QGROUPS * W1_GS].rearrange("p (g n) -> p g n", n=W1_GS)
            V.tensor_reduce(wsum[0:C, 0, :], W1v, AX.X, ALU.add)
            V.tensor_reduce(wsum[:, 1, :], W2f[:, :, 0:QGROUPS * W2_GS].rearrange("p t (g n) -> p g t n", n=W2_GS),
                            AX.XY, ALU.add).then_inc(wsum_ready, 1)
            V.memset(W1b[0:C, QGROUPS * W1_GS:HID], 0.0)
            V.memset(W2b[:, :, QGROUPS * W2_GS:C], 0.0)
            dve.wait_ge(wmean_sum, 1)
            V.tensor_scalar(wmean[0:C, 0, :], S[3][0:C, 0, 0:QGROUPS], 1.0 / (W1_GS * C), None, ALU.mult)
            link(V.tensor_scalar(wmean[:, 1, :], S[3][:, 1, 0:QGROUPS], 1.0 / (W2_GS * HID), None, ALU.mult))
            m1 = wmean[0:C, 0, :].rearrange("p (g a) -> p g a", a=1).to_broadcast([C, QGROUPS, W1_GS])
            pa = part_a[0:C, 0:QGROUPS * W1_GS].rearrange("p (g n) -> p g n", n=W1_GS)
            pb = part_b[0:C, 0:QGROUPS * W1_GS].rearrange("p (g n) -> p g n", n=W1_GS)
            V.tensor_tensor(pa, W1v, m1, ALU.is_gt)
            link(V.tensor_tensor(pb, W1v, m1, ALU.is_lt))
            link(V.tensor_tensor(W1b[0:C, 0:QGROUPS * W1_GS].rearrange("p (g n) -> p g n", n=W1_GS),
                                 pa, pb, ALU.subtract))
            m2 = wmean[:, 1, :].rearrange("p (g a) -> p g a", a=1).to_broadcast([P, QGROUPS, W2_GS])
            for t in range(TILES):
                w = W2f[:, t, 0:QGROUPS * W2_GS].rearrange("p (g n) -> p g n", n=W2_GS)
                V.tensor_tensor(part_a[:, t * C:t * C + QGROUPS * W2_GS].rearrange("p (g n) -> p g n", n=W2_GS),
                                w, m2, ALU.is_gt)
                ins = V.tensor_tensor(part_b[:, t * C:t * C + QGROUPS * W2_GS].rearrange(
                    "p (g n) -> p g n", n=W2_GS), w, m2, ALU.is_lt)
            link(ins)
            for t in range(TILES):
                n = QGROUPS * W2_GS
                ins = V.tensor_tensor(W2b[:, t, 0:n], part_a[:, t * C:t * C + n], part_b[:, t * C:t * C + n],
                                      ALU.subtract)
            link(ins)

            def bf16_parts(dst, src, rows, width, masks):
                a, b, h = part_a[rows, 0:width], part_b[rows, 0:width], part_h[rows, 0:width]
                link(V.tensor_copy(h, src))
                link(V.tensor_scalar(a, h, masks[:, 0:1], None, ALU.mult))
                link(V.tensor_tensor(b, src, h, ALU.subtract))
                link(V.tensor_copy(h, b))
                link(V.scalar_tensor_tensor(a, h, masks[:, 1:2], a, ALU.mult, ALU.add))
                link(V.tensor_tensor(b, b, h, ALU.subtract))
                link(V.scalar_tensor_tensor(dst, b, masks[:, 2:3], a, ALU.mult, ALU.add))

            rows = slice(C, C + PARTS)
            bf16_parts(W1b[rows, :], fb1r[rows, :], rows, HID, con[rows, K_PART96:K_PART96 + PARTS])
            dve.wait_ge(lam_exp, 1)
            link(V.tensor_tensor(lam_e[:, 2:3], lam_e[:, 0:1], lam_e[:, 1:2], ALU.subtract))
            link(V.tensor_scalar(lam_e[:, 3:4], lam_e[:, 2:3], LAMBDA_INIT, None, ALU.add))
            link(V.tensor_scalar(lam_e[:, 2:3], lam_e[:, 3:4], -1.0, 1.0, ALU.mult, ALU.add))
            V.tensor_scalar(gauss[:, :], con[0:C, K_GAUSS:K_GAUSS + C], lam_e[:, 2:3], None,
                            ALU.mult).then_inc(fold_in, 1)

            with dve.Fori(0, SLABS) as s:
                for r in range(2):
                    dve.wait_ge(x_loaded[r], 16 * (s + 1))
                    for j in range(4 * r, 4 * r + 4):
                        for h in range(2):
                            ins = V.bn_stats(gn_st[:, j, h, :], x_all[:, s * SLAB + j, h * HALF:(h + 1) * HALF])
                    ins.then_inc(gn_stats, 1)
                    wait_apart(dve, gn_stats, 2 * s + r + 1, dve_passed)
                    for j in range(4 * r, 4 * r + 4):
                        ins = V.bn_aggr(gn_mv[:, j, :], gn_st[:, j, :, :].rearrange("p h k -> p (h k)"))
                    ins.then_inc(gn_mv_ready, 1)
                dve.wait_ge(gn_group, s + 1)
                V.tensor_copy(gn_avg[:, :, :].rearrange("p j k -> p (j k)"),
                              S[0][0:C, 0, 0:2 * SLAB]).then_inc(gn_avg_ready, 1)
                dve.wait_ge(gn_avg_ready, s + 1)
                V.tensor_tensor(gn_dev[:, :], gn_mv[:, :, 0], gn_avg[:, :, 0], ALU.subtract).then_inc(gn_dev_ready, 1)
                dve.wait_ge(gn_dev_ready, s + 1)
                V.tensor_tensor(gn_dev2[:, :], gn_dev[:, :], gn_dev[:, :], ALU.mult).then_inc(gn_dev2_ready, 1)
                dve.wait_ge(gn_between, s + 1)
                V.scalar_tensor_tensor(gn_var[:, :], S[0][0:C, 1, 0:SLAB], GN_EPS, gn_avg[:, :, 1],
                                       ALU.add, ALU.add).then_inc(gn_var_ready, 1)
                dve.wait_ge(gn_rstd, s + 1)
                V.scalar_tensor_tensor(gn_shift[:, bass.ds(s * SLAB, SLAB)], gn_avg[:, :, 0], -1.0,
                                       gn_scale[:, bass.ds(s * SLAB, SLAB)], ALU.mult, ALU.mult).then_inc(gn_coef, 1)

            def bc(v):
                return v.rearrange("p (n a) -> p n a", a=1).to_broadcast([TOK, NT, E])

            sv = stage[0:TOK, :]
            first = sv[:, 0:NT * E].rearrange("p (n e) -> p n e", e=E)
            second = sv[:, NT * E:2 * NT * E].rearrange("p (n e) -> p n e", e=E)
            work = sv[:, 2 * NT * E:3 * NT * E].rearrange("p (n e) -> p n e", e=E)
            gbv = gb[:, :].rearrange("p (a e) -> p a e", a=1).to_broadcast([TOK, NT, E])
            pref = prefer[:, :].rearrange("p (a e) -> p a e", a=1).to_broadcast([TOK, NT, E])
            dve.wait_ge(gates_done, SLABS)
            dve.wait_ge(logits_ready, SLABS)
            link(V.tensor_tensor(logits[:, :, :], logits[:, :, :], gbv, ALU.add))
            link(V.tensor_reduce(top[:, 0, :], logits[:, :, :], AX.X, ALU.max))
            V.tensor_tensor(logits[:, :, :], logits[:, :, :], bc(top[:, 0, :]), ALU.subtract).then_inc(gate_exp_in, 1)
            dve.wait_ge(gate_exp, 1)
            link(V.tensor_reduce(top[:, 1, :], logits[:, :, :], AX.X, ALU.add))
            link(V.reciprocal(top[:, 0, :], top[:, 1, :]))
            link(V.tensor_tensor(logits[:, :, :], logits[:, :, :], bc(top[:, 0, :]), ALU.mult))

            def pick(onehot, value):
                link(V.tensor_reduce(value, logits[:, :, :], AX.X, ALU.max))
                link(V.tensor_tensor(work, logits[:, :, :], bc(value), ALU.is_equal))
                link(V.tensor_tensor(work, work, pref, ALU.mult))
                link(V.tensor_reduce(top[:, 3, :], work, AX.X, ALU.max))
                link(V.tensor_tensor(onehot, work, bc(top[:, 3, :]), ALU.is_equal))

            pick(first, top[:, 0, :])
            link(V.scalar_tensor_tensor(logits[:, :, :], first, -2.0, logits[:, :, :], ALU.mult, ALU.add))
            pick(second, top[:, 1, :])
            V.tensor_reduce(present[:, 0, :], first.rearrange("p n e -> p e n"), AX.X, ALU.max)
            V.tensor_reduce(present[:, 1, :], second.rearrange("p n e -> p e n"), AX.X, ALU.max).then_inc(present_ready, 1)
            V.tensor_tensor(top[:, 2, :], top[:, 1, :], top[:, 0, :], ALU.subtract).then_inc(gate_exp_in, 1)
            dve.wait_ge(top_exp, 1)
            link(V.tensor_scalar(top[:, 3, :], top[:, 2, :], 1.0, None, ALU.add))
            V.reciprocal(w0[:, :], top[:, 3, :])
            dve.wait_ge(counts_ready, 1)
            link(V.tensor_scalar(flags[:, :, :].rearrange("p k e -> p (k e)"), S[0][:, 0, 0:2 * E], 1.0, None, ALU.min))
            link(V.tensor_tensor(flags[:, 0, :], flags[:, 0, :], flags[:, 1, :], ALU.subtract))
            expert = con[:, K_EXPERT:K_EXPERT + TILES * E].rearrange("p (t e) -> p t e", e=E)
            for v in range(2):
                fl = flags[:, v, :].rearrange("p (a e) -> p a e", a=1).to_broadcast([P, TILES, E])
                link(V.tensor_tensor(flag_tmp[:, :, :], expert, fl, ALU.mult))
                link(V.tensor_reduce(row_flag[:, v, :], flag_tmp[:, :, :], AX.X, ALU.add))
            for t in range(TILES):
                for v in range(2):
                    V.tensor_scalar(w2s[:, t, v * C:(v + 1) * C], w2T[:, t, :], row_flag[:, v, t:t + 1], None, ALU.mult)
            for v in range(2):
                fl = flags[:, v, :].rearrange("p (e a) -> p e a", a=1).to_broadcast([P, E, C])
                tv = part_a[:, :].rearrange("p (e c) -> p e c", c=C)
                link(V.tensor_tensor(tv, b2all[:, :, :], fl, ALU.mult))
                link(V.tensor_reduce(bias2[:, v, :], tv.rearrange("p e c -> p c e"), AX.X, ALU.add))
            bf16_parts(bias2_parts[:, 0, :, :].rearrange("p v c -> p (v c)"),
                       bias2[:, :, :].rearrange("p v c -> p (v c)"), slice(0, P), 2 * C,
                       con[:, K_PART:K_PART + PARTS])
            V.tensor_copy(bias2_parts[:, 1, :, :], bias2_parts[:, 0, :, :]).then_inc(conv_ready, 1)

            def stats(n, src, b, count):
                for j in range(CHUNKS):
                    ins = V.bn_stats(ln_st[:, j, :], src[:, j, :])
                ins.then_inc(ln_stats, 1)
                wait_apart(dve, ln_stats, count, dve_passed)
                for j in range(CHUNKS):
                    ins = V.bn_aggr(ln_mv[n][:, j, :], ln_st[:, j, :])
                ins.then_inc(ln_mean[n], 1)

            def apply(n, src, dst, b, done):
                dve.wait_ge(ln_rstd[n], b + 1)
                for j in range(CHUNKS):
                    ins = V.tensor_scalar(dst[:, j, :], src[:, j, :], ln_mv[n][:, j, 0:1], ln_rs[n][:, j:j + 1],
                                          ALU.subtract, ALU.mult)
                ins.then_inc(done, 1)

            def absmax(f, t, k):
                dve.wait_ge(y_ready, 3 * f + t + 1)
                V.tensor_reduce(ymax[:, bass.ds(3 * f + t, 1)], halves(k, P), AX.XY, ALU.max,
                                apply_absolute_value=True).then_inc(ymax_done, 1)

            def step(m, r, s1_=True, s2_=True, s3=True, ffn=True):
                i = 2 * m + r
                a, f = i - 1, i - 2
                if s3 and ffn:
                    apply(1, t2, xh2, f, xh2_ready)
                if s2_:
                    for q, (k, j0, n) in enumerate(((3, 0, CH_A), (2, CH_A, CHUNKS - CH_A))):
                        dve.wait_ge(e_ready, 2 * a + q + 1)
                        V.scalar_tensor_tensor(fkv[:, j0:j0 + n, :], ekv[:, j0:j0 + n, :], 1.0,
                                               chunks(k, n, 256, 2 * C), ALU.min, ALU.max).then_inc(f_ready, 1)
                if s1_:
                    for q, (k, j0, n) in enumerate(((1, 0, CH_A), (0, CH_A, CHUNKS - CH_A))):
                        dve.wait_ge(yx_ready, 2 * i + q + 1)
                        o = chunks(k, n, 256, 2 * C)
                        wv = w0[:, bass.ds(i * CHUNKS + j0, n)].rearrange("p (n a) -> p n a", a=1).to_broadcast([TOK, n, C])
                        V.tensor_tensor(tmp[:, j0:j0 + n, :], o[:, :, 0:C], wv, ALU.mult).then_inc(tmp_ready, 1)
                        dve.wait_ge(tmp_ready, 2 * i + q + 1)
                        V.tensor_tensor(t1[r][:, j0:j0 + n, :], tmp[:, j0:j0 + n, :], o[:, :, C:2 * C],
                                        ALU.add).then_inc(t1_ready, 1)
                if s2_:
                    dve.wait_ge(a_ready, i)
                    V.tensor_tensor(Am[:, :], S[3][0:C, 0, 0:C], gauss[:, :], ALU.mult).then_inc(am_ready, 1)
                if s1_:
                    dve.wait_ge(t1_ready, 2 * i + 2)
                    stats(0, t1[r], i, 1 if isinstance(i, int) and i == 0 else 2 * i)
                if s3 and ffn:
                    dve.wait_ge(hi_ready, f + 1)
                    V.tensor_tensor(big[0:C, f, 1, :].rearrange("p (j t) -> p j t", t=TOK),
                                    flat(1)[0:C, 0:CHUNKS * P].rearrange("p (j t) -> p j t", t=P)[:, :, 0:TOK],
                                    big[0:C, f, 0, :].rearrange("p (j t) -> p j t", t=TOK),
                                    ALU.subtract).then_inc(lo_ready, 1)
                    absmax(f, 0, 0)
                if s2_:
                    dve.wait_ge(rp_ready, i)
                    V.tensor_tensor(R[:, :], S[3][0:C + 1, 0, 0:C], projb[:, :], ALU.add).then_inc(r_ready, 1)
                if s1_:
                    apply(0, t1[r], xh1, i, xh1_ready)
                if s3 and ffn:
                    absmax(f, 1, 2)
                    absmax(f, 2, 1)
                if s2_:
                    dve.wait_ge(ao_ready, i)
                    V.tensor_tensor(t2[:, :, :], t1[1 - r][:, :, :], chunks(3, CHUNKS, P, C),
                                    ALU.add).then_inc(t2_ready, 1)
                    if not (isinstance(i, int) and i - 1 >= QIMAGES):
                        dve.wait_ge(t2_ready, i)
                        stats(1, t2, a, 2 * i + 1)

            dve.wait_ge(params_loaded, 16 * N_PARAMS)
            for i in range(FIRST):
                step(i // 2, i % 2, s2_=i >= 1, s3=i >= 2)
            with dve.Fori(FIRST // 2, LAST // 2) as m:
                for r in range(2):
                    step(m, r)
            step(LAST // 2, 0, s1_=False, ffn=False)

            dve.wait_ge(ymax_done, 3 * QIMAGES)
            V.tensor_reduce(gmax1[:, :], ymax[:, :].rearrange("p (g n) -> p g n", g=QGROUPS), AX.X,
                            ALU.max).then_inc(gmax_ready, 1)
            dve.wait_ge(gmaxT, 1)
            link(V.tensor_reduce(gcol[:, :], S[0][0:QGROUPS, 0, 0:P], AX.X, ALU.max))
            V.tensor_scalar(gdiag[:, :], ident[0:QGROUPS, 0:QGROUPS], gcol[:, 0:1], None, ALU.mult).then_inc(gdiag_ready, 1)
            dve.wait_ge(gbc, 1)
            link(V.tensor_scalar(s1e[:, :], S[0][:, 1, 0:QGROUPS], Q_EPS, 1.0 / QMAX, ALU.add, ALU.mult))
            V.reciprocal(s1[:, :], s1e[:, :]).then_inc(s1_ready, 1)

            def split(m, r):
                b = 2 * m + r
                for t in range(TILES):
                    n = 3 * b + t
                    dve.wait_ge(gelu_ready, n + 1)
                    if t == 0:
                        wait_count(dve, y2_ready, b - 1)
                    V.tensor_scalar(h_hi[r][:, t, :], gel_buf(r, t), Q_CLIP, None, ALU.min).then_inc(hhi_ready, 1)
                    dve.wait_ge(hhi_ready, n + 1)
                    V.scalar_tensor_tensor(h_lo[r][:, t, :], gel_buf(r, t), Q_CLIP, h_hi[r][:, t, :],
                                           ALU.min, ALU.subtract).then_inc(hlo_ready, 1)

            def y2_absmax(b):
                dve.wait_ge(y2_evac, b + 1)
                V.tensor_reduce(y2max[:, bass.ds(b, 1)], y2_all[:, b, :], AX.X, ALU.max,
                                apply_absolute_value=True).then_inc(y2max_done, 1)

            def group_scale(g):
                dve.wait_ge(y2max_done, (g + 1) * QB)
                V.tensor_reduce(gmax2[:, :], y2max[:, bass.ds(g * QB, QB)], AX.X, ALU.max).then_inc(g2_ready, 1)
                dve.wait_ge(g2T, g + 1)
                V.tensor_reduce(g2one[:, :], S[3][0:1, 0, 400:400 + C], AX.X, ALU.max).then_inc(g2one_ready, 1)
                dve.wait_ge(g2bc, g + 1)
                V.tensor_scalar(s2e[:, :], S[3][0:C, 1, 400:401], Q_EPS, 1.0 / QMAX, ALU.add, ALU.mult).then_inc(s2e_ready, 1)
                dve.wait_ge(s2e_ready, g + 1)
                V.reciprocal(s2[:, bass.ds(g, 1)], s2e[:, :]).then_inc(s2_ready, 1)

            def finish(g, m, r):
                b = 2 * m + r
                dve.wait_ge(s2_ready, g + 1)
                V.tensor_scalar(qv[r][:, :], y2_all[:, b, :], s2[:, bass.ds(g, 1)], Q_CLIP,
                                ALU.mult, ALU.min).then_inc(qv_ready, 1)
                dve.wait_ge(qv_ready, b + 1)
                dve.wait_ge(tc_loaded[r], 16 * (m + 1))
                V.scalar_tensor_tensor(tc_buf[r][:, :], qv[r][:, :], -Q_CLIP, tc_buf[r][:, :],
                                       ALU.max, ALU.add).then_inc(o_ready, 1)

            def ffn_pair(m):
                for r in range(2):
                    split(m, r)
                    y2_absmax(2 * m + r)

            ffn_pair(0)
            with dve.Fori(1, QB // 2) as q:
                ffn_pair(q)
            group_scale(0)
            with dve.Fori(1, QGROUPS) as g:
                with dve.Fori(0, QB // 2) as q:
                    m = g * (QB // 2) + q
                    for r in range(2):
                        split(m, r)
                        finish(g - 1, m - QB // 2, r)
                        y2_absmax(2 * m + r)
                group_scale(g)
            for q in range(QB // 2):
                for r in range(2):
                    finish(QGROUPS - 1, (QGROUPS - 1) * (QB // 2) + q, r)


_INS = ['x', 'L0_conv_gate_w', 'L0_conv_gate_b', 'L0_conv_w1', 'L0_conv_b1', 'L0_conv_w2', 'L0_conv_b2',
        'L1_attn_qkv_w', 'L1_attn_qkv_b', 'L1_attn_proj_w', 'L1_attn_proj_b', 'L1_attn_lambda_k1',
        'L1_attn_lambda_v1', 'L1_attn_lambda_k2', 'L1_attn_lambda_v2', 'L1_ffn_W1', 'L1_ffn_b1',
        'L1_ffn_W2', 'L1_ffn_b2']


def kernel(**inputs):
    import concourse.bacc as _bacc
    from concourse.bass_utils import run_bass_kernel_spmd as _run

    nc = _bacc.Bacc("TRN2", target_bir_lowering=False, num_devices=1)
    arrays, args = {}, []
    for name in _INS:
        a = np.ascontiguousarray(inputs[name])
        arrays[f"in_{name}"] = a
        args.append(nc.dram_tensor(f"in_{name}", a.shape, mybir.dt.from_np(a.dtype), kind="ExternalInput").ap())
    k = shape_constants()
    arrays["shape_consts"] = k
    args.append(nc.dram_tensor("shape_consts", k.shape, F32, kind="ExternalInput").ap())
    args.append(nc.dram_tensor("out", (BATCH, C, 28, 28), F32, kind="ExternalOutput").ap())
    build(nc, *args)
    r = _run(nc, [arrays], core_ids=[0])
    return r.results[0]["out"]
```

```python
from contextlib import ExitStack

import numpy as np

import concourse.bass as bass
from concourse import mybir

ALU = mybir.AluOpType
ACT = mybir.ActivationFunctionType
AX = mybir.AxisListType
F32 = mybir.dt.float32
F16 = mybir.dt.float16
BF16 = mybir.dt.bfloat16

P = 128
BATCH, C, HW = 32, 96, 784
HALF = HW // 2
TOK = 112
CHUNKS = HW // TOK
CH_A = 4
E = 4
HID = E * C
TILES = HID // P
HEADS, HD = 12, 8
GN_GROUPS = 32
GN_C = C // GN_GROUPS
SLAB = 8
SLABS = BATCH // SLAB
QGROUPS = 5
QB = BATCH // QGROUPS
QIMAGES = QGROUPS * QB
W1_GS = HID // QGROUPS
W2_GS = C // QGROUPS
QMAX = 128.0
Q_EPS = 1e-5
Q_CLIP = float(np.float32(QMAX - Q_EPS))
GN_EPS = 1e-5
LN_EPS = 1e-5
LAMBDA_INIT = 0.8 - 0.6 * float(np.exp(-0.3))
SIGMA = 0.5
PARTS = 3

K_ID, K_GAUSS, K_HEAD, K_GROUP, K_EXPERT, K_PART, K_PART96, K_LAST, K_END = np.cumsum(
    [0, P, C, C, C, TILES * E, PARTS, PARTS, C + 1]).tolist()


def shape_constants():
    k = np.zeros((P, K_END), np.float32)
    k[:, K_ID:K_ID + P] = np.eye(P)
    row = np.arange(C)
    same_head = row[:, None] // HD == row[None, :] // HD
    dist = (row[:, None] % HD - row[None, :] % HD).astype(np.float32)
    k[:C, K_GAUSS:K_GAUSS + C] = np.exp(-dist ** 2 / (2.0 * SIGMA ** 2)) * same_head
    k[:C, K_HEAD:K_HEAD + C] = same_head
    k[:C, K_GROUP:K_GROUP + C] = (row[:, None] // GN_C == row[None, :] // GN_C) / np.float32(GN_C)
    for t in range(TILES):
        for e in range(E):
            k[:, K_EXPERT + t * E + e] = (np.arange(P) + t * P) // C == e
    for n in range(PARTS):
        k[n, K_PART + n] = 1.0
        k[C + n, K_PART96 + n] = 1.0
    k[0, K_LAST + C] = 1.0
    return k


def wait_count(eng, sem, count):
    if isinstance(count, int) and count <= 0:
        return
    eng.wait_ge(sem, count)


def wait_apart(eng, sem, count, passed):
    eng.wait_ge(sem, count)
    eng.sem_inc(passed, 1)


def build(nc, x, gate_w, gate_b, w1, b1, w2, b2, qkv_w, qkv_b, proj_w, proj_b,
          lk1, lv1, lk2, lv2, W1, fb1, W2, fb2, consts, out):
    with ExitStack() as ctx:
        def sb(name, shape, dt=F32):
            return ctx.enter_context(nc.sbuf_tensor(name, shape, dt))

        def sem(name):
            return ctx.enter_context(nc.semaphore(name))

        ctx.enter_context(nc.allow_non_contiguous_dma(reason="small parameter columns"))
        ctx.enter_context(nc.allow_low_precision(reason="float32 carried as exact parts"))

        S = [ctx.enter_context(nc.psum_tensor(f"slot{k}", [P, 2, 512], F32)) for k in range(4)]

        def one_other(r):
            return (1, 3) if r == 0 else (3, 1)

        def halves(k, rows):
            return S[k][0:rows, :, 0:HALF]

        def flat(k):
            return S[k][:, :, :].rearrange("p a b -> p (a b)")

        def chunks(k, n, width, used):
            return flat(k)[0:TOK, 0:n * width].rearrange("p (j c) -> p j c", c=width)[:, :, 0:used]

        con = sb("con", [P, K_END])
        ident = con[:, K_ID:K_ID + P]
        w1_raw = sb("w1_raw", [C, E, C])
        w2_raw = sb("w2_raw", [C, E, C])
        w1T = sb("w1T", [C, HID])
        b1c = sb("b1c", [P, TILES])
        w2T = sb("w2T", [P, TILES, C])
        w2s = sb("w2s", [P, 2, TILES, C])
        b2all = sb("b2all", [P, E, C])
        bias2 = sb("bias2", [P, 2, C])
        bias2_parts = sb("bias2_parts", [P, 2, CH_A, C], BF16)
        differ = sb("differ", [1, 1], mybir.dt.int32)
        ones_b = sb("ones_b", [P, TOK], BF16)
        ones_f = sb("ones_f", [P, P])
        gw = sb("gw", [C, E])
        gb = sb("gb", [TOK, E])
        qkvw = sb("qkvw", [C + 1, 3 * C])
        wqT = sb("wqT", [C, C + 1])
        projw = sb("projw", [C, C])
        projb = sb("projb", [C, C])
        lam = sb("lam", [C, 4])
        lam_e = sb("lam_e", [C, 4])
        gauss = sb("gauss", [C, C])
        W1_raw = sb("W1_raw", [P, TILES, C])
        W1f = sb("W1f", [C, HID])
        W1b = sb("W1b", [C + PARTS, HID], BF16)
        fb1r = sb("fb1r", [C + PARTS, HID])
        W2_raw = sb("W2_raw", [C, HID])
        W2f = sb("W2f", [P, TILES, C])
        W2b = sb("W2b", [P, TILES, C], BF16)
        fb2c = sb("fb2c", [C, 1])
        wsum = sb("wsum", [P, 2, QGROUPS])
        wmean = sb("wmean", [P, 2, QGROUPS])
        part_a = sb("part_a", [P, HID])
        part_b = sb("part_b", [P, HID])
        part_h = sb("part_h", [P, HID], BF16)
        minus_one = sb("minus_one", [TOK, 1])
        ln_eps = sb("ln_eps", [TOK, CHUNKS])
        minus_ones = sb("minus_ones", [TOK, CHUNKS])
        pow_half = sb("pow_half", [P, 2 * SLAB])

        big = sb("big", [C + PARTS, BATCH, 2, HW], F16)
        x_all = big[0:C, :, :, :].rearrange("p b s n -> p (b s n)").bitcast(F32).rearrange(
            "p (b n) -> p b n", n=HW)
        y2_all = x_all
        stage = sb("stage", [P, SLAB * HW])
        gn_scale = sb("gn_scale", [C, BATCH])
        gn_shift = sb("gn_shift", [C, BATCH])
        w0 = sb("w0", [TOK, BATCH * CHUNKS])
        ymax = sb("ymax", [P, QIMAGES * TILES])
        y2max = sb("y2max", [C, QIMAGES])

        xn_slab = stage[0:C, :].rearrange("p (j n) -> p j n", n=HW)
        gn_st = sb("gn_st", [C, SLAB, 2, 6])
        gn_mv = sb("gn_mv", [C, SLAB, 2])
        gn_avg = sb("gn_avg", [C, SLAB, 2])
        gn_dev = sb("gn_dev", [C, SLAB])
        gn_dev2 = sb("gn_dev2", [C, SLAB])
        gn_var = sb("gn_var", [C, SLAB])
        NT = BATCH * CHUNKS
        hT = sb("hT", [P, TILES, HW])
        logits = hT[0:TOK, :, :].rearrange("p t n -> p (t n)")[:, 0:NT * E].rearrange("p (n e) -> p n e", e=E)
        top = sb("top", [TOK, 4, NT])
        present = sb("present", [TOK, 2, E])
        flags = sb("flags", [P, 2, E])
        flag_tmp = sb("flag_tmp", [P, TILES, E])
        row_flag = sb("row_flag", [P, 2, TILES])
        differ_f = sb("differ_f", [1, 1])
        prefer = sb("prefer", [TOK, E])

        xs = [sb(f"xs{r}", [C, HW]) for r in range(2)]
        xn = [sb(f"xn{r}", [C, HW]) for r in range(2)]
        tmp = stage[0:TOK, 4 * CHUNKS * C:5 * CHUNKS * C].rearrange("p (j c) -> p j c", c=C)
        t1 = [sb(f"t1_{r}", [TOK, CHUNKS, C]) for r in range(2)]
        t2 = sb("t2", [TOK, CHUNKS, C])
        ln_st = sb("ln_st", [TOK, CHUNKS, 6])
        ln_mv = [sb(f"ln_mv{n}", [TOK, CHUNKS, 2]) for n in range(2)]
        ln_ve = [sb(f"ln_ve{n}", [TOK, CHUNKS]) for n in range(2)]
        ln_nm = sb("ln_nm", [TOK, CHUNKS])
        ln_nb = sb("ln_nb", [TOK, CHUNKS])
        ln_rs = [sb(f"ln_rs{n}", [TOK, CHUNKS]) for n in range(2)]
        xh1 = sb("xh1", [TOK, CHUNKS, C])
        xh2 = sb("xh2", [TOK, CHUNKS, C])
        xh1T = sb("xh1T", [C + 1, HW])
        ekv = stage[0:TOK, 0:CHUNKS * 2 * C].rearrange("p (j c) -> p j c", c=2 * C)
        fkv = stage[0:TOK, CHUNKS * 2 * C:2 * CHUNKS * 2 * C].rearrange("p (j c) -> p j c", c=2 * C)
        Am = sb("Am", [C, C])
        St = sb("St", [C, C + 1])
        R = sb("R", [C + 1, C])
        t2T = [sb(f"t2T{r}", [C, HW]) for r in range(2)]

        gel = hT

        def y1_slot(r, t):
            return (3 * r + t) % 2

        stage16 = stage[:, :].bitcast(F16)
        SPL = TILES * HW
        h_hi = [stage16[:, (2 * r) * SPL:(2 * r + 1) * SPL].rearrange("p (t n) -> p t n", t=TILES) for r in range(2)]
        h_lo = [stage16[:, (2 * r + 1) * SPL:(2 * r + 2) * SPL].rearrange("p (t n) -> p t n", t=TILES) for r in range(2)]
        tc_buf = xs
        qv = xn
        gmax1 = sb("gmax1", [P, QGROUPS])
        gcol = sb("gcol", [QGROUPS, 1])
        gdiag = sb("gdiag", [QGROUPS, QGROUPS])
        s1 = sb("s1", [P, QGROUPS])
        s1e = sb("s1e", [P, QGROUPS])
        gmax2 = sb("gmax2", [C, 1])
        g2one = sb("g2one", [1, 1])
        s2e = sb("s2e", [C, 1])
        s2 = sb("s2", [C, QGROUPS])

        act_passed = sem("act_passed")
        dve_passed = sem("dve_passed")
        params_loaded = sem("params_loaded")
        gate_params = sem("gate_params")
        x_loaded = [sem(f"x_loaded{r}") for r in range(2)]
        ones_ready = sem("ones_ready")
        bigones_ready = sem("bigones_ready")
        setup_T = sem("setup_T")
        setup_dve = sem("setup_dve")
        fold_in = sem("fold_in")
        wsum_ready = sem("wsum_ready")
        lam_prod = sem("lam_prod")
        lam_sum = sem("lam_sum")
        lam_exp = sem("lam_exp")
        wmean_sum = sem("wmean_sum")
        gn_stats = sem("gn_stats")
        gn_mv_ready = sem("gn_mv_ready")
        gn_group = sem("gn_group")
        gn_avg_ready = sem("gn_avg_ready")
        gn_dev_ready = sem("gn_dev_ready")
        gn_dev2_ready = sem("gn_dev2_ready")
        gn_between = sem("gn_between")
        gn_var_ready = sem("gn_var_ready")
        gn_rstd = sem("gn_rstd")
        gn_coef = sem("gn_coef")
        xn_slab_ready = sem("xn_slab_ready")
        gates_done = sem("gates_done")
        logits_ready = sem("logits_ready")
        gate_exp_in = sem("gate_exp_in")
        gate_exp = sem("gate_exp")
        top_exp = sem("top_exp")
        present_ready = sem("present_ready")
        counts_ready = sem("counts_ready")
        conv_ready = sem("conv_ready")

        xs_loaded = [sem(f"xs_loaded{r}") for r in range(2)]
        xn_ready = sem("xn_ready")
        z_ready = sem("z_ready")
        h_ready = sem("h_ready")
        yx_ready = sem("yx_ready")
        tmp_ready = sem("tmp_ready")
        t1_ready = sem("t1_ready")
        ln_stats = sem("ln_stats")
        ln_mean = [sem("ln1_mean"), sem("ln2_mean")]
        ln_var = [sem("ln1_var"), sem("ln2_var")]
        ln_rstd = [sem("ln1_rstd"), sem("ln2_rstd")]
        ln2_bias = sem("ln2_bias")
        xh1_ready = sem("xh1_ready")
        xh2_ready = sem("xh2_ready")
        x1T_ready = sem("x1T_ready")
        xh1T_ready = sem("xh1T_ready")
        kv_ready = sem("kv_ready")
        e_ready = sem("e_ready")
        f_ready = sem("f_ready")
        a_ready = sem("a_ready")
        am_ready = sem("am_ready")
        stp_ready = sem("stp_ready")
        st_ready = sem("st_ready")
        rp_ready = sem("rp_ready")
        r_ready = sem("r_ready")
        d_ready = sem("d_ready")
        ao_ready = sem("ao_ready")
        t2_ready = sem("t2_ready")
        t2p_ready = sem("t2p_ready")
        t2T_evac = sem("t2T_evac")
        t2T_stored = [sem(f"t2T_stored{r}") for r in range(2)]
        x2p_ready = sem("x2p_ready")
        hi_ready = sem("hi_ready")
        lo_ready = sem("lo_ready")
        y_ready = sem("y_ready")
        ymax_done = sem("ymax_done")

        gmax_ready = sem("gmax_ready")
        gmaxT = sem("gmaxT")
        gdiag_ready = sem("gdiag_ready")
        gbc = sem("gbc")
        s1_ready = sem("s1_ready")
        y1_ready = sem("y1_ready")
        gelu_ready = sem("gelu_ready")
        hhi_ready = sem("hhi_ready")
        hlo_ready = sem("hlo_ready")
        y2_ready = sem("y2_ready")
        y2_evac = sem("y2_evac")
        y2max_done = sem("y2max_done")
        g2_ready = sem("g2_ready")
        g2T = sem("g2T")
        g2one_ready = sem("g2one_ready")
        g2bc = sem("g2bc")
        s2e_ready = sem("s2e_ready")
        s2_ready = sem("s2_ready")
        tc_loaded = [sem(f"tc_loaded{r}") for r in range(2)]
        qv_ready = sem("qv_ready")
        qc_ready = sem("qc_ready")
        ahi_ready = sem("ahi_ready")
        o_ready = sem("o_ready")
        o_stored = [sem(f"o_stored{r}") for r in range(2)]

        block = ctx.enter_context(nc.Block())

        x_bcn = x.rearrange("b c h w -> b c (h w)")
        out_bcn = out.rearrange("b c h w -> b c (h w)")

        FIRST, LAST = 4, BATCH
        N_PARAMS = 17
        CONSTS_SET = (ones_ready, 12)

        @block.sync
        def _(sp):
            for r in range(2):
                sp.dma_start(x_all[:, 4 * r:4 * r + 4, :],
                             x_bcn[4 * r:4 * r + 4].rearrange("b c n -> c b n")).then_inc(x_loaded[r], 16)
            with sp.Fori(1, SLABS) as s:
                for r in range(2):
                    sp.wait_ge(x_loaded[r], 16 * s)
                    b0 = s * SLAB + 4 * r
                    sp.dma_start(x_all[:, bass.ds(b0, 4), :],
                                 x_bcn[bass.ds(b0, 4)].rearrange("b c n -> c b n")).then_inc(x_loaded[r], 16)
            for r in range(2):
                sp.dma_start(xs[r][:, :], x_bcn[r]).then_inc(xs_loaded[r], 16)

            def step(m, r, load=True):
                i = 2 * m + r
                if load:
                    wait_count(sp, yx_ready, i + 1)
                    sp.dma_start(xs[r][:, :], x_bcn[i + 2]).then_inc(xs_loaded[r], 16)
                if not isinstance(i, int) or i >= 2:
                    sp.wait_ge(t2T_evac, i - 1)
                    sp.dma_start(out_bcn[i - 2], t2T[r][:, :]).then_inc(t2T_stored[r], 16)

            for m in range(FIRST // 2):
                for r in range(2):
                    step(m, r)
            with sp.Fori(FIRST // 2, LAST // 2 - 1) as m:
                for r in range(2):
                    step(m, r)
            for m in (LAST // 2 - 1, LAST // 2):
                for r in range(2):
                    step(m, r, load=False)
            for r in range(2):
                sp.wait_ge(t2T_stored[r], 16 * (BATCH // 2))

            def load_c(b, m, r):
                wait_count(sp, o_stored[r], 16 * m)
                sp.dma_start(tc_buf[r][:, :], out_bcn[b]).then_inc(tc_loaded[r], 16)

            def store_c(b, m, r):
                sp.wait_ge(o_ready, b + 1)
                sp.dma_start(out_bcn[b], tc_buf[r][:, :]).then_inc(o_stored[r], 16)

            for r in range(2):
                sp.dma_start(tc_buf[r][:, :], out_bcn[r]).then_inc(tc_loaded[r], 16)
            with sp.Fori(0, QIMAGES // 2 - 1) as m:
                for r in range(2):
                    store_c(2 * m + r, m, r)
                for r in range(2):
                    load_c(2 * m + 2 + r, m + 1, r)
            for r in range(2):
                store_c(QIMAGES - 2 + r, QIMAGES // 2 - 1, r)
            for r in range(2):
                sp.wait_ge(o_stored[r], 16 * (QIMAGES // 2))

        @block.gpsimd
        def _(pool):
            nc.gpsimd.memset(ones_b[:, :], 1.0).then_inc(ones_ready, 1)
            nc.gpsimd.memset(ones_f[:, :], 1.0).then_inc(ones_ready, 1)
            nc.gpsimd.memset(minus_one[:, :], -1.0).then_inc(ones_ready, 1)
            nc.gpsimd.memset(minus_ones[:, :], -1.0).then_inc(ones_ready, 1)
            nc.gpsimd.memset(ln_eps[:, :], LN_EPS).then_inc(ones_ready, 1)
            nc.gpsimd.memset(pow_half[:, :], -0.5).then_inc(ones_ready, 1)
            nc.gpsimd.memset(projb[:, :], 0.0).then_inc(ones_ready, 1)
            for e in range(E):
                nc.gpsimd.memset(prefer[:, e:e + 1], float(E - e)).then_inc(ones_ready, 1)
            pool.wait_ge(ones_ready, CONSTS_SET[1] - 1)
            nc.gpsimd.memset(xh1T[C:C + 1, :], 1.0).then_inc(ones_ready, 1)
            pool.wait_ge(*CONSTS_SET)
            with pool.Fori(0, SLABS) as s:
                pool.wait_ge(gn_var_ready, s + 1)
                nc.gpsimd.tensor_tensor(gn_scale[:, bass.ds(s * SLAB, SLAB)], gn_var[:, :],
                                        pow_half[0:C, 0:SLAB], ALU.pow).then_inc(gn_rstd, 1)
            pool.wait_ge(gn_rstd, SLABS)
            nc.gpsimd.memset(big[C:C + PARTS, 0:QIMAGES, 0, :], 1.0).then_inc(bigones_ready, 1)
            pool.wait_ge(bigones_ready, 1)

            def rstd(n, b):
                pool.wait_ge(ln_mean[n], b + 1)
                nc.gpsimd.tensor_tensor(ln_ve[n][:, :], ln_mv[n][:, :, 1], ln_eps[:, :],
                                        ALU.add).then_inc(ln_var[n], 1)
                pool.wait_ge(ln_var[n], b + 1 if n == 0 else 2 * b + 1)
                nc.gpsimd.tensor_tensor(ln_rs[n][:, :], ln_ve[n][:, :], pow_half[0:TOK, 0:CHUNKS],
                                        ALU.pow).then_inc(ln_rstd[n], 1)
                if n == 1:
                    nc.gpsimd.tensor_tensor(ln_nm[:, :], ln_mv[n][:, :, 0], minus_ones[:, :],
                                            ALU.mult).then_inc(ln_var[n], 1)
                    pool.wait_ge(ln_rstd[n], b + 1)
                    pool.wait_ge(ln_var[n], 2 * b + 2)
                    nc.gpsimd.tensor_tensor(ln_nb[:, :], ln_nm[:, :], ln_rs[n][:, :],
                                            ALU.mult).then_inc(ln2_bias, 1)

            def step(i):
                rstd(0, i)
                rstd(1, i - 1)

            rstd(0, 0)
            with pool.Fori(1, LAST) as i:
                step(i)

            def finish(m, r):
                pool.wait_ge(tc_loaded[r], 16 * (m + 1))
                pool.wait_ge(qc_ready, 2 * m + r + 1)
                nc.gpsimd.tensor_tensor(tc_buf[r][:, :], tc_buf[r][:, :], qv[r][:, :], ALU.add).then_inc(o_ready, 1)

            with pool.Fori(0, QIMAGES // 2) as m:
                for r in range(2):
                    finish(m, r)

        @block.scalar
        def _(act):
            def load(dst, src):
                act.dma_start(dst, src).then_inc(params_loaded, 16)

            act.dma_start(con[:, :], consts).then_inc(gate_params, 16)
            act.dma_start(gw[:, :], gate_w).then_inc(gate_params, 16)
            load(w1_raw[:, :, :], w1.rearrange("e d c -> d e c"))
            load(w2_raw[:, :, :], w2.rearrange("e o d -> o e d"))
            load(b1c[:, :], b1.rearrange("e d -> (e d)").rearrange("(t p) -> p t", p=P))
            load(b2all[:, :, :], b2.rearrange("(a e) o -> a e o", a=1).to_broadcast([P, E, C]))
            load(gb[:, :], gate_b.rearrange("(a e) -> a e", a=1).to_broadcast([TOK, E]))
            load(qkvw[0:C, :], qkv_w)
            load(qkvw[C:C + 1, :], qkv_b.rearrange("(a n) -> a n", a=1))
            load(projw[:, :], proj_w)
            for n, l in enumerate((lk1, lv1, lk2, lv2)):
                load(lam[:, n:n + 1], l.rearrange("h (d a) -> (h d) a", a=1))
            load(W1_raw[:, :, :], W1.rearrange("(t p) c -> p t c", p=P))
            load(fb1r[C:C + PARTS, :], fb1.rearrange("(a n) -> a n", a=1).to_broadcast([PARTS, HID]))
            load(W2_raw[:, :], W2)
            load(fb2c[:, :], fb2.rearrange("(c a) -> c a", a=1))
            act.wait_ge(*CONSTS_SET)
            load(projb[0:1, :], proj_b.rearrange("(a n) -> a n", a=1))

            def norm_half(s, h):
                u = 2 * s + h
                if h == 0:
                    wait_apart(act, gn_coef, s + 1, act_passed)
                wait_count(act, gates_done, u - 1)
                if not isinstance(u, int):
                    act.sem_inc(act_passed, 1)
                for j in range(4 * h, 4 * h + 4):
                    b = s * SLAB + j
                    ins = nc.scalar.activation(xn_slab[:, j, :], x_all[:, b, :], ACT.Identity,
                                               scale=gn_scale[:, bass.ds(b, 1)], bias=gn_shift[:, bass.ds(b, 1)])
                ins.then_inc(xn_slab_ready, 1)

            def logits_out(s, h):
                wait_apart(act, gates_done, 2 * s + h + 1, act_passed)
                nc.scalar.copy(logits[:, bass.ds((2 * s + h) * NH, NH), :],
                               S[1][0:TOK, h, 0:NH * E].rearrange("p (n e) -> p n e", e=E)).then_inc(logits_ready, 1)

            NH = 4 * CHUNKS
            norm_half(0, 0)
            norm_half(0, 1)
            logits_out(0, 0)
            with act.Fori(1, SLABS) as s:
                norm_half(s, 0)
                logits_out(s - 1, 1)
                norm_half(s, 1)
                logits_out(s, 0)
            logits_out(SLABS - 1, 1)
            act.wait_ge(lam_sum, 1)
            nc.scalar.activation(lam_e[:, 0:2], S[2][0:C, 0, 400:402], ACT.Exp).then_inc(lam_exp, 1)
            act.wait_ge(gate_exp_in, 1)
            nc.scalar.activation(logits[:, :, :], logits[:, :, :], ACT.Exp).then_inc(gate_exp, 1)
            act.wait_ge(gate_exp_in, 2)
            nc.scalar.activation(top[:, 2, :], top[:, 2, :], ACT.Exp).then_inc(top_exp, 1)

            def norm_image(m, r, i):
                act.wait_ge(xs_loaded[r], 16 * (m + 1))
                if isinstance(i, int):
                    wait_count(act, z_ready, 3 * (i - 1))
                else:
                    wait_apart(act, z_ready, 3 * (i - 1), act_passed)
                nc.scalar.activation(xn[r][:, :], xs[r][:, :], ACT.Identity, scale=gn_scale[:, bass.ds(i, 1)],
                                     bias=gn_shift[:, bass.ds(i, 1)]).then_inc(xn_ready, 1)

            def channels(dst, k):
                return (dst.rearrange("p (j t) -> p j t", t=TOK),
                        flat(k)[0:C, 0:CHUNKS * P].rearrange("p (j t) -> p j t", t=P)[:, :, 0:TOK])

            def step(m, r, s1_=True, s2_=True, s3=True, ffn=True, next_=True):
                i = 2 * m + r
                one, other = one_other(r)
                for t in range(TILES):
                    if s1_:
                        act.wait_ge(z_ready, 3 * i + t + 1)
                        nc.scalar.activation(hT[:, t, :].rearrange("p (a n) -> p a n", a=2),
                                             halves((0, one, 0)[t], P),
                                             ACT.Relu, bias=b1c[:, t:t + 1]).then_inc(h_ready, 1)
                    if s2_ and t == 1:
                        act.wait_ge(x1T_ready, i)
                        nc.scalar.copy(*channels(xh1T[0:C, :], 2)).then_inc(xh1T_ready, 1)
                if s2_:
                    for q, (k, j0, n) in enumerate(((other, 0, CH_A), (2, CH_A, CHUNKS - CH_A))):
                        act.wait_ge(kv_ready, 2 * (i - 1) + q + 1)
                        nc.scalar.activation(ekv[:, j0:j0 + n, :], chunks(k, n, 256, 2 * C), ACT.Exp,
                                             bias=minus_one[:, :]).then_inc(e_ready, 1)
                if s3 and ffn:
                    act.wait_ge(ln2_bias, i - 1)
                    for j in range(CHUNKS):
                        ins = nc.scalar.activation(xh2[:, j, :], t2[:, j, :], ACT.Identity,
                                                   scale=ln_rs[1][:, j:j + 1], bias=ln_nb[:, j:j + 1])
                    ins.then_inc(xh2_ready, 1)
                if s3:
                    act.wait_ge(t2p_ready, i - 1)
                    wait_count(act, t2T_stored[r], 16 * (m - 1))
                    nc.scalar.copy(*channels(t2T[r][:, :], one)).then_inc(t2T_evac, 1)
                    if ffn:
                        wait_apart(act, x2p_ready, i - 1, act_passed)
                        nc.scalar.copy(*channels(big[0:C, i - 2, 0, :], 0)).then_inc(hi_ready, 1)
                if s1_ and next_:
                    norm_image(m + r, 1 - r, i + 1)
                if s2_:
                    act.wait_ge(stp_ready, i)
                    nc.scalar.copy(St[:, :], S[one][0:C, 1, 0:C + 1]).then_inc(st_ready, 1)
                    act.wait_ge(rp_ready, i)
                    nc.scalar.copy(R[:, :], S[one][0:C + 1, 0, 0:C]).then_inc(r_ready, 1)

            norm_image(0, 0, 0)
            for i in range(FIRST):
                step(i // 2, i % 2, s2_=i >= 1, s3=i >= 2)
            with act.Fori(FIRST // 2, LAST // 2 - 1) as m:
                for r in range(2):
                    step(m, r)
            step(LAST // 2 - 1, 0)
            step(LAST // 2 - 1, 1, next_=False)
            step(LAST // 2, 0, s1_=False, ffn=False)
            step(LAST // 2, 1, s1_=False, s2_=False, ffn=False)

            act.wait_ge(s1_ready, 1)

            def gelu_tile(g, b, t, r):
                wait_count(act, hlo_ready, 3 * b + t - 2)
                wait_apart(act, y1_ready, 3 * b + t + 1, act_passed)
                nc.scalar.activation(gel[:, t, :].rearrange("p (a n) -> p a n", a=2), halves(y1_slot(r, t), P),
                                     ACT.Gelu, scale=s1[:, bass.ds(g, 1)]).then_inc(gelu_ready, 1)

            def gelu_hi(b, t, r):
                wait_apart(act, gelu_ready, 3 * b + t + 1, act_passed)
                if t == 0:
                    wait_count(act, y2_ready, b - 1)
                    if not isinstance(b, int):
                        act.sem_inc(act_passed, 1)
                nc.scalar.copy(h_hi[r][:, t, :], gel[:, t, :]).then_inc(ahi_ready, 1)

            def y2_out(b, r):
                wait_apart(act, y2_ready, b + 1, act_passed)
                nc.scalar.activation(y2_all[:, b, :].rearrange("p (a n) -> p a n", a=2), halves(2 + r, C),
                                     ACT.Identity, bias=fb2c[:, 0:1]).then_inc(y2_evac, 1)

            def ffn(g, m):
                for r in range(2):
                    b = 2 * m + r
                    gelu_tile(g, b, 0, r)
                    gelu_tile(g, b, 1, r)
                    gelu_hi(b, 0, r)
                    gelu_tile(g, b, 2, r)
                    gelu_hi(b, 1, r)
                    if not (isinstance(b, int) and b == 0):
                        y2_out(b - 1, 1 - r)

            ffn(0, 0)
            with act.Fori(1, QB // 2) as q:
                ffn(0, q)
            with act.Fori(1, QGROUPS) as g:
                with act.Fori(0, QB // 2) as q:
                    ffn(g, g * (QB // 2) + q)
            y2_out(QIMAGES - 1, 1)

        @block.tensor
        def _(pe):
            mm = nc.tensor.matmul

            def tr(o, i, start=True):
                rows = i.shape[0]
                return mm(o, i, ident[0:rows, 0:rows], start=start, stop=True, is_transpose=True,
                          skip_group_check=True)

            def slab(s):
                pe.wait_ge(gn_mv_ready, 2 * s + 2)
                mm(S[0][0:C, 0, 0:2 * SLAB], con[0:C, K_GROUP:K_GROUP + C],
                   gn_mv[:, :, :].rearrange("p j k -> p (j k)"), start=True, stop=True).then_inc(gn_group, 1)
                pe.wait_ge(gn_dev2_ready, s + 1)
                mm(S[0][0:C, 1, 0:SLAB], con[0:C, K_GROUP:K_GROUP + C], gn_dev2[:, :],
                   start=True, stop=True).then_inc(gn_between, 1)
                for h in range(2):
                    pe.wait_ge(xn_slab_ready, 2 * s + h + 1)
                    wait_count(pe, logits_ready, 2 * s + h - 1)
                    for j in range(4):
                        for c in range(CHUNKS):
                            n = (j * CHUNKS + c) * E
                            ins = mm(S[1][0:TOK, h, n:n + E], xn_slab[:, 4 * h + j, c * TOK:(c + 1) * TOK], gw[:, :],
                                     start=True, stop=True, skip_group_check=True)
                    ins.then_inc(gates_done, 1)

            pe.wait_ge(gate_params, 32)
            pe.wait_ge(*CONSTS_SET)
            slab(0)
            pe.wait_ge(params_loaded, 16 * N_PARAMS)
            for e in range(E):
                tr(S[2][0:C, 0, e * C:(e + 1) * C], w1_raw[:, e, :])
            for t in range(TILES):
                tr(S[2][:, 1, t * C:(t + 1) * C],
                   w2_raw[:, :, :].rearrange("p e d -> p (e d)")[:, t * P:(t + 1) * P])
            tr(S[2][0:C, 1, HID:HID + C + 1], qkvw[:, 0:C])
            for t in range(TILES):
                tr(S[3][0:C, 0, t * P:(t + 1) * P], W1_raw[:, t, :])
            for t in range(TILES):
                ins = tr(S[3][:, 1, t * C:(t + 1) * C], W2_raw[:, t * P:(t + 1) * P])
            ins.then_inc(setup_T, 1)
            with pe.Fori(1, SLABS) as s:
                slab(s)
            pe.wait_ge(wsum_ready, 1)
            pe.wait_ge(lam_prod, 1)
            mm(S[2][0:C, 0, 400:402], con[0:C, K_HEAD:K_HEAD + C], lam_e[:, 2:4],
               start=True, stop=True, skip_group_check=True).then_inc(lam_sum, 1)
            mm(S[3][0:C, 0, 400:400 + QGROUPS], ones_f[0:C, 0:C], wsum[0:C, 0, :], start=True, stop=True,
               skip_group_check=True)
            mm(S[3][:, 1, 400:400 + QGROUPS], ones_f[:, :], wsum[:, 1, :], start=True, stop=True,
               skip_group_check=True).then_inc(wmean_sum, 1)
            pe.wait_ge(fold_in, 1)

            pe.wait_ge(present_ready, 1)
            mm(S[0][:, 0, 0:2 * E], ones_f[0:TOK, :], present[:, :, :].rearrange("p k e -> p (k e)"),
               start=True, stop=True).then_inc(counts_ready, 1)

            pe.wait_ge(conv_ready, 1)
            pe.wait_ge(bigones_ready, 1)

            mixed = pe.value_load(differ[0:1, 0:1], min_val=0, max_val=1)

            def hidden(t, k, r, i):
                for h in range(2):
                    ins = mm(S[k][:, h, 0:HALF], w1T[:, t * P:(t + 1) * P],
                             xn[r][:, h * HALF:(h + 1) * HALF], start=True, stop=True)
                ins.then_inc(z_ready, 1)

            def to_channels(k, src, done):
                for j in range(CHUNKS):
                    ins = tr(flat(k)[0:C, j * P:j * P + TOK], src[:, j, :], start=j % CH_A == 0)
                ins.then_inc(done, 1)

            def mix(v, k, r, with_x, part):
                o = chunks(k, CHUNKS, P, C)
                j0, n = ((0, CH_A), (CH_A, CHUNKS - CH_A))[part]
                if with_x:
                    for j in range(j0, j0 + n):
                        tr(o[:, j, :], xs[r][:, j * TOK:(j + 1) * TOK], start=j == j0)
                mm(o[:, j0:j0 + n, :], ones_b[:, :], bias2_parts[:, v, 0:n, :],
                   start=not with_x, stop=False, skip_group_check=True)
                for j in range(j0, j0 + n):
                    for t in range(TILES):
                        ins = mm(o[:, j, :], hT[:, t, j * TOK:(j + 1) * TOK], w2s[:, v, t, :],
                                 start=False, stop=t == TILES - 1, skip_group_check=True)
                return ins

            def ffn_tile(f, t, k):
                w = W1b[:, t * P:(t + 1) * P]
                for h in range(2):
                    mm(S[k][:, h, 0:HALF], w, big[:, f, 0, h * HALF:(h + 1) * HALF],
                       start=True, stop=False, skip_group_check=True)
                for h in range(2):
                    ins = mm(S[k][:, h, 0:HALF], w[0:C, :], big[0:C, f, 1, h * HALF:(h + 1) * HALF],
                             start=False, stop=True, skip_group_check=True)
                return ins

            def step(m, r, s1_=True, s2_=True, s3=True, ffn=True):
                i = 2 * m + r
                one, other = one_other(r)
                if s1_:
                    pe.wait_ge(xn_ready, i + 1)
                    wait_count(pe, ymax_done, 3 * (i - 3) + 1)
                    hidden(0, 0, r, i)
                    wait_count(pe, ymax_done, 3 * (i - 3) + 3)
                    wait_count(pe, t1_ready, i)
                    hidden(1, one, r, i)
                if s2_:
                    pe.wait_ge(xh1_ready, i)
                    wait_count(pe, ymax_done, 3 * (i - 3) + 2)
                    to_channels(2, xh1, x1T_ready)
                if s1_:
                    pe.wait_ge(h_ready, 3 * i + 1)
                    hidden(2, 0, r, i)
                if s2_:
                    pe.wait_ge(xh1T_ready, i)
                    wait_count(pe, t2_ready, i - 1)
                    for k, j0, n in ((other, 0, CH_A), (2, CH_A, CHUNKS - CH_A)):
                        for j in range(n):
                            ins = mm(chunks(k, n, 256, 2 * C)[:, j, :], xh1T[:, (j0 + j) * TOK:(j0 + j + 1) * TOK],
                                     qkvw[:, C:3 * C], start=True, stop=True, skip_group_check=True)
                        ins.then_inc(kv_ready, 1)
                if s1_:
                    pe.wait_ge(h_ready, 3 * i + 2)
                if s3:
                    pe.wait_ge(t2_ready, i - 1)
                    if not s1_ and s2_:
                        pe.wait_ge(ymax_done, 3 * QIMAGES)
                    to_channels(one, t2, t2p_ready)
                if s1_:
                    pe.wait_ge(h_ready, 3 * i + 3)
                    if s2_:
                        pe.wait_ge(f_ready, 2 * i - 1)
                    mix(1, other, r, True, 0)
                if s3 and ffn:
                    pe.wait_ge(xh2_ready, i - 1)
                    to_channels(0, xh2, x2p_ready)
                if s1_:
                    mix(1, other, r, True, 1).then_inc(yx_ready, 1)
                    if s2_:
                        pe.wait_ge(f_ready, 2 * i)
                    with pe.If(mixed):
                        mix(0, 2, r, False, 0)
                        mix(0, 2, r, False, 1).then_inc(d_ready, 1)
                if s2_:
                    pe.wait_ge(f_ready, 2 * i)
                    if s3:
                        pe.wait_ge(t2T_evac, i - 1)
                    for j in range(CHUNKS):
                        ins = mm(S[one][0:C, 0, 0:C], fkv[:, j, 0:C], fkv[:, j, C:2 * C],
                                 start=j == 0, stop=j == CHUNKS - 1)
                    ins.then_inc(a_ready, 1)
                if s3 and ffn:
                    pe.wait_ge(hi_ready, i - 1)
                    pe.wait_ge(lo_ready, i - 1)
                    ffn_tile(i - 2, 0, 0).then_inc(y_ready, 1)
                if s2_:
                    pe.wait_ge(am_ready, i)
                    mm(S[one][0:C, 1, 0:C + 1], Am[:, :], wqT[:, :], start=True, stop=True).then_inc(stp_ready, 1)
                    mm(S[one][0:C + 1, 0, 0:C], con[0:C, K_LAST:K_LAST + C + 1], projb[:, :],
                       start=True, stop=False)
                if s3 and ffn:
                    pe.wait_ge(t1_ready, i + 1)
                    ffn_tile(i - 2, 1, 2).then_inc(y_ready, 1)
                if s2_:
                    pe.wait_ge(st_ready, i)
                    mm(S[one][0:C + 1, 0, 0:C], St[:, :], projw[:, :], start=False, stop=True).then_inc(rp_ready, 1)
                if s3 and ffn:
                    ffn_tile(i - 2, 2, other).then_inc(y_ready, 1)
                if s2_:
                    pe.wait_ge(r_ready, i)
                    for j in range(CHUNKS):
                        ins = mm(flat(one)[0:TOK, j * P:j * P + C], xh1T[:, j * TOK:(j + 1) * TOK], R[:, :],
                                 start=True, stop=True, skip_group_check=True)
                    ins.then_inc(ao_ready, 1)

            for i in range(FIRST):
                step(i // 2, i % 2, s2_=i >= 1, s3=i >= 2)
            with pe.Fori(FIRST // 2, LAST // 2) as m:
                for r in range(2):
                    step(m, r)
            step(LAST // 2, 0, s1_=False, ffn=False)
            step(LAST // 2, 1, s1_=False, s2_=False, ffn=False)

            pe.wait_ge(gmax_ready, 1)
            pe.wait_ge(t2T_evac, BATCH)
            tr(S[0][0:QGROUPS, 0, 0:P], gmax1[:, :]).then_inc(gmaxT, 1)
            pe.wait_ge(gdiag_ready, 1)
            mm(S[0][:, 1, 0:QGROUPS], ones_f[0:QGROUPS, :], gdiag[:, :], start=True, stop=True).then_inc(gbc, 1)
            pe.wait_ge(s1_ready, 1)

            def ffn_up(b, r):
                for t in range(TILES):
                    wait_count(pe, gelu_ready, 3 * b + t - 1)
                    ffn_tile(b, t, y1_slot(r, t)).then_inc(y1_ready, 1)

            def ffn_down(b, r):
                k = 2 + r
                wait_count(pe, y2_evac, b - 1)
                for t in range(TILES):
                    pe.wait_ge(hlo_ready, 3 * b + t + 1)
                    for part, src in enumerate((h_hi[r], h_lo[r])):
                        for h in range(2):
                            ins = mm(S[k][0:C, h, 0:HALF], W2b[:, t, :], src[:, t, h * HALF:(h + 1) * HALF],
                                     start=t == 0 and part == 0, stop=t == TILES - 1 and part == 1,
                                     skip_group_check=True)
                ins.then_inc(y2_ready, 1)

            def group_scale(g):
                pe.wait_ge(g2_ready, g + 1)
                tr(S[3][0:1, 0, 400:400 + C], gmax2[:, :]).then_inc(g2T, 1)
                pe.wait_ge(g2one_ready, g + 1)
                mm(S[3][0:C, 1, 400:401], ones_f[0:1, 0:C], g2one[:, :], start=True, stop=True,
                   skip_group_check=True).then_inc(g2bc, 1)

            def ffn_pair(m, scale=None, last=False):
                for r in range(2):
                    b = 2 * m + r
                    if not (last and r == 1):
                        ffn_up(b + 1, 1 - r)
                    if scale is not None and r == 0:
                        group_scale(scale)
                    ffn_down(b, r)

            ffn_up(0, 0)
            ffn_pair(0)
            with pe.Fori(1, QB // 2) as q:
                ffn_pair(q)
            with pe.Fori(1, QGROUPS - 1) as g:
                ffn_pair(g * (QB // 2), scale=g - 1)
                with pe.Fori(1, QB // 2) as q:
                    ffn_pair(g * (QB // 2) + q)
            g = QGROUPS - 1
            ffn_pair(g * (QB // 2), scale=g - 1)
            ffn_pair(g * (QB // 2) + 1)
            ffn_pair(g * (QB // 2) + 2, last=True)
            group_scale(g)

        @block.vector
        def _(dve):
            V = nc.vector
            links = [0]

            def link(ins):
                links[0] += 1
                ins.then_inc(setup_dve, 1)
                dve.wait_ge(setup_dve, links[0])

            def gn_half(s, r):
                dve.wait_ge(x_loaded[r], 16 * (s + 1))
                for j in range(4 * r, 4 * r + 4):
                    for h in range(2):
                        ins = V.bn_stats(gn_st[:, j, h, :], x_all[:, s * SLAB + j, h * HALF:(h + 1) * HALF])
                ins.then_inc(gn_stats, 1)
                wait_apart(dve, gn_stats, 2 * s + r + 1, dve_passed)
                for j in range(4 * r, 4 * r + 4):
                    ins = V.bn_aggr(gn_mv[:, j, :], gn_st[:, j, :, :].rearrange("p h k -> p (h k)"))
                ins.then_inc(gn_mv_ready, 1)

            def gn_groups(s):
                dve.wait_ge(gn_group, s + 1)
                V.tensor_copy(gn_avg[:, :, :].rearrange("p j k -> p (j k)"),
                              S[0][0:C, 0, 0:2 * SLAB]).then_inc(gn_avg_ready, 1)
                dve.wait_ge(gn_avg_ready, s + 1)
                V.tensor_tensor(gn_dev[:, :], gn_mv[:, :, 0], gn_avg[:, :, 0], ALU.subtract).then_inc(gn_dev_ready, 1)
                dve.wait_ge(gn_dev_ready, s + 1)
                V.tensor_tensor(gn_dev2[:, :], gn_dev[:, :], gn_dev[:, :], ALU.mult).then_inc(gn_dev2_ready, 1)
                dve.wait_ge(gn_between, s + 1)
                V.scalar_tensor_tensor(gn_var[:, :], S[0][0:C, 1, 0:SLAB], GN_EPS, gn_avg[:, :, 1],
                                       ALU.add, ALU.add).then_inc(gn_var_ready, 1)

            def gn_shifts(s):
                dve.wait_ge(gn_rstd, s + 1)
                V.scalar_tensor_tensor(gn_shift[:, bass.ds(s * SLAB, SLAB)], gn_avg[:, :, 0], -1.0,
                                       gn_scale[:, bass.ds(s * SLAB, SLAB)], ALU.mult, ALU.mult).then_inc(gn_coef, 1)

            gn_half(0, 0)
            gn_half(0, 1)
            gn_groups(0)
            gn_shifts(0)
            with dve.Fori(1, SLABS) as s:
                gn_half(s, 0)
                gn_half(s, 1)
                gn_groups(s)
                gn_shifts(s)

            dve.wait_ge(params_loaded, 16 * N_PARAMS)
            dve.wait_ge(*CONSTS_SET)
            V.tensor_tensor(lam_e[:, 2:4], lam[:, 0:4:2], lam[:, 1:4:2], ALU.mult).then_inc(lam_prod, 1)
            dve.wait_ge(setup_T, 1)
            V.tensor_copy(w1T[:, :], S[2][0:C, 0, 0:HID])
            V.tensor_copy(w2T[:, :, :], S[2][:, 1, 0:TILES * C].rearrange("p (t c) -> p t c", c=C))
            V.tensor_scalar(wqT[:, :], S[2][0:C, 1, HID:HID + C + 1], float(HD) ** -0.5, None, ALU.mult)
            V.tensor_copy(W1f[:, :], S[3][0:C, 0, 0:HID])
            link(V.tensor_copy(W2f[:, :, :], S[3][:, 1, 0:TILES * C].rearrange("p (t c) -> p t c", c=C)))
            V.tensor_scalar(qkvw[C:C + 1, C:3 * C], qkvw[C:C + 1, C:3 * C], 1.0, None, ALU.add)
            W1v = W1f[:, 0:QGROUPS * W1_GS].rearrange("p (g n) -> p g n", n=W1_GS)
            V.tensor_reduce(wsum[0:C, 0, :], W1v, AX.X, ALU.add)
            V.tensor_reduce(wsum[:, 1, :], W2f[:, :, 0:QGROUPS * W2_GS].rearrange("p t (g n) -> p g t n", n=W2_GS),
                            AX.XY, ALU.add).then_inc(wsum_ready, 1)
            V.memset(W1b[0:C, QGROUPS * W1_GS:HID], 0.0)
            V.memset(W2b[:, :, QGROUPS * W2_GS:C], 0.0)
            dve.wait_ge(wmean_sum, 1)
            V.tensor_scalar(wmean[0:C, 0, :], S[3][0:C, 0, 400:400 + QGROUPS], 1.0 / (W1_GS * C), None, ALU.mult)
            link(V.tensor_scalar(wmean[:, 1, :], S[3][:, 1, 400:400 + QGROUPS], 1.0 / (W2_GS * HID), None, ALU.mult))
            m1 = wmean[0:C, 0, :].rearrange("p (g a) -> p g a", a=1).to_broadcast([C, QGROUPS, W1_GS])
            pa = part_a[0:C, 0:QGROUPS * W1_GS].rearrange("p (g n) -> p g n", n=W1_GS)
            pb = part_b[0:C, 0:QGROUPS * W1_GS].rearrange("p (g n) -> p g n", n=W1_GS)
            V.tensor_tensor(pa, W1v, m1, ALU.is_gt)
            link(V.tensor_tensor(pb, W1v, m1, ALU.is_lt))
            link(V.tensor_tensor(W1b[0:C, 0:QGROUPS * W1_GS].rearrange("p (g n) -> p g n", n=W1_GS),
                                 pa, pb, ALU.subtract))
            m2 = wmean[:, 1, :].rearrange("p (g a) -> p g a", a=1).to_broadcast([P, QGROUPS, W2_GS])
            for t in range(TILES):
                w = W2f[:, t, 0:QGROUPS * W2_GS].rearrange("p (g n) -> p g n", n=W2_GS)
                V.tensor_tensor(part_a[:, t * C:t * C + QGROUPS * W2_GS].rearrange("p (g n) -> p g n", n=W2_GS),
                                w, m2, ALU.is_gt)
                ins = V.tensor_tensor(part_b[:, t * C:t * C + QGROUPS * W2_GS].rearrange(
                    "p (g n) -> p g n", n=W2_GS), w, m2, ALU.is_lt)
            link(ins)
            for t in range(TILES):
                n = QGROUPS * W2_GS
                ins = V.tensor_tensor(W2b[:, t, 0:n], part_a[:, t * C:t * C + n], part_b[:, t * C:t * C + n],
                                      ALU.subtract)
            link(ins)

            def bf16_parts(dst, src, rows, width, masks):
                a, b, h = part_a[rows, 0:width], part_b[rows, 0:width], part_h[rows, 0:width]
                if len(src.shape) == 3:
                    a, b, h = (v.rearrange("p (v c) -> p v c", v=src.shape[1]) for v in (a, b, h))
                link(V.tensor_copy(h, src))
                link(V.tensor_scalar(a, h, masks[:, 0:1], None, ALU.mult))
                link(V.tensor_tensor(b, src, h, ALU.subtract))
                link(V.tensor_copy(h, b))
                link(V.scalar_tensor_tensor(a, h, masks[:, 1:2], a, ALU.mult, ALU.add))
                link(V.tensor_tensor(b, b, h, ALU.subtract))
                link(V.scalar_tensor_tensor(dst, b, masks[:, 2:3], a, ALU.mult, ALU.add))

            rows = slice(C, C + PARTS)
            bf16_parts(W1b[rows, :], fb1r[rows, :], rows, HID, con[rows, K_PART96:K_PART96 + PARTS])
            dve.wait_ge(lam_exp, 1)
            link(V.tensor_tensor(lam_e[:, 2:3], lam_e[:, 0:1], lam_e[:, 1:2], ALU.subtract))
            link(V.tensor_scalar(lam_e[:, 3:4], lam_e[:, 2:3], LAMBDA_INIT, None, ALU.add))
            link(V.tensor_scalar(lam_e[:, 2:3], lam_e[:, 3:4], -1.0, 1.0, ALU.mult, ALU.add))
            V.tensor_scalar(gauss[:, :], con[0:C, K_GAUSS:K_GAUSS + C], lam_e[:, 2:3], None,
                            ALU.mult).then_inc(fold_in, 1)

            def bc(v):
                return v.rearrange("p (n a) -> p n a", a=1).to_broadcast([TOK, NT, E])

            sv = stage[0:TOK, :]
            first = sv[:, 0:NT * E].rearrange("p (n e) -> p n e", e=E)
            second = sv[:, NT * E:2 * NT * E].rearrange("p (n e) -> p n e", e=E)
            work = sv[:, 2 * NT * E:3 * NT * E].rearrange("p (n e) -> p n e", e=E)
            gbv = gb[:, :].rearrange("p (a e) -> p a e", a=1).to_broadcast([TOK, NT, E])
            pref = prefer[:, :].rearrange("p (a e) -> p a e", a=1).to_broadcast([TOK, NT, E])
            dve.wait_ge(gates_done, 2 * SLABS)
            dve.wait_ge(logits_ready, 2 * SLABS)
            link(V.tensor_tensor(logits[:, :, :], logits[:, :, :], gbv, ALU.add))
            link(V.tensor_reduce(top[:, 0, :], logits[:, :, :], AX.X, ALU.max))
            V.tensor_tensor(logits[:, :, :], logits[:, :, :], bc(top[:, 0, :]), ALU.subtract).then_inc(gate_exp_in, 1)
            dve.wait_ge(gate_exp, 1)
            link(V.tensor_reduce(top[:, 1, :], logits[:, :, :], AX.X, ALU.add))
            link(V.reciprocal(top[:, 0, :], top[:, 1, :]))
            link(V.tensor_tensor(logits[:, :, :], logits[:, :, :], bc(top[:, 0, :]), ALU.mult))

            def pick(onehot, value):
                link(V.tensor_reduce(value, logits[:, :, :], AX.X, ALU.max))
                link(V.tensor_tensor(work, logits[:, :, :], bc(value), ALU.is_equal))
                link(V.tensor_tensor(work, work, pref, ALU.mult))
                link(V.tensor_reduce(top[:, 3, :], work, AX.X, ALU.max))
                link(V.tensor_tensor(onehot, work, bc(top[:, 3, :]), ALU.is_equal))

            pick(first, top[:, 0, :])
            link(V.scalar_tensor_tensor(logits[:, :, :], first, -2.0, logits[:, :, :], ALU.mult, ALU.add))
            pick(second, top[:, 1, :])
            V.tensor_reduce(present[:, 0, :], first.rearrange("p n e -> p e n"), AX.X, ALU.max)
            V.tensor_reduce(present[:, 1, :], second.rearrange("p n e -> p e n"), AX.X, ALU.max).then_inc(present_ready, 1)
            V.tensor_tensor(top[:, 2, :], top[:, 1, :], top[:, 0, :], ALU.subtract).then_inc(gate_exp_in, 1)
            dve.wait_ge(top_exp, 1)
            link(V.tensor_scalar(top[:, 3, :], top[:, 2, :], 1.0, None, ALU.add))
            V.reciprocal(w0[:, :], top[:, 3, :])
            dve.wait_ge(counts_ready, 1)
            link(V.tensor_scalar(flags[:, :, :].rearrange("p k e -> p (k e)"), S[0][:, 0, 0:2 * E], 1.0, None, ALU.min))
            link(V.tensor_tensor(flags[:, 0, :], flags[:, 0, :], flags[:, 1, :], ALU.subtract))
            expert = con[:, K_EXPERT:K_EXPERT + TILES * E].rearrange("p (t e) -> p t e", e=E)
            for v in range(2):
                fl = flags[:, v, :].rearrange("p (a e) -> p a e", a=1).to_broadcast([P, TILES, E])
                link(V.tensor_tensor(flag_tmp[:, :, :], expert, fl, ALU.mult))
                link(V.tensor_reduce(row_flag[:, v, :], flag_tmp[:, :, :], AX.X, ALU.add))
            for t in range(TILES):
                for v in range(2):
                    V.tensor_scalar(w2s[:, v, t, :], w2T[:, t, :], row_flag[:, v, t:t + 1], None, ALU.mult)
            for v in range(2):
                fl = flags[:, v, :].rearrange("p (e a) -> p e a", a=1).to_broadcast([P, E, C])
                tv = part_a[:, :].rearrange("p (e c) -> p e c", c=C)
                link(V.tensor_tensor(tv, b2all[:, :, :], fl, ALU.mult))
                link(V.tensor_reduce(bias2[:, v, :], tv.rearrange("p e c -> p c e"), AX.X, ALU.add))
            bf16_parts(bias2_parts[:, :, 0, :], bias2[:, :, :], slice(0, P), 2 * C,
                       con[:, K_PART:K_PART + PARTS])
            for n in range(1, CH_A):
                V.tensor_copy(bias2_parts[:, :, n, :], bias2_parts[:, :, 0, :])
            link(V.tensor_reduce(differ_f[:, :], flags[0:1, 0, :], AX.X, ALU.max, apply_absolute_value=True))
            V.tensor_copy(differ[:, :], differ_f[:, :]).then_inc(conv_ready, 1)
            dve.wait_ge(conv_ready, 1)
            mixed = dve.value_load(differ[0:1, 0:1], min_val=0, max_val=1)

            def mask_a(i, k):
                dve.wait_ge(a_ready, i)
                V.tensor_tensor(Am[:, :], S[k][0:C, 0, 0:C], gauss[:, :], ALU.mult).then_inc(am_ready, 1)

            def stats(n, src, b, count, mask=None):
                for j in range(CHUNKS):
                    ins = V.bn_stats(ln_st[:, j, :], src[:, j, :])
                ins.then_inc(ln_stats, 1)
                if mask is not None:
                    mask_a(b, mask)
                wait_apart(dve, ln_stats, count, dve_passed)
                for j in range(CHUNKS):
                    ins = V.bn_aggr(ln_mv[n][:, j, :], ln_st[:, j, :])
                ins.then_inc(ln_mean[n], 1)

            def apply(n, src, dst, b, done):
                dve.wait_ge(ln_rstd[n], b + 1)
                for j in range(CHUNKS):
                    ins = V.tensor_scalar(dst[:, j, :], src[:, j, :], ln_mv[n][:, j, 0:1], ln_rs[n][:, j:j + 1],
                                          ALU.subtract, ALU.mult)
                ins.then_inc(done, 1)

            def absmax(f, t, k):
                dve.wait_ge(y_ready, 3 * f + t + 1)
                V.tensor_reduce(ymax[:, bass.ds(3 * f + t, 1)], halves(k, P), AX.XY, ALU.max,
                                apply_absolute_value=True).then_inc(ymax_done, 1)

            def step(m, r, s1_=True, s2_=True, s3=True, ffn=True):
                i = 2 * m + r
                a, f = i - 1, i - 2
                one, other = one_other(r)
                if s2_:
                    for q, (k, j0, n) in enumerate(((other, 0, CH_A), (2, CH_A, CHUNKS - CH_A))):
                        dve.wait_ge(e_ready, 2 * a + q + 1)
                        V.scalar_tensor_tensor(fkv[:, j0:j0 + n, :], ekv[:, j0:j0 + n, :], 1.0,
                                               chunks(k, n, 256, 2 * C), ALU.min, ALU.max).then_inc(f_ready, 1)
                if s3 and ffn:
                    dve.wait_ge(hi_ready, f + 1)
                    V.tensor_tensor(big[0:C, f, 1, :].rearrange("p (j t) -> p j t", t=TOK),
                                    flat(0)[0:C, 0:CHUNKS * P].rearrange("p (j t) -> p j t", t=P)[:, :, 0:TOK],
                                    big[0:C, f, 0, :].rearrange("p (j t) -> p j t", t=TOK),
                                    ALU.subtract).then_inc(lo_ready, 1)
                if s1_:
                    wv = w0[:, bass.ds(i * CHUNKS, CHUNKS)].rearrange("p (n a) -> p n a", a=1).to_broadcast(
                        [TOK, CHUNKS, C])
                    with dve.If(mixed):
                        dve.wait_ge(d_ready, i + 1)
                        V.tensor_tensor(tmp[:, :, :], chunks(2, CHUNKS, P, C), wv, ALU.mult).then_inc(tmp_ready, 1)
                        dve.wait_ge(yx_ready, i + 1)
                        dve.wait_ge(tmp_ready, i + 1)
                        V.tensor_tensor(t1[r][:, :, :], tmp[:, :, :], chunks(other, CHUNKS, P, C),
                                        ALU.add).then_inc(t1_ready, 1)
                    with dve.Else():
                        dve.wait_ge(yx_ready, i + 1)
                        V.tensor_copy(t1[r][:, :, :], chunks(other, CHUNKS, P, C)).then_inc(t1_ready, 1)
                    dve.wait_ge(t1_ready, i + 1)
                    stats(0, t1[r], i, 1 if isinstance(i, int) and i == 0 else 2 * i, one if s2_ else None)
                if s2_ and not s1_:
                    mask_a(i, one)
                if s3 and ffn:
                    absmax(f, 0, 0)
                    absmax(f, 1, 2)
                    absmax(f, 2, other)
                if s2_:
                    dve.wait_ge(ao_ready, i)
                    V.tensor_tensor(t2[:, :, :], t1[1 - r][:, :, :], chunks(one, CHUNKS, P, C),
                                    ALU.add).then_inc(t2_ready, 1)
                if s1_:
                    apply(0, t1[r], xh1, i, xh1_ready)
                if s2_ and not (isinstance(i, int) and i - 1 >= QIMAGES):
                    dve.wait_ge(t2_ready, i)
                    stats(1, t2, a, 2 * i + 1)

            for i in range(FIRST):
                step(i // 2, i % 2, s2_=i >= 1, s3=i >= 2)
            with dve.Fori(FIRST // 2, LAST // 2) as m:
                for r in range(2):
                    step(m, r)
            step(LAST // 2, 0, s1_=False, ffn=False)

            dve.wait_ge(ymax_done, 3 * QIMAGES)
            V.tensor_reduce(gmax1[:, :], ymax[:, :].rearrange("p (g n) -> p g n", g=QGROUPS), AX.X,
                            ALU.max).then_inc(gmax_ready, 1)
            dve.wait_ge(gmaxT, 1)
            link(V.tensor_reduce(gcol[:, :], S[0][0:QGROUPS, 0, 0:P], AX.X, ALU.max))
            V.tensor_scalar(gdiag[:, :], ident[0:QGROUPS, 0:QGROUPS], gcol[:, 0:1], None, ALU.mult).then_inc(gdiag_ready, 1)
            dve.wait_ge(gbc, 1)
            link(V.tensor_scalar(s1e[:, :], S[0][:, 1, 0:QGROUPS], Q_EPS, 1.0 / QMAX, ALU.add, ALU.mult))
            V.reciprocal(s1[:, :], s1e[:, :]).then_inc(s1_ready, 1)

            def split(m, r):
                b = 2 * m + r
                for t in range(TILES):
                    if t < 2:
                        dve.wait_ge(ahi_ready, 2 * b + t + 1)
                    else:
                        dve.wait_ge(gelu_ready, 3 * b + 3)
                        V.tensor_scalar(h_hi[r][:, t, :], gel[:, t, :], Q_CLIP, None, ALU.min).then_inc(hhi_ready, 1)
                        dve.wait_ge(hhi_ready, b + 1)
                    if t == 0:
                        wait_count(dve, y2_ready, b - 1)
                    V.scalar_tensor_tensor(h_lo[r][:, t, :], gel[:, t, :], Q_CLIP, h_hi[r][:, t, :],
                                           ALU.min, ALU.subtract).then_inc(hlo_ready, 1)

            def y2_absmax(b):
                dve.wait_ge(y2_evac, b + 1)
                V.tensor_reduce(y2max[:, bass.ds(b, 1)], y2_all[:, b, :], AX.X, ALU.max,
                                apply_absolute_value=True).then_inc(y2max_done, 1)

            def group_scale(g):
                dve.wait_ge(y2max_done, (g + 1) * QB)
                V.tensor_reduce(gmax2[:, :], y2max[:, bass.ds(g * QB, QB)], AX.X, ALU.max).then_inc(g2_ready, 1)
                dve.wait_ge(g2T, g + 1)
                V.tensor_reduce(g2one[:, :], S[3][0:1, 0, 400:400 + C], AX.X, ALU.max).then_inc(g2one_ready, 1)
                dve.wait_ge(g2bc, g + 1)
                V.tensor_scalar(s2e[:, :], S[3][0:C, 1, 400:401], Q_EPS, 1.0 / QMAX, ALU.add, ALU.mult).then_inc(s2e_ready, 1)
                dve.wait_ge(s2e_ready, g + 1)
                V.reciprocal(s2[:, bass.ds(g, 1)], s2e[:, :]).then_inc(s2_ready, 1)

            def clipped(g, m, r):
                b = 2 * m + r
                dve.wait_ge(s2_ready, g + 1)
                wait_count(dve, o_ready, b - 1)
                V.tensor_scalar(qv[r][:, :], y2_all[:, b, :], s2[:, bass.ds(g, 1)], Q_CLIP,
                                ALU.mult, ALU.min).then_inc(qv_ready, 1)
                dve.wait_ge(qv_ready, b + 1)
                V.tensor_scalar(qv[r][:, :], qv[r][:, :], -Q_CLIP, None, ALU.max).then_inc(qc_ready, 1)

            def ffn_pair(m, g=None, scale=False, first=False):
                for r in range(2):
                    split(m, r)
                    if not (first and r == 0):
                        y2_absmax(2 * m + r - 1)
                    if scale and r == 0:
                        group_scale(g - 1)
                    if g is not None:
                        clipped(g - 1, m - QB // 2, r)

            ffn_pair(0, first=True)
            with dve.Fori(1, QB // 2) as q:
                ffn_pair(q)
            ffn_pair(QB // 2, g=1, scale=True)
            with dve.Fori(1, QB // 2) as q:
                ffn_pair(QB // 2 + q, g=1)
            with dve.Fori(2, QGROUPS) as g:
                ffn_pair(g * (QB // 2), g=g, scale=True)
                with dve.Fori(1, QB // 2) as q:
                    ffn_pair(g * (QB // 2) + q, g=g)
            y2_absmax(QIMAGES - 1)
            group_scale(QGROUPS - 1)
            for q in range(QB // 2):
                for r in range(2):
                    clipped(QGROUPS - 1, (QGROUPS - 1) * (QB // 2) + q, r)


_INS = ['x', 'L0_conv_gate_w', 'L0_conv_gate_b', 'L0_conv_w1', 'L0_conv_b1', 'L0_conv_w2', 'L0_conv_b2',
        'L1_attn_qkv_w', 'L1_attn_qkv_b', 'L1_attn_proj_w', 'L1_attn_proj_b', 'L1_attn_lambda_k1',
        'L1_attn_lambda_v1', 'L1_attn_lambda_k2', 'L1_attn_lambda_v2', 'L1_ffn_W1', 'L1_ffn_b1',
        'L1_ffn_W2', 'L1_ffn_b2']


def kernel(**inputs):
    import concourse.bacc as _bacc
    from concourse.bass_utils import run_bass_kernel_spmd as _run

    nc = _bacc.Bacc("TRN2", target_bir_lowering=False, num_devices=1)
    arrays, args = {}, []
    for name in _INS:
        a = np.ascontiguousarray(inputs[name])
        arrays[f"in_{name}"] = a
        args.append(nc.dram_tensor(f"in_{name}", a.shape, mybir.dt.from_np(a.dtype), kind="ExternalInput").ap())
    k = shape_constants()
    arrays["shape_consts"] = k
    args.append(nc.dram_tensor("shape_consts", k.shape, F32, kind="ExternalInput").ap())
    args.append(nc.dram_tensor("out", (BATCH, C, 28, 28), F32, kind="ExternalOutput").ap())
    build(nc, *args)
    r = _run(nc, [arrays], core_ids=[0])
    return r.results[0]["out"]
```

```python
from contextlib import ExitStack

import numpy as np

import concourse.bass as bass
from concourse import mybir

ALU = mybir.AluOpType
ACT = mybir.ActivationFunctionType
AX = mybir.AxisListType
F32 = mybir.dt.float32
F16 = mybir.dt.float16
BF16 = mybir.dt.bfloat16
I32 = mybir.dt.int32


P = 128
BATCH, C, HW = 32, 96, 784
HALF = HW // 2
TOK = 112
CHUNKS = HW // TOK
CH_A = 4
E = 4
HID = E * C
TILES = HID // P
HEADS, HD = 12, 8
GN_GROUPS = 32
GN_C = C // GN_GROUPS
SLAB = 8
SLABS = BATCH // SLAB
QGROUPS = 5
QB = BATCH // QGROUPS
QIMAGES = QGROUPS * QB
W1_GS = HID // QGROUPS
W2_GS = C // QGROUPS
QMAX = 128.0
Q_EPS = 1e-5
Q_CLIP = float(np.float32(QMAX - Q_EPS))
GN_EPS = 1e-5
LN_EPS = 1e-5
LAMBDA_INIT = 0.8 - 0.6 * float(np.exp(-0.3))
SIGMA = 0.5
F32_EXPONENT = 0x7F800000
W1_TINY = 1e-30
PARTS = 3
B_ROWS = PARTS * E

K_ID, K_GAUSS, K_HEAD, K_GROUP, K_EXPERT, K_PART, K_PART96, K_LAST, K_END = np.cumsum(
    [0, P, C, C, C, (TILES + 1) * E, PARTS, PARTS, C + 1]).tolist()


def shape_constants():
    k = np.zeros((P, K_END), np.float32)
    k[:, K_ID:K_ID + P] = np.eye(P)
    row = np.arange(C)
    same_head = row[:, None] // HD == row[None, :] // HD
    dist = (row[:, None] % HD - row[None, :] % HD).astype(np.float32)
    k[:C, K_GAUSS:K_GAUSS + C] = np.exp(-dist ** 2 / (2.0 * SIGMA ** 2)) * same_head
    k[:C, K_HEAD:K_HEAD + C] = same_head
    k[:C, K_GROUP:K_GROUP + C] = (row[:, None] // GN_C == row[None, :] // GN_C) / np.float32(GN_C)
    for t in range(TILES):
        for e in range(E):
            k[:, K_EXPERT + t * E + e] = (np.arange(P) + t * P) // C == e
    for n in range(PARTS):
        for e in range(E):
            k[n * E + e, K_EXPERT + TILES * E + e] = 1.0
            k[n * E + e, K_PART + n] = 1.0
        k[C + n, K_PART96 + n] = 1.0
    k[0, K_LAST + C] = 1.0
    return k


def wait_count(eng, sem, count):
    if isinstance(count, int) and count <= 0:
        return
    eng.wait_ge(sem, count)


def wait_apart(eng, sem, count, passed):
    eng.wait_ge(sem, count)
    eng.sem_inc(passed, 1)


def build(nc, x, gate_w, gate_b, w1, b1, w2, b2, qkv_w, qkv_b, proj_w, proj_b,
          lk1, lv1, lk2, lv2, W1, fb1, W2, fb2, consts, out):
    with ExitStack() as ctx:
        def sb(name, shape, dt=F32):
            return ctx.enter_context(nc.sbuf_tensor(name, shape, dt))

        def sem(name):
            return ctx.enter_context(nc.semaphore(name))

        ctx.enter_context(nc.allow_non_contiguous_dma(reason="small parameter columns"))
        ctx.enter_context(nc.allow_low_precision(reason="float32 carried as exact parts"))

        S = [ctx.enter_context(nc.psum_tensor(f"slot{k}", [P, 2, 512], F32)) for k in range(4)]

        def one_other(r):
            return (1, 3) if r == 0 else (3, 1)

        def halves(k, rows):
            return S[k][0:rows, :, 0:HALF]

        def flat(k):
            return S[k][:, :, :].rearrange("p a b -> p (a b)")

        def chunks(k, n, width, used):
            return flat(k)[0:TOK, 0:n * width].rearrange("p (j c) -> p j c", c=width)[:, :, 0:used]

        con = sb("con", [P, K_END])
        ident = con[:, K_ID:K_ID + P]
        w1_raw = sb("w1_raw", [P, TILES, C])
        w2_raw = sb("w2_raw", [C, E, C])
        w1_max = sb("w1_max", [P, TILES])
        w1_unit = sb("w1_unit", [P, TILES])
        w1_inv = sb("w1_inv", [P, TILES])
        w1_hi = sb("w1_hi", [C, HID], F16)
        w1_lo = sb("w1_lo", [C, HID], F16)
        b1c = sb("b1c", [P, TILES])
        w2T = sb("w2T", [P, TILES, C])
        w2s = sb("w2s", [P, 2, TILES, C])
        b2r = sb("b2r", [B_ROWS, C])
        b2_parts = sb("b2_parts", [B_ROWS, C], BF16)
        bias2_parts = sb("bias2_parts", [B_ROWS, 2, C], BF16)
        differ = sb("differ", [1, 1], mybir.dt.int32)
        ones_b = sb("ones_b", [P, TOK], BF16)
        ones_f = sb("ones_f", [P, P])
        gw = sb("gw", [C, E])
        gb = sb("gb", [TOK, E])
        qkvw = sb("qkvw", [C + 1, 3 * C])
        wqT = sb("wqT", [C, C + 1])
        projw = sb("projw", [C, C])
        projb = sb("projb", [C, C])
        lam = sb("lam", [C, 4])
        lam_e = sb("lam_e", [C, 4])
        gauss = sb("gauss", [C, C])
        W1_raw = sb("W1_raw", [P, TILES, C])
        W1f = sb("W1f", [C, HID])
        W1b = sb("W1b", [C + PARTS, HID], BF16)
        fb1r = sb("fb1r", [C + PARTS, HID])
        W2_raw = sb("W2_raw", [C, HID])
        W2f = sb("W2f", [P, TILES, C])
        W2b = sb("W2b", [P, TILES, C], BF16)
        W2last = sb("W2last", [P, C])
        fb2c = sb("fb2c", [C, 1])
        wsum = sb("wsum", [P, 2, QGROUPS])
        wmean = sb("wmean", [P, 2, QGROUPS])
        part_a = sb("part_a", [P, HID])
        part_b = sb("part_b", [P, HID])
        part_h = sb("part_h", [P, HID], BF16)
        minus_one = sb("minus_one", [TOK, 1])
        gelu_warm = sb("gelu_warm", [TOK, 1])
        ln_eps = sb("ln_eps", [TOK, CHUNKS])
        pow_half = sb("pow_half", [P, 2 * SLAB])

        big = sb("big", [C + PARTS, BATCH, 2, HW], F16)
        x_all = big[0:C, :, :, :].rearrange("p b s n -> p (b s n)").bitcast(F32).rearrange(
            "p (b n) -> p b n", n=HW)
        y2_all = x_all
        stage = sb("stage", [P, SLAB * HW])
        gn_scale = sb("gn_scale", [C, BATCH])
        gn_shift = sb("gn_shift", [C, BATCH])
        w0 = sb("w0", [TOK, BATCH * CHUNKS])
        ymax = sb("ymax", [P, QIMAGES * TILES])
        y2max = sb("y2max", [C, QIMAGES])

        xn_slab = stage[0:C, :].rearrange("p (j n) -> p j n", n=HW)
        gn_st = sb("gn_st", [C, SLAB, 2, 6])
        gn_mv = sb("gn_mv", [C, SLAB, 2])
        gn_avg = sb("gn_avg", [C, SLAB, 2])
        gn_dev = sb("gn_dev", [C, SLAB])
        gn_dev2 = sb("gn_dev2", [C, SLAB])
        gn_var = sb("gn_var", [C, SLAB])
        NS = SLAB * CHUNKS
        top = sb("top", [TOK, 4, NS])
        present_s = sb("present_s", [TOK, SLABS, 2, E])
        present = sb("present", [TOK, 2, E])
        flags = sb("flags", [P, 2, E])
        flag_tmp = sb("flag_tmp", [P, TILES + 1, E])
        row_flag = sb("row_flag", [P, 2, TILES + 1])
        differ_f = sb("differ_f", [1, 1])
        prefer = sb("prefer", [TOK, E])

        hT = sb("hT", [P, TILES, HW])
        xs = [sb(f"xs{r}", [C, HW]) for r in range(2)]
        xn = [sb(f"xn{r}", [C, HW]) for r in range(2)]
        xn_hi = [sb(f"xn_hi{r}", [C, HW], F16) for r in range(2)]
        xn_lo = [sb(f"xn_lo{r}", [C, HW], F16) for r in range(2)]
        tmp = stage[0:TOK, 4 * CHUNKS * C:5 * CHUNKS * C].rearrange("p (j c) -> p j c", c=C)
        t1 = [sb(f"t1_{r}", [TOK, CHUNKS, C]) for r in range(2)]
        t2 = sb("t2", [TOK, CHUNKS, C])
        ln_st = sb("ln_st", [TOK, CHUNKS, 6])
        ln_mv = [sb(f"ln_mv{n}", [TOK, CHUNKS, 2]) for n in range(2)]
        ln_ve = [sb(f"ln_ve{n}", [TOK, CHUNKS]) for n in range(2)]
        ln_rs = [sb(f"ln_rs{n}", [TOK, CHUNKS]) for n in range(2)]
        xh1 = sb("xh1", [TOK, CHUNKS, C])
        xh2 = sb("xh2", [TOK, CHUNKS, C])
        xh1T = sb("xh1T", [C + 1, HW])
        ekv = stage[0:TOK, 0:CHUNKS * 2 * C].rearrange("p (j c) -> p j c", c=2 * C)
        fkv = stage[0:TOK, CHUNKS * 2 * C:2 * CHUNKS * 2 * C].rearrange("p (j c) -> p j c", c=2 * C)
        logits, gate, first = (
            t2[:, :, :].rearrange("p j c -> p (j c)")[:, n * NS * E:(n + 1) * NS * E].rearrange(
                "p (n e) -> p n e", e=E) for n in range(3))
        second, work = (
            xh2[:, :, :].rearrange("p j c -> p (j c)")[:, n * NS * E:(n + 1) * NS * E].rearrange(
                "p (n e) -> p n e", e=E) for n in range(2))
        Am = sb("Am", [C, C])
        St = sb("St", [C, C + 1])
        R = sb("R", [C + 1, C])
        t2T = [sb(f"t2T{r}", [C, HW]) for r in range(2)]

        gel = hT

        stage16 = stage[:, :].bitcast(F16)
        SPLIT = TILES - 1
        part = SPLIT * HW
        per_r = 2 * part + 2 * HW
        h_hi, h_lo = ([stage16[:, r * per_r + n * part:r * per_r + (n + 1) * part].rearrange(
            "p (t n) -> p t n", t=SPLIT) for r in range(2)] for n in range(2))
        h_last = [stage16[:, r * per_r + 2 * part:(r + 1) * per_r].bitcast(F32) for r in range(2)]
        t2_tail = y2_all
        tc_buf = xs
        qv = xn
        gmax1 = sb("gmax1", [P, QGROUPS])
        gcol = sb("gcol", [QGROUPS, 1])
        gdiag = sb("gdiag", [QGROUPS, QGROUPS])
        s1 = sb("s1", [P, QGROUPS])
        s1e = sb("s1e", [P, QGROUPS])
        gmax2 = sb("gmax2", [C, 1])
        g2one = sb("g2one", [1, 1])
        s2e = sb("s2e", [C, 1])
        s2 = sb("s2", [C, QGROUPS])

        act_passed = sem("act_passed")
        dve_passed = sem("dve_passed")
        params_loaded = sem("params_loaded")
        gate_params = sem("gate_params")
        x_loaded = [sem(f"x_loaded{r}") for r in range(2)]
        ones_ready = sem("ones_ready")
        bigones_ready = sem("bigones_ready")
        setup_T = sem("setup_T")
        setup_dve = sem("setup_dve")
        top_step = sem("top_step")
        fold_in = sem("fold_in")
        wsum_ready = sem("wsum_ready")
        lam_prod = sem("lam_prod")
        lam_sum = sem("lam_sum")
        lam_exp = sem("lam_exp")
        wmean_sum = sem("wmean_sum")
        gn_stats = sem("gn_stats")
        gn_mv_ready = sem("gn_mv_ready")
        gn_group = sem("gn_group")
        gn_avg_ready = sem("gn_avg_ready")
        gn_dev_ready = sem("gn_dev_ready")
        gn_dev2_ready = sem("gn_dev2_ready")
        gn_between = sem("gn_between")
        gn_var_ready = sem("gn_var_ready")
        gn_rstd = sem("gn_rstd")
        gn_coef = sem("gn_coef")
        xn_slab_ready = sem("xn_slab_ready")
        gates_done = sem("gates_done")
        logits_ready = sem("logits_ready")
        gate_exp_in = sem("gate_exp_in")
        gate_exp = sem("gate_exp")
        top_exp = sem("top_exp")
        present_ready = sem("present_ready")
        counts_ready = sem("counts_ready")
        conv_ready = sem("conv_ready")

        xs_loaded = [sem(f"xs_loaded{r}") for r in range(2)]
        xn_ready = sem("xn_ready")
        xn_hi_ready = sem("xn_hi_ready")
        xn_lo_ready = sem("xn_lo_ready")
        w1_scaled = sem("w1_scaled")
        z_ready = sem("z_ready")
        h_ready = sem("h_ready")
        yx_part = sem("yx_part")
        yx_ready = sem("yx_ready")
        t1_part = sem("t1_part")
        tmp_ready = sem("tmp_ready")
        t1_ready = sem("t1_ready")
        ln_stats = sem("ln_stats")
        ln_mean = [sem("ln1_mean"), sem("ln2_mean")]
        ln_var = [sem("ln1_var"), sem("ln2_var")]
        ln_rstd = [sem("ln1_rstd"), sem("ln2_rstd")]
        xh1_ready = sem("xh1_ready")
        xh2_ready = sem("xh2_ready")
        x1T_ready = sem("x1T_ready")
        xh1T_ready = sem("xh1T_ready")
        kv_ready = sem("kv_ready")
        e_ready = sem("e_ready")
        f_ready = sem("f_ready")
        a_ready = sem("a_ready")
        am_ready = sem("am_ready")
        stp_ready = sem("stp_ready")
        st_ready = sem("st_ready")
        rp_ready = sem("rp_ready")
        r_ready = sem("r_ready")
        d_ready = sem("d_ready")
        ao_ready = sem("ao_ready")
        t2_ready = sem("t2_ready")
        t2p_ready = sem("t2p_ready")
        t2T_evac = sem("t2T_evac")
        t2T_stored = [sem(f"t2T_stored{r}") for r in range(2)]
        x2p_ready = sem("x2p_ready")
        hi_ready = sem("hi_ready")
        lo_ready = sem("lo_ready")
        y_ready = sem("y_ready")
        ymax_done = sem("ymax_done")

        gmax_ready = sem("gmax_ready")
        gmaxT = sem("gmaxT")
        gdiag_ready = sem("gdiag_ready")
        gbc = sem("gbc")
        s1_ready = sem("s1_ready")
        y1_ready = sem("y1_ready")
        gelu_ready = sem("gelu_ready")
        parts_ready = sem("parts_ready")
        y2_ready = sem("y2_ready")
        y2_evac = sem("y2_evac")
        y2max_done = sem("y2max_done")
        g2_ready = sem("g2_ready")
        g2T = sem("g2T")
        g2one_ready = sem("g2one_ready")
        g2bc = sem("g2bc")
        s2e_ready = sem("s2e_ready")
        s2_ready = sem("s2_ready")
        tc_loaded = [sem(f"tc_loaded{r}") for r in range(2)]
        qv_ready = sem("qv_ready")
        qc_ready = sem("qc_ready")
        hi_parts = sem("hi_parts")
        o_ready = sem("o_ready")
        tail_loaded = sem("tail_loaded")
        tail_clip = sem("tail_clip")
        tail_ready = sem("tail_ready")
        tail_stored = [sem(f"tail_stored{r}") for r in range(2)]
        o_stored = [sem(f"o_stored{r}") for r in range(2)]

        block = ctx.enter_context(nc.Block())

        x_bcn = x.rearrange("b c h w -> b c (h w)")
        out_bcn = out.rearrange("b c h w -> b c (h w)")

        FIRST, LAST = 4, BATCH
        N_PARAMS = 19
        CONSTS_SET = (ones_ready, 11)

        @block.sync
        def _(sp):
            for r in range(2):
                sp.dma_start(x_all[:, 4 * r:4 * r + 4, :],
                             x_bcn[4 * r:4 * r + 4].rearrange("b c n -> c b n")).then_inc(x_loaded[r], 16)
            with sp.Fori(1, SLABS) as s:
                for r in range(2):
                    sp.wait_ge(x_loaded[r], 16 * s)
                    b0 = s * SLAB + 4 * r
                    sp.dma_start(x_all[:, bass.ds(b0, 4), :],
                                 x_bcn[bass.ds(b0, 4)].rearrange("b c n -> c b n")).then_inc(x_loaded[r], 16)
            for r in range(2):
                sp.dma_start(xs[r][:, :], x_bcn[r]).then_inc(xs_loaded[r], 16)

            def step(m, r, load=True):
                i = 2 * m + r
                if load:
                    wait_count(sp, yx_ready, i + 1)
                    sp.dma_start(xs[r][:, :], x_bcn[i + 2]).then_inc(xs_loaded[r], 16)
                if not isinstance(i, int) or i >= 2:
                    sp.wait_ge(t2T_evac, i - 1)
                    sp.dma_start(out_bcn[i - 2], t2T[r][:, :]).then_inc(t2T_stored[r], 16)

            for m in range(FIRST // 2):
                for r in range(2):
                    step(m, r)
            with sp.Fori(FIRST // 2, LAST // 2 - 1) as m:
                for r in range(2):
                    step(m, r)
            for m in (LAST // 2 - 1, LAST // 2):
                for r in range(2):
                    step(m, r, load=False)
            for r in range(2):
                sp.wait_ge(t2T_stored[r], 16 * (BATCH // 2))

            def load_c(b, m, r):
                wait_count(sp, o_stored[r], 16 * m)
                sp.dma_start(tc_buf[r][:, :], out_bcn[b]).then_inc(tc_loaded[r], 16)

            def store_c(b, m, r):
                sp.wait_ge(o_ready, b + 1)
                sp.dma_start(out_bcn[b], tc_buf[r][:, :]).then_inc(o_stored[r], 16)

            for r in range(2):
                sp.dma_start(tc_buf[r][:, :], out_bcn[r]).then_inc(tc_loaded[r], 16)
            FINISHED = (QIMAGES - QB) // 2

            def pair_c(m):
                for r in range(2):
                    store_c(2 * m + r, m, r)
                for r in range(2):
                    load_c(2 * m + 2 + r, m + 1, r)

            with sp.Fori(0, QB // 2) as m:
                pair_c(m)
            sp.wait_ge(qv_ready, QB)
            sp.dma_start(t2_tail[:, 0:QB, :],
                         out_bcn[QIMAGES - QB:QIMAGES].rearrange("b c n -> c b n")).then_inc(tail_loaded, 16)
            with sp.Fori(QB // 2, FINISHED - 1) as m:
                pair_c(m)
            for r in range(2):
                store_c(2 * (FINISHED - 1) + r, FINISHED - 1, r)
            for j in range(QB):
                sp.wait_ge(tail_ready, j + 1)
                sp.dma_start(out_bcn[QIMAGES - QB + j], t2_tail[:, j, :]).then_inc(tail_stored[j % 2], 16)
            for r in range(2):
                sp.wait_ge(tail_stored[r], 16 * (QB // 2))
                sp.wait_ge(o_stored[r], 16 * FINISHED)

        @block.gpsimd
        def _(pool):
            nc.gpsimd.memset(ones_b[:, :], 1.0).then_inc(ones_ready, 1)
            nc.gpsimd.memset(ones_f[:, :], 1.0).then_inc(ones_ready, 1)
            nc.gpsimd.memset(minus_one[:, :], -1.0).then_inc(ones_ready, 1)
            nc.gpsimd.memset(ln_eps[:, :], LN_EPS).then_inc(ones_ready, 1)
            nc.gpsimd.memset(pow_half[:, :], -0.5).then_inc(ones_ready, 1)
            nc.gpsimd.memset(projb[:, :], 0.0).then_inc(ones_ready, 1)
            for e in range(E):
                nc.gpsimd.memset(prefer[:, e:e + 1], float(E - e)).then_inc(ones_ready, 1)
            pool.wait_ge(ones_ready, CONSTS_SET[1] - 1)
            nc.gpsimd.memset(xh1T[C:C + 1, :], 1.0).then_inc(ones_ready, 1)
            pool.wait_ge(*CONSTS_SET)
            def gn_power(u, b0, j0, n):
                pool.wait_ge(gn_var_ready, u + 1)
                nc.gpsimd.tensor_tensor(gn_scale[:, bass.ds(b0, n)], gn_var[:, j0:j0 + n],
                                        pow_half[0:C, 0:n], ALU.pow).then_inc(gn_rstd, 1)

            for h in range(2):
                gn_power(h, 4 * h, 4 * h, 4)
            with pool.Fori(1, SLABS) as s:
                gn_power(s + 1, s * SLAB, 0, SLAB)
            pool.wait_ge(gn_rstd, SLABS + 1)
            nc.gpsimd.memset(big[C:C + PARTS, 0:QIMAGES, 0, :], 1.0).then_inc(bigones_ready, 1)

            def rstd(n, b):
                pool.wait_ge(ln_mean[n], b + 1)
                nc.gpsimd.tensor_tensor(ln_ve[n][:, :], ln_mv[n][:, :, 1], ln_eps[:, :],
                                        ALU.add).then_inc(ln_var[n], 1)
                pool.wait_ge(ln_var[n], b + 1)
                nc.gpsimd.tensor_tensor(ln_rs[n][:, :], ln_ve[n][:, :], pow_half[0:TOK, 0:CHUNKS],
                                        ALU.pow).then_inc(ln_rstd[n], 1)

            def xn_rest(r, i):
                pool.wait_ge(xn_hi_ready, i + 1)
                nc.gpsimd.tensor_tensor(xn_lo[r][:, :], xn[r][:, :], xn_hi[r][:, :],
                                        ALU.subtract).then_inc(xn_lo_ready, 1)

            def step(m, r, next_=True):
                i = 2 * m + r
                if next_:
                    xn_rest(1 - r, i + 1)
                rstd(0, i)
                if not isinstance(i, int) or 0 < i <= QIMAGES:
                    rstd(1, i - 1)

            xn_rest(0, 0)
            step(0, 0)
            step(0, 1)
            with pool.Fori(1, LAST // 2 - 1) as m:
                for r in range(2):
                    step(m, r)
            step(LAST // 2 - 1, 0)
            step(LAST // 2 - 1, 1, next_=False)

            def finish(m, r):
                pool.wait_ge(tc_loaded[r], 16 * (m + 1))
                pool.wait_ge(qc_ready, 2 * m + r + 1)
                nc.gpsimd.tensor_tensor(tc_buf[r][:, :], tc_buf[r][:, :], qv[r][:, :], ALU.add).then_inc(o_ready, 1)

            with pool.Fori(0, (QIMAGES - QB) // 2) as m:
                for r in range(2):
                    finish(m, r)

        @block.scalar
        def _(act):
            def load(dst, src):
                act.dma_start(dst, src).then_inc(params_loaded, 16)

            act.dma_start(con[:, :], consts).then_inc(gate_params, 16)
            act.dma_start(gw[:, :], gate_w).then_inc(gate_params, 16)
            load(w1_raw[:, :, :], w1.rearrange("e d c -> (e d) c").rearrange("(t p) c -> p t c", p=P))
            load(w2_raw[:, :, :], w2.rearrange("e o d -> o e d"))
            load(b1c[:, :], b1.rearrange("e d -> (e d)").rearrange("(t p) -> p t", p=P))
            for n in range(PARTS):
                load(b2r[n * E:(n + 1) * E, :], b2)
            load(gb[:, :], gate_b.rearrange("(a e) -> a e", a=1).to_broadcast([TOK, E]))
            load(qkvw[0:C, :], qkv_w)
            load(qkvw[C:C + 1, :], qkv_b.rearrange("(a n) -> a n", a=1))
            load(projw[:, :], proj_w)
            for n, l in enumerate((lk1, lv1, lk2, lv2)):
                load(lam[:, n:n + 1], l.rearrange("h (d a) -> (h d) a", a=1))
            load(W1_raw[:, :, :], W1.rearrange("(t p) c -> p t c", p=P))
            load(fb1r[C:C + PARTS, :], fb1.rearrange("(a n) -> a n", a=1).to_broadcast([PARTS, HID]))
            load(W2_raw[:, :], W2)
            load(fb2c[:, :], fb2.rearrange("(c a) -> c a", a=1))
            act.wait_ge(*CONSTS_SET)
            load(projb[0:1, :], proj_b.rearrange("(a n) -> a n", a=1))

            def norm_half(s, h):
                u = 2 * s + h
                if isinstance(s, int):
                    act.wait_ge(gn_coef, h + 1)
                elif h == 0:
                    wait_apart(act, gn_coef, s + 2, act_passed)
                wait_count(act, gates_done, u - 1)
                if not isinstance(u, int):
                    act.sem_inc(act_passed, 1)
                for j in range(4 * h, 4 * h + 4):
                    b = s * SLAB + j
                    ins = nc.scalar.activation(xn_slab[:, j, :], x_all[:, b, :], ACT.Identity,
                                               scale=gn_scale[:, bass.ds(b, 1)], bias=gn_shift[:, bass.ds(b, 1)])
                ins.then_inc(xn_slab_ready, 1)

            def logits_out(s, h):
                wait_apart(act, gates_done, 2 * s + h + 1, act_passed)
                nc.scalar.copy(logits[:, h * NH:(h + 1) * NH, :],
                               S[1][0:TOK, h, 0:NH * E].rearrange("p (n e) -> p n e", e=E)).then_inc(logits_ready, 1)

            NH = 4 * CHUNKS
            def gate_softmax(s):
                act.wait_ge(gate_exp_in, 2 * s + 1)
                nc.scalar.activation(gate, gate, ACT.Exp).then_inc(gate_exp, 1)

            def top_softmax(s):
                act.wait_ge(gate_exp_in, 2 * s + 2)
                nc.scalar.activation(top[:, 2, :], top[:, 2, :], ACT.Exp).then_inc(top_exp, 1)

            norm_half(0, 0)
            norm_half(0, 1)
            logits_out(0, 0)
            act.wait_ge(lam_sum, 1)
            nc.scalar.activation(lam_e[:, 0:2], S[2][0:C, 0, 400:402], ACT.Exp).then_inc(lam_exp, 1)
            with act.Fori(1, SLABS) as s:
                norm_half(s, 0)
                logits_out(s - 1, 1)
                norm_half(s, 1)
                gate_softmax(s - 1)
                top_softmax(s - 1)
                logits_out(s, 0)

            def norm_image(m, r, i):
                act.wait_ge(xs_loaded[r], 16 * (m + 1))
                if isinstance(i, int):
                    wait_count(act, z_ready, 3 * (i - 1))
                    wait_count(act, xn_lo_ready, i - 1)
                else:
                    wait_apart(act, z_ready, 3 * (i - 1), act_passed)
                    wait_apart(act, xn_lo_ready, i - 1, act_passed)
                nc.scalar.activation(xn[r][:, :], xs[r][:, :], ACT.Identity, scale=gn_scale[:, bass.ds(i, 1)],
                                     bias=gn_shift[:, bass.ds(i, 1)]).then_inc(xn_ready, 1)
                wait_apart(act, xn_ready, i + 1, act_passed)
                nc.scalar.copy(xn_hi[r][:, :], xn[r][:, :]).then_inc(xn_hi_ready, 1)

            def channels(dst, k):
                return (dst.rearrange("p (j t) -> p j t", t=TOK),
                        flat(k)[0:C, 0:CHUNKS * P].rearrange("p (j t) -> p j t", t=P)[:, :, 0:TOK])

            def step(m, r, experts=True, attend=True, out_=True, ffn=True, next_=True):
                i = 2 * m + r
                one, other = one_other(r)
                def relu(t):
                    act.wait_ge(z_ready, 3 * i + t + 1)
                    nc.scalar.activation(hT[:, t, :].rearrange("p (a n) -> p a n", a=2),
                                         halves((0, one, 2)[t], P),
                                         ACT.Relu, scale=w1_unit[:, t:t + 1],
                                         bias=b1c[:, t:t + 1]).then_inc(h_ready, 1)

                def exp_kv(q, k, j0, n):
                    act.wait_ge(kv_ready, 2 * (i - 1) + q + 1)
                    nc.scalar.activation(ekv[:, j0:j0 + n, :], chunks(k, n, 256, 2 * C), ACT.Exp,
                                         bias=minus_one[:, :]).then_inc(e_ready, 1)

                if experts:
                    relu(0)
                    relu(1)
                    relu(2)
                if attend:
                    act.wait_ge(x1T_ready, i)
                    nc.scalar.copy(*channels(xh1T[0:C, :], 0)).then_inc(xh1T_ready, 1)
                if out_:
                    act.wait_ge(t2p_ready, i - 1)
                    wait_count(act, t2T_stored[r], 16 * (m - 1))
                    nc.scalar.copy(*channels(t2T[r][:, :], one)).then_inc(t2T_evac, 1)
                if attend:
                    exp_kv(0, other, 0, CH_A)
                    exp_kv(1, 0, CH_A, CHUNKS - CH_A)
                if out_ and ffn:
                    wait_apart(act, x2p_ready, i - 1, act_passed)
                    nc.scalar.copy(*channels(big[0:C, i - 2, 0, :], other)).then_inc(hi_ready, 1)
                if experts and next_:
                    norm_image(m + r, 1 - r, i + 1)
                if attend:
                    act.wait_ge(stp_ready, i)
                    nc.scalar.copy(St[:, :], S[one][0:C, 1, 0:C + 1]).then_inc(st_ready, 1)
                    act.wait_ge(rp_ready, i)
                    nc.scalar.copy(R[:, :], S[one][0:C + 1, 0, 0:C]).then_inc(r_ready, 1)

            norm_image(0, 0, 0)
            logits_out(SLABS - 1, 1)
            gate_softmax(SLABS - 1)
            step(0, 0, attend=False, out_=False)
            top_softmax(SLABS - 1)
            for i in range(1, FIRST):
                step(i // 2, i % 2, out_=i >= 2)
            with act.Fori(FIRST // 2, LAST // 2 - 1) as m:
                for r in range(2):
                    step(m, r)
            step(LAST // 2 - 1, 0)
            step(LAST // 2 - 1, 1, next_=False)
            step(LAST // 2, 0, experts=False, ffn=False)


            def gelu_tile(g, b, t):
                wait_count(act, parts_ready, 3 * b + t - 2)
                wait_apart(act, y1_ready, 3 * b + t + 1, act_passed)
                nc.scalar.activation(gel[:, t, :].rearrange("p (a n) -> p a n", a=2), halves(t, P),
                                     ACT.Gelu, scale=s1[:, bass.ds(g, 1)]).then_inc(gelu_ready, 1)

            def gelu_hi(b, t, r):
                wait_apart(act, gelu_ready, 3 * b + t + 1, act_passed)
                if t == 0:
                    wait_count(act, y2_ready, b - 1)
                    if not isinstance(b, int):
                        act.sem_inc(act_passed, 1)
                nc.scalar.copy(h_hi[r][:, t, :], gel[:, t, :]).then_inc(hi_parts, 1)

            def y2_out(b):
                wait_apart(act, y2_ready, b + 1, act_passed)
                nc.scalar.activation(y2_all[:, b, :].rearrange("p (a n) -> p a n", a=2), halves(3, C),
                                     ACT.Identity, bias=fb2c[:, 0:1]).then_inc(y2_evac, 1)

            def ffn(g, m, started=False):
                for r in range(2):
                    b = 2 * m + r
                    if not (started and r == 0):
                        gelu_tile(g, b, 0)
                    gelu_tile(g, b, 1)
                    gelu_hi(b, 0, r)
                    gelu_tile(g, b, 2)
                    gelu_hi(b, 1, r)
                    if not (isinstance(b, int) and b == 0):
                        y2_out(b - 1)

            nc.scalar.activation(gelu_warm[:, :], minus_one[:, :], ACT.Gelu)
            act.wait_ge(s1_ready, 1)
            gelu_tile(0, 0, 0)
            step(LAST // 2, 1, experts=False, attend=False, ffn=False)
            ffn(0, 0, started=True)
            with act.Fori(1, QB // 2) as q:
                ffn(0, q)
            with act.Fori(1, QGROUPS) as g:
                with act.Fori(0, QB // 2) as q:
                    ffn(g, g * (QB // 2) + q)
            y2_out(QIMAGES - 1)

        @block.tensor
        def _(pe):
            mm = nc.tensor.matmul

            def tr(o, i, start=True):
                rows = i.shape[0]
                return mm(o, i, ident[0:rows, 0:rows], start=start, stop=True, is_transpose=True,
                          skip_group_check=True)

            def group_means(u, j0=0, n=SLAB):
                pe.wait_ge(gn_mv_ready, 1 if isinstance(u, int) and u == 0 else 2 * u)
                mm(S[0][0:C, 0, 2 * j0:2 * (j0 + n)], con[0:C, K_GROUP:K_GROUP + C],
                   gn_mv[:, j0:j0 + n, :].rearrange("p j k -> p (j k)"), start=True, stop=True).then_inc(gn_group, 1)

            def group_between(u, j0=0, n=SLAB):
                pe.wait_ge(gn_dev2_ready, u + 1)
                mm(S[0][0:C, 1, j0:j0 + n], con[0:C, K_GROUP:K_GROUP + C], gn_dev2[:, j0:j0 + n],
                   start=True, stop=True).then_inc(gn_between, 1)

            def gate_images(h, images):
                for j in images:
                    for c in range(CHUNKS):
                        n = (j * CHUNKS + c) * E
                        ins = mm(S[1][0:TOK, h, n:n + E], xn_slab[:, 4 * h + j, c * TOK:(c + 1) * TOK], gw[:, :],
                                 start=True, stop=True, skip_group_check=True)
                return ins

            def gate_half(s, h, next_norm=False):
                pe.wait_ge(xn_slab_ready, 2 * s + h + 1)
                wait_count(pe, logits_ready, 2 * s + h - 1)
                if next_norm:
                    group_means(s + 2)
                gate_images(h, range(1))
                if next_norm:
                    group_between(s + 2)
                gate_images(h, range(1, 4)).then_inc(gates_done, 1)

            pe.wait_ge(gate_params, 32)
            pe.wait_ge(*CONSTS_SET)
            for h in range(2):
                group_means(h, 4 * h, 4)
                group_between(h, 4 * h, 4)
            gate_half(0, 0)
            pe.wait_ge(params_loaded, 16 * N_PARAMS)
            pe.wait_ge(w1_scaled, 1)
            for t in range(TILES):
                tr(S[2][0:C, 0, t * P:(t + 1) * P], w1_raw[:, t, :])
            for t in range(TILES):
                tr(S[2][:, 1, t * C:(t + 1) * C],
                   w2_raw[:, :, :].rearrange("p e d -> p (e d)")[:, t * P:(t + 1) * P])
            tr(S[2][0:C, 1, HID:HID + C + 1], qkvw[:, 0:C])
            for t in range(TILES):
                tr(S[3][0:C, 0, t * P:(t + 1) * P], W1_raw[:, t, :])
            for t in range(TILES):
                ins = tr(S[3][:, 1, t * C:(t + 1) * C], W2_raw[:, t * P:(t + 1) * P])
            ins.then_inc(setup_T, 1)
            pe.wait_ge(lam_prod, 1)
            mm(S[2][0:C, 0, 400:402], con[0:C, K_HEAD:K_HEAD + C], lam_e[:, 2:4],
               start=True, stop=True, skip_group_check=True).then_inc(lam_sum, 1)
            gate_half(0, 1, next_norm=True)
            pe.wait_ge(wsum_ready, 1)
            mm(S[3][0:C, 0, 400:400 + QGROUPS], ones_f[0:C, 0:C], wsum[0:C, 0, :], start=True, stop=True,
               skip_group_check=True)
            mm(S[3][:, 1, 400:400 + QGROUPS], ones_f[:, :], wsum[:, 1, :], start=True, stop=True,
               skip_group_check=True).then_inc(wmean_sum, 1)
            with pe.Fori(1, SLABS - 1) as s:
                gate_half(s, 0)
                gate_half(s, 1, next_norm=True)
            gate_half(SLABS - 1, 0)
            gate_half(SLABS - 1, 1)
            pe.wait_ge(logits_ready, 2 * SLABS)

            def hidden(t, k, r):
                rows = slice(t * P, (t + 1) * P)
                for n, (w, x_part) in enumerate(((w1_hi, xn_hi[r]), (w1_hi, xn_lo[r]), (w1_lo, xn_hi[r]))):
                    for h in range(2):
                        ins = mm(S[k][:, h, 0:HALF], w[:, rows], x_part[:, h * HALF:(h + 1) * HALF],
                                 start=n == 0, stop=n == 2, skip_group_check=True)
                ins.then_inc(z_ready, 1)

            def to_channels(k, src, done):
                for j in range(CHUNKS):
                    ins = tr(flat(k)[0:C, j * P:j * P + TOK], src[:, j, :], start=j % CH_A == 0)
                ins.then_inc(done, 1)

            def mix(v, k, r, with_x, j0, n):
                o = chunks(k, CHUNKS, P, C)
                if with_x:
                    for j in range(j0, j0 + n):
                        tr(o[:, j, :], xs[r][:, j * TOK:(j + 1) * TOK], start=j % CH_A == 0)
                mm(o[:, j0:j0 + n, :], ones_b[0:B_ROWS, :],
                   bias2_parts[:, v:v + 1, :].to_broadcast([B_ROWS, n, C]),
                   start=not with_x, stop=False, skip_group_check=True)
                for j in range(j0, j0 + n):
                    for t in range(TILES):
                        ins = mm(o[:, j, :], hT[:, t, j * TOK:(j + 1) * TOK], w2s[:, v, t, :],
                                 start=False, stop=t == TILES - 1, skip_group_check=True)
                return ins

            def ffn_tile(f, t, k):
                w = W1b[:, t * P:(t + 1) * P]
                for h in range(2):
                    mm(S[k][:, h, 0:HALF], w, big[:, f, 0, h * HALF:(h + 1) * HALF],
                       start=True, stop=False, skip_group_check=True)
                for h in range(2):
                    ins = mm(S[k][:, h, 0:HALF], w[0:C, :], big[0:C, f, 1, h * HALF:(h + 1) * HALF],
                             start=False, stop=True, skip_group_check=True)
                return ins

            def presences():
                pe.wait_ge(present_ready, 1)
                pe.wait_ge(fold_in, 1)
                mm(S[3][:, 0, 0:2 * E], ones_f[0:TOK, :], present[:, :, :].rearrange("p k e -> p (k e)"),
                   start=True, stop=True).then_inc(counts_ready, 1)
                pe.wait_ge(conv_ready, 1)
                pe.wait_ge(bigones_ready, 1)
                return pe.value_load(differ[0:1, 0:1], min_val=0, max_val=1)

            def y1_max_row():
                pe.wait_ge(gmax_ready, 1)
                tr(S[2][0:QGROUPS, 0, 0:P], gmax1[:, :]).then_inc(gmaxT, 1)

            def y1_max_spread():
                pe.wait_ge(gdiag_ready, 1)
                mm(S[2][:, 1, 0:QGROUPS], ones_f[0:QGROUPS, :], gdiag[:, :], start=True, stop=True).then_inc(gbc, 1)

            def step(m, r, experts=True, attend=True, out_=True, ffn=True, scales=False):
                nonlocal mixed
                i = 2 * m + r
                one, other = one_other(r)

                def kv(q, k, j0, n):
                    for j in range(n):
                        ins = mm(chunks(k, n, 256, 2 * C)[:, j, :], xh1T[:, (j0 + j) * TOK:(j0 + j + 1) * TOK],
                                 qkvw[:, C:3 * C], start=True, stop=True, skip_group_check=True)
                    ins.then_inc(kv_ready, 1)

                if experts:
                    pe.wait_ge(xn_lo_ready, i + 1)
                    wait_count(pe, t1_ready, i)
                    wait_count(pe, ymax_done, 3 * (i - 3) + 1)
                    hidden(0, 0, r)
                    wait_count(pe, ymax_done, 3 * (i - 3) + 2)
                    hidden(1, one, r)
                    wait_count(pe, ymax_done, 3 * (i - 3) + 3)
                    hidden(2, 2, r)
                    pe.wait_ge(h_ready, 3 * i + 1)
                if attend:
                    pe.wait_ge(xh1_ready, i)
                    if not experts:
                        pe.wait_ge(ymax_done, 3 * QIMAGES)
                    to_channels(0, xh1, x1T_ready)
                if experts:
                    pe.wait_ge(h_ready, 3 * i + 2)
                if out_:
                    pe.wait_ge(t2_ready, i - 1)
                    to_channels(one, t2, t2p_ready)
                if experts:
                    pe.wait_ge(h_ready, 3 * i + 3)
                    if mixed is None:
                        mixed = presences()
                    mix(1, 2, r, True, 0, 2)
                if attend:
                    pe.wait_ge(xh1T_ready, i)
                    wait_count(pe, t2_ready, i - 1)
                    kv(0, other, 0, CH_A)
                if experts:
                    mix(1, 2, r, True, 2, CH_A - 2).then_inc(yx_part, 1)
                if attend:
                    kv(1, 0, CH_A, CHUNKS - CH_A)
                if scales:
                    y1_max_row()
                if experts:
                    mix(1, 2, r, True, CH_A, 1)
                if out_ and ffn:
                    pe.wait_ge(xh2_ready, i - 1)
                    pe.wait_ge(f_ready, 2 * i - 1)
                    to_channels(other, xh2, x2p_ready)
                if experts:
                    mix(1, 2, r, True, CH_A + 1, CHUNKS - CH_A - 1).then_inc(yx_ready, 1)
                    if attend:
                        pe.wait_ge(f_ready, 2 * i)
                    with pe.If(mixed):
                        mix(0, 0, r, False, 0, CH_A)
                        mix(0, 0, r, False, CH_A, CHUNKS - CH_A).then_inc(d_ready, 1)
                        pe.wait_ge(t1_ready, i + 1)
                if attend:
                    pe.wait_ge(f_ready, 2 * i)
                    if out_:
                        pe.wait_ge(t2T_evac, i - 1)
                    for j in range(CHUNKS):
                        ins = mm(S[one][0:C, 0, 0:C], fkv[:, j, 0:C], fkv[:, j, C:2 * C],
                                 start=j == 0, stop=j == CHUNKS - 1)
                    ins.then_inc(a_ready, 1)
                if scales:
                    y1_max_spread()
                if out_ and ffn:
                    pe.wait_ge(hi_ready, i - 1)
                    pe.wait_ge(lo_ready, i - 1)
                    ffn_tile(i - 2, 0, 0).then_inc(y_ready, 1)
                if attend:
                    pe.wait_ge(am_ready, i)
                    mm(S[one][0:C, 1, 0:C + 1], Am[:, :], wqT[:, :], start=True, stop=True).then_inc(stp_ready, 1)
                    mm(S[one][0:C + 1, 0, 0:C], con[0:C, K_LAST:K_LAST + C + 1], projb[:, :],
                       start=True, stop=False)
                if out_ and ffn:
                    pe.wait_ge(t1_ready, i + 1)
                    ffn_tile(i - 2, 1, 2).then_inc(y_ready, 1)
                if scales:
                    pe.wait_ge(s1_ready, 1)
                    ffn_tile(0, 0, 0).then_inc(y1_ready, 1)
                if attend:
                    pe.wait_ge(st_ready, i)
                    mm(S[one][0:C + 1, 0, 0:C], St[:, :], projw[:, :], start=False, stop=True).then_inc(rp_ready, 1)
                if out_ and ffn:
                    ffn_tile(i - 2, 2, other).then_inc(y_ready, 1)
                if attend:
                    pe.wait_ge(r_ready, i)
                    for j in range(CHUNKS):
                        ins = mm(flat(one)[0:TOK, j * P:j * P + C], xh1T[:, j * TOK:(j + 1) * TOK], R[:, :],
                                 start=True, stop=True, skip_group_check=True)
                    ins.then_inc(ao_ready, 1)

            mixed = None
            for i in range(FIRST):
                step(i // 2, i % 2, attend=i >= 1, out_=i >= 2)
            with pe.Fori(FIRST // 2, LAST // 2) as m:
                for r in range(2):
                    step(m, r)
            step(LAST // 2, 0, experts=False, ffn=False, scales=True)
            step(LAST // 2, 1, experts=False, attend=False, ffn=False)

            def ffn_up(b, scale=None, t0=0):
                for t in range(t0, TILES):
                    wait_count(pe, gelu_ready, 3 * b + t - 2)
                    ffn_tile(b, t, t).then_inc(y1_ready, 1)
                    if scale is not None and t == 1:
                        wait_count(pe, y2_evac, b - 1)
                        y2_max_row(scale)
                if scale is not None:
                    y2_max_spread(scale)

            def ffn_down(b, r):
                if isinstance(b, int) and b == 0:
                    pe.wait_ge(t2T_evac, BATCH)
                wait_count(pe, y2_evac, b)
                for t in range(SPLIT):
                    pe.wait_ge(parts_ready, 3 * b + t + 1)
                    for part, src in enumerate((h_hi[r], h_lo[r])):
                        for h in range(2):
                            mm(S[3][0:C, h, 0:HALF], W2b[:, t, :], src[:, t, h * HALF:(h + 1) * HALF],
                               start=t == 0 and part == 0, stop=False, skip_group_check=True)
                pe.wait_ge(parts_ready, 3 * b + TILES)
                for h in range(2):
                    ins = mm(S[3][0:C, h, 0:HALF], W2last[:, :], h_last[r][:, h * HALF:(h + 1) * HALF],
                             start=False, stop=True, skip_group_check=True)
                ins.then_inc(y2_ready, 1)

            def y2_max_row(g):
                pe.wait_ge(g2_ready, g + 1)
                tr(S[3][0:1, 0, 400:400 + C], gmax2[:, :]).then_inc(g2T, 1)

            def y2_max_spread(g):
                pe.wait_ge(g2one_ready, g + 1)
                mm(S[3][0:C, 1, 400:401], ones_f[0:1, 0:C], g2one[:, :], start=True, stop=True,
                   skip_group_check=True).then_inc(g2bc, 1)
                pe.wait_ge(s2e_ready, g + 1)

            def ffn_pair(m, scale=None, last=False):
                for r in range(2):
                    b = 2 * m + r
                    if not (last and r == 1):
                        ffn_up(b + 1, scale if r == 1 else None)
                    ffn_down(b, r)

            ffn_up(0, t0=1)
            ffn_pair(0)
            with pe.Fori(1, QB // 2) as q:
                ffn_pair(q)
            with pe.Fori(1, QGROUPS - 1) as g:
                ffn_pair(g * (QB // 2), scale=g - 1)
                with pe.Fori(1, QB // 2) as q:
                    ffn_pair(g * (QB // 2) + q)
            g = QGROUPS - 1
            ffn_pair(g * (QB // 2), scale=g - 1)
            ffn_pair(g * (QB // 2) + 1)
            ffn_pair(g * (QB // 2) + 2, last=True)
            y2_max_row(g)
            y2_max_spread(g)

        @block.vector
        def _(dve):
            V = nc.vector
            links = [0]

            def link(ins):
                links[0] += 1
                ins.then_inc(setup_dve, 1)
                dve.wait_ge(setup_dve, links[0])

            def gn_half(s, r, before=None):
                dve.wait_ge(x_loaded[r], 16 * (s + 1))
                for j in range(4 * r, 4 * r + 4):
                    if before is not None and j % 4 == 2:
                        gn_shifts(*before)
                    for h in range(2):
                        ins = V.bn_stats(gn_st[:, j, h, :], x_all[:, s * SLAB + j, h * HALF:(h + 1) * HALF])
                ins.then_inc(gn_stats, 1)
                wait_apart(dve, gn_stats, 2 * s + r + 1, dve_passed)
                for j in range(4 * r, 4 * r + 4):
                    ins = V.bn_aggr(gn_mv[:, j, :], gn_st[:, j, :, :].rearrange("p h k -> p (h k)"))
                ins.then_inc(gn_mv_ready, 1)

            def gn_groups(u, j0=0, n=SLAB):
                js = slice(j0, j0 + n)
                dve.wait_ge(gn_group, u + 1)
                V.tensor_copy(gn_avg[:, js, :].rearrange("p j k -> p (j k)"),
                              S[0][0:C, 0, 2 * j0:2 * (j0 + n)]).then_inc(gn_avg_ready, 1)
                dve.wait_ge(gn_avg_ready, u + 1)
                V.tensor_tensor(gn_dev[:, js], gn_mv[:, js, 0], gn_avg[:, js, 0],
                                ALU.subtract).then_inc(gn_dev_ready, 1)
                dve.wait_ge(gn_dev_ready, u + 1)
                V.tensor_tensor(gn_dev2[:, js], gn_dev[:, js], gn_dev[:, js], ALU.mult).then_inc(gn_dev2_ready, 1)
                dve.wait_ge(gn_between, u + 1)
                V.scalar_tensor_tensor(gn_var[:, js], S[0][0:C, 1, js], GN_EPS, gn_avg[:, js, 1],
                                       ALU.add, ALU.add).then_inc(gn_var_ready, 1)

            def gn_shifts(u, b0, j0=0, n=SLAB):
                dve.wait_ge(gn_rstd, u + 1)
                V.scalar_tensor_tensor(gn_shift[:, bass.ds(b0, n)], gn_avg[:, j0:j0 + n, 0], -1.0,
                                       gn_scale[:, bass.ds(b0, n)], ALU.mult, ALU.mult).then_inc(gn_coef, 1)

            steps = [0]
            TOP_STEPS = 19

            def bc(v):
                return v.rearrange("p (n a) -> p n a", a=1).to_broadcast([TOK, NS, E])

            gbv = gb[:, :].rearrange("p (a e) -> p a e", a=1).to_broadcast([TOK, NS, E])
            pref = prefer[:, :].rearrange("p (a e) -> p a e", a=1).to_broadcast([TOK, NS, E])

            def then(s, ins):
                steps[0] += 1
                ins.then_inc(top_step, 1)
                dve.wait_ge(top_step, TOP_STEPS * s + steps[0])

            def choose(s):
                def pick(onehot, value):
                    then(s, V.tensor_reduce(value, gate, AX.X, ALU.max))
                    then(s, V.tensor_tensor(work, gate, bc(value), ALU.is_equal))
                    then(s, V.tensor_tensor(work, work, pref, ALU.mult))
                    then(s, V.tensor_reduce(top[:, 3, :], work, AX.X, ALU.max))
                    then(s, V.tensor_tensor(onehot, work, bc(top[:, 3, :]), ALU.is_equal))

                steps[0] = 0
                dve.wait_ge(logits_ready, 2 * s + 2)
                then(s, V.tensor_tensor(gate, logits, gbv, ALU.add))
                then(s, V.tensor_reduce(top[:, 0, :], gate, AX.X, ALU.max))
                V.tensor_tensor(gate, gate, bc(top[:, 0, :]), ALU.subtract).then_inc(gate_exp_in, 1)
                dve.wait_ge(gate_exp, s + 1)
                then(s, V.tensor_reduce(top[:, 1, :], gate, AX.X, ALU.add))
                then(s, V.reciprocal(top[:, 0, :], top[:, 1, :]))
                then(s, V.tensor_tensor(gate, gate, bc(top[:, 0, :]), ALU.mult))
                pick(first, top[:, 0, :])
                then(s, V.scalar_tensor_tensor(gate, first, -2.0, gate, ALU.mult, ALU.add))
                pick(second, top[:, 1, :])
                for k, choice in enumerate((first, second)):
                    ins = V.tensor_reduce(present_s[:, bass.ds(s, 1), k, :].rearrange("p s e -> p (s e)"),
                                          choice.rearrange("p n e -> p e n"), AX.X, ALU.max)
                then(s, ins)

            def weigh(s):
                V.tensor_tensor(top[:, 2, :], top[:, 1, :], top[:, 0, :], ALU.subtract).then_inc(gate_exp_in, 1)
                dve.wait_ge(top_exp, s + 1)
                then(s, V.tensor_scalar(top[:, 3, :], top[:, 2, :], 1.0, None, ALU.add))
                then(s, V.reciprocal(w0[:, bass.ds(s * NS, NS)], top[:, 3, :]))
                assert steps[0] == TOP_STEPS

            gn_half(0, 0)
            gn_groups(0, 0, 4)
            gn_half(0, 1, before=(0, 0, 0, 4))
            gn_groups(1, 4, 4)
            gn_half(1, 0, before=(1, 4, 4, 4))
            dve.wait_ge(params_loaded, 16 * N_PARAMS)
            link(V.tensor_reduce(w1_max[:, :], w1_raw[:, :, :], AX.X, ALU.max, apply_absolute_value=True))
            link(V.tensor_scalar(w1_max[:, :], w1_max[:, :], W1_TINY, None, ALU.max))
            link(V.tensor_scalar(w1_unit[:, :].bitcast(I32), w1_max[:, :].bitcast(I32), F32_EXPONENT, None,
                                 ALU.bitwise_and))
            link(V.reciprocal(w1_inv[:, :], w1_unit[:, :]))
            V.tensor_tensor(w1_raw[:, :, :], w1_raw[:, :, :],
                            w1_inv[:, :].rearrange("p (t a) -> p t a", a=1).to_broadcast([P, TILES, C]),
                            ALU.mult).then_inc(w1_scaled, 1)
            V.tensor_tensor(lam_e[:, 2:4], lam[:, 0:4:2], lam[:, 1:4:2], ALU.mult).then_inc(lam_prod, 1)
            gn_half(1, 1)
            dve.wait_ge(*CONSTS_SET)
            dve.wait_ge(lam_exp, 1)
            dve.wait_ge(setup_T, 1)
            link(V.tensor_copy(w1_hi[:, :], S[2][0:C, 0, 0:HID]))
            V.tensor_tensor(w1_lo[:, :], S[2][0:C, 0, 0:HID], w1_hi[:, :], ALU.subtract)
            V.tensor_copy(w2T[:, :, :], S[2][:, 1, 0:TILES * C].rearrange("p (t c) -> p t c", c=C))
            V.tensor_scalar(wqT[:, :], S[2][0:C, 1, HID:HID + C + 1], float(HD) ** -0.5, None, ALU.mult)
            V.tensor_copy(W1f[:, :], S[3][0:C, 0, 0:HID])
            link(V.tensor_copy(W2f[:, :, :], S[3][:, 1, 0:TILES * C].rearrange("p (t c) -> p t c", c=C)))
            V.tensor_scalar(qkvw[C:C + 1, C:3 * C], qkvw[C:C + 1, C:3 * C], 1.0, None, ALU.add)
            W1v = W1f[:, 0:QGROUPS * W1_GS].rearrange("p (g n) -> p g n", n=W1_GS)
            V.tensor_reduce(wsum[0:C, 0, :], W1v, AX.X, ALU.add)
            V.tensor_reduce(wsum[:, 1, :], W2f[:, :, 0:QGROUPS * W2_GS].rearrange("p t (g n) -> p g t n", n=W2_GS),
                            AX.XY, ALU.add).then_inc(wsum_ready, 1)
            gn_groups(2)
            gn_shifts(2, SLAB)
            with dve.Fori(1, SLABS - 1) as s:
                gn_half(s + 1, 0)
                gn_half(s + 1, 1)
                choose(s - 1)
                gn_groups(s + 2)
                weigh(s - 1)
                gn_shifts(s + 2, (s + 1) * SLAB)

            V.memset(W1b[0:C, QGROUPS * W1_GS:HID], 0.0)
            V.memset(W2b[:, :, QGROUPS * W2_GS:C], 0.0)
            dve.wait_ge(wmean_sum, 1)
            V.tensor_scalar(wmean[0:C, 0, :], S[3][0:C, 0, 400:400 + QGROUPS], 1.0 / (W1_GS * C), None, ALU.mult)
            link(V.tensor_scalar(wmean[:, 1, :], S[3][:, 1, 400:400 + QGROUPS], 1.0 / (W2_GS * HID), None, ALU.mult))
            m1 = wmean[0:C, 0, :].rearrange("p (g a) -> p g a", a=1).to_broadcast([C, QGROUPS, W1_GS])
            pa = part_a[0:C, 0:QGROUPS * W1_GS].rearrange("p (g n) -> p g n", n=W1_GS)
            pb = part_b[0:C, 0:QGROUPS * W1_GS].rearrange("p (g n) -> p g n", n=W1_GS)
            V.tensor_tensor(pa, W1v, m1, ALU.is_gt)
            link(V.tensor_tensor(pb, W1v, m1, ALU.is_lt))
            link(V.tensor_tensor(W1b[0:C, 0:QGROUPS * W1_GS].rearrange("p (g n) -> p g n", n=W1_GS),
                                 pa, pb, ALU.subtract))
            m2 = wmean[:, 1, :].rearrange("p (g a) -> p g a", a=1).to_broadcast([P, QGROUPS, W2_GS])
            for t in range(TILES):
                w = W2f[:, t, 0:QGROUPS * W2_GS].rearrange("p (g n) -> p g n", n=W2_GS)
                V.tensor_tensor(part_a[:, t * C:t * C + QGROUPS * W2_GS].rearrange("p (g n) -> p g n", n=W2_GS),
                                w, m2, ALU.is_gt)
                ins = V.tensor_tensor(part_b[:, t * C:t * C + QGROUPS * W2_GS].rearrange(
                    "p (g n) -> p g n", n=W2_GS), w, m2, ALU.is_lt)
            link(ins)
            for t in range(TILES):
                n = QGROUPS * W2_GS
                ins = V.tensor_tensor(W2b[:, t, 0:n], part_a[:, t * C:t * C + n], part_b[:, t * C:t * C + n],
                                      ALU.subtract)
            link(ins)
            V.tensor_copy(W2last[:, :], W2b[:, TILES - 1, :])

            def bf16_parts(dst, src, rows, width, masks):
                a, b, h = part_a[rows, 0:width], part_b[rows, 0:width], part_h[rows, 0:width]
                link(V.tensor_copy(h, src))
                link(V.tensor_scalar(a, h, masks[:, 0:1], None, ALU.mult))
                link(V.tensor_tensor(b, src, h, ALU.subtract))
                link(V.tensor_copy(h, b))
                link(V.scalar_tensor_tensor(a, h, masks[:, 1:2], a, ALU.mult, ALU.add))
                link(V.tensor_tensor(b, b, h, ALU.subtract))
                link(V.scalar_tensor_tensor(dst, b, masks[:, 2:3], a, ALU.mult, ALU.add))

            rows = slice(C, C + PARTS)
            bf16_parts(W1b[rows, :], fb1r[rows, :], rows, HID, con[rows, K_PART96:K_PART96 + PARTS])
            rows = slice(0, B_ROWS)
            bf16_parts(b2_parts[:, :], b2r[:, :], rows, C, con[rows, K_PART:K_PART + PARTS])
            link(V.tensor_tensor(lam_e[:, 2:3], lam_e[:, 0:1], lam_e[:, 1:2], ALU.subtract))
            link(V.tensor_scalar(lam_e[:, 3:4], lam_e[:, 2:3], LAMBDA_INIT, None, ALU.add))
            link(V.tensor_scalar(lam_e[:, 2:3], lam_e[:, 3:4], -1.0, 1.0, ALU.mult, ALU.add))
            V.tensor_scalar(gauss[:, :], con[0:C, K_GAUSS:K_GAUSS + C], lam_e[:, 2:3], None,
                            ALU.mult).then_inc(fold_in, 1)

            choose(SLABS - 2)
            weigh(SLABS - 2)
            choose(SLABS - 1)
            V.tensor_reduce(present[:, :, :].rearrange("p k e -> p (k e)"),
                            present_s[:, :, :, :].rearrange("p s k e -> p (k e) s"),
                            AX.X, ALU.max).then_inc(present_ready, 1)
            dve.wait_ge(counts_ready, 1)
            link(V.tensor_scalar(flags[:, :, :].rearrange("p k e -> p (k e)"), S[3][:, 0, 0:2 * E], 1.0, None, ALU.min))
            link(V.tensor_tensor(flags[:, 0, :], flags[:, 0, :], flags[:, 1, :], ALU.subtract))
            expert = con[:, K_EXPERT:K_EXPERT + (TILES + 1) * E].rearrange("p (t e) -> p t e", e=E)
            for v in range(2):
                fl = flags[:, v, :].rearrange("p (a e) -> p a e", a=1).to_broadcast([P, TILES + 1, E])
                link(V.tensor_tensor(flag_tmp[:, :, :], expert, fl, ALU.mult))
                link(V.tensor_reduce(row_flag[:, v, :], flag_tmp[:, :, :], AX.X, ALU.add))
            for v in range(2):
                V.tensor_tensor(w2s[:, v, :, :], w2T[:, :, :],
                                row_flag[:, v, 0:TILES].rearrange("p (t a) -> p t a", a=1).to_broadcast([P, TILES, C]),
                                ALU.mult)
                V.tensor_scalar(bias2_parts[:, v, :], b2_parts[:, :], row_flag[0:B_ROWS, v, TILES:TILES + 1],
                                None, ALU.mult)
            link(V.tensor_reduce(differ_f[:, :], flags[0:1, 0, :], AX.X, ALU.max, apply_absolute_value=True))
            V.tensor_copy(differ[:, :], differ_f[:, :]).then_inc(conv_ready, 1)
            dve.wait_ge(conv_ready, 1)
            weigh(SLABS - 1)
            mixed = dve.value_load(differ[0:1, 0:1], min_val=0, max_val=1)

            def mask_a(i, k):
                dve.wait_ge(a_ready, i)
                V.tensor_tensor(Am[:, :], S[k][0:C, 0, 0:C], gauss[:, :], ALU.mult).then_inc(am_ready, 1)

            def chunk_stats(src, chunks_):
                for j in chunks_:
                    ins = V.bn_stats(ln_st[:, j, :], src[:, j, :])
                return ins

            def stats(n, src, count, j0=0):
                chunk_stats(src, range(j0, CHUNKS)).then_inc(ln_stats, 1)
                wait_apart(dve, ln_stats, count, dve_passed)
                for j in range(CHUNKS):
                    ins = V.bn_aggr(ln_mv[n][:, j, :], ln_st[:, j, :])
                ins.then_inc(ln_mean[n], 1)

            def apply(n, src, dst, b, done):
                dve.wait_ge(ln_rstd[n], b + 1)
                for j in range(CHUNKS):
                    ins = V.tensor_scalar(dst[:, j, :], src[:, j, :], ln_mv[n][:, j, 0:1], ln_rs[n][:, j:j + 1],
                                          ALU.subtract, ALU.mult)
                ins.then_inc(done, 1)

            def absmax(f, t, k):
                dve.wait_ge(y_ready, 3 * f + t + 1)
                V.tensor_reduce(ymax[:, bass.ds(3 * f + t, 1)], halves(k, P), AX.XY, ALU.max,
                                apply_absolute_value=True).then_inc(ymax_done, 1)

            def y1_max():
                dve.wait_ge(ymax_done, 3 * QIMAGES)
                V.tensor_reduce(gmax1[:, :], ymax[:, :].rearrange("p (g n) -> p g n", g=QGROUPS), AX.X,
                                ALU.max).then_inc(gmax_ready, 1)

            def y1_max_diagonal():
                dve.wait_ge(gmaxT, 1)
                link(V.tensor_reduce(gcol[:, :], S[2][0:QGROUPS, 0, 0:P], AX.X, ALU.max))
                V.tensor_scalar(gdiag[:, :], ident[0:QGROUPS, 0:QGROUPS], gcol[:, 0:1], None,
                                ALU.mult).then_inc(gdiag_ready, 1)

            def y1_scale():
                dve.wait_ge(gbc, 1)
                link(V.tensor_scalar(s1e[:, :], S[2][:, 1, 0:QGROUPS], Q_EPS, 1.0 / QMAX, ALU.add, ALU.mult))
                V.reciprocal(s1[:, :], s1e[:, :]).then_inc(s1_ready, 1)

            def step(m, r, experts=True, attend=True, out_=True, ffn=True, scales=False):
                i = 2 * m + r
                a, f = i - 1, i - 2
                one, other = one_other(r)

                def feature_map(q, k, j0, n):
                    dve.wait_ge(e_ready, 2 * a + q + 1)
                    V.scalar_tensor_tensor(fkv[:, j0:j0 + n, :], ekv[:, j0:j0 + n, :], 1.0,
                                           chunks(k, n, 256, 2 * C), ALU.min, ALU.max).then_inc(f_ready, 1)

                first_part, rest = slice(0, CH_A), slice(CH_A, CHUNKS)
                yx = chunks(2, CHUNKS, P, C)
                if scales:
                    y1_max()
                if attend:
                    feature_map(0, other, 0, CH_A)
                if experts:
                    with dve.If(mixed):
                        dve.sem_inc(dve_passed, 1)
                        if attend:
                            feature_map(1, 0, CH_A, CHUNKS - CH_A)
                    with dve.Else():
                        dve.wait_ge(yx_part, i + 1)
                        V.tensor_copy(t1[r][:, first_part, :], yx[:, first_part, :]).then_inc(t1_part, 1)
                        if attend:
                            feature_map(1, 0, CH_A, CHUNKS - CH_A)
                        dve.wait_ge(t1_part, i + 1)
                        chunk_stats(t1[r], range(CH_A))
                elif attend:
                    feature_map(1, 0, CH_A, CHUNKS - CH_A)
                if scales:
                    y1_max_diagonal()
                if out_ and ffn:
                    dve.wait_ge(hi_ready, f + 1)
                    V.tensor_tensor(big[0:C, f, 1, :].rearrange("p (j t) -> p j t", t=TOK),
                                    flat(other)[0:C, 0:CHUNKS * P].rearrange("p (j t) -> p j t", t=P)[:, :, 0:TOK],
                                    big[0:C, f, 0, :].rearrange("p (j t) -> p j t", t=TOK),
                                    ALU.subtract).then_inc(lo_ready, 1)
                if experts:
                    wv = w0[:, bass.ds(i * CHUNKS, CHUNKS)].rearrange("p (n a) -> p n a", a=1).to_broadcast(
                        [TOK, CHUNKS, C])
                    with dve.If(mixed):
                        dve.wait_ge(d_ready, i + 1)
                        V.tensor_tensor(tmp[:, :, :], chunks(0, CHUNKS, P, C), wv, ALU.mult).then_inc(tmp_ready, 1)
                        dve.wait_ge(yx_ready, i + 1)
                        dve.wait_ge(tmp_ready, i + 1)
                        V.tensor_tensor(t1[r][:, :, :], tmp[:, :, :], yx, ALU.add).then_inc(t1_part, 1)
                        dve.wait_ge(t1_part, i + 1)
                        chunk_stats(t1[r], range(CH_A)).then_inc(t1_ready, 1)
                    with dve.Else():
                        dve.wait_ge(yx_ready, i + 1)
                        V.tensor_copy(t1[r][:, rest, :], yx[:, rest, :]).then_inc(t1_ready, 1)
                    dve.wait_ge(t1_ready, i + 1)
                if attend:
                    mask_a(i, one)
                if scales:
                    y1_scale()
                if experts:
                    stats(0, t1[r], 1 if isinstance(i, int) and i == 0 else 2 * i, CH_A)
                if out_ and ffn:
                    for t, k in ((0, 0), (2, other), (1, 2)):
                        absmax(f, t, k)
                if experts:
                    apply(0, t1[r], xh1, i, xh1_ready)
                if attend:
                    dve.wait_ge(ao_ready, i)
                    V.tensor_tensor(t2[:, :, :], t1[1 - r][:, :, :], chunks(one, CHUNKS, P, C),
                                    ALU.add).then_inc(t2_ready, 1)
                if attend and not (isinstance(i, int) and i - 1 >= QIMAGES):
                    dve.wait_ge(t2_ready, i)
                    stats(1, t2, 2 * i + 1)
                    apply(1, t2, xh2, a, xh2_ready)

            for i in range(FIRST):
                step(i // 2, i % 2, attend=i >= 1, out_=i >= 2)
            with dve.Fori(FIRST // 2, LAST // 2 - 1) as m:
                for r in range(2):
                    step(m, r)
            for r in range(2):
                step(LAST // 2 - 1, r)
            step(LAST // 2, 0, experts=False, ffn=False, scales=True)

            def split(m, r):
                b = 2 * m + r
                for t in range(SPLIT):
                    dve.wait_ge(hi_parts, SPLIT * b + t + 1)
                    V.scalar_tensor_tensor(h_lo[r][:, t, :], gel[:, t, :], Q_CLIP, h_hi[r][:, t, :],
                                           ALU.min, ALU.subtract).then_inc(parts_ready, 1)
                dve.wait_ge(gelu_ready, 3 * b + 3)
                V.tensor_scalar(h_last[r][:, :], gel[:, 2, :], Q_CLIP, None, ALU.min).then_inc(parts_ready, 1)

            def y2_absmax(b):
                dve.wait_ge(y2_evac, b + 1)
                V.tensor_reduce(y2max[:, bass.ds(b, 1)], y2_all[:, b, :], AX.X, ALU.max,
                                apply_absolute_value=True).then_inc(y2max_done, 1)

            def group_max(g):
                dve.wait_ge(y2max_done, (g + 1) * QB)
                V.tensor_reduce(gmax2[:, :], y2max[:, bass.ds(g * QB, QB)], AX.X, ALU.max).then_inc(g2_ready, 1)

            def group_scale(g):
                dve.wait_ge(g2T, g + 1)
                V.tensor_reduce(g2one[:, :], S[3][0:1, 0, 400:400 + C], AX.X, ALU.max).then_inc(g2one_ready, 1)
                dve.wait_ge(g2bc, g + 1)
                V.tensor_scalar(s2e[:, :], S[3][0:C, 1, 400:401], Q_EPS, 1.0 / QMAX,
                                ALU.add, ALU.mult).then_inc(s2e_ready, 1)
                dve.wait_ge(s2e_ready, g + 1)
                V.reciprocal(s2[:, bass.ds(g, 1)], s2e[:, :]).then_inc(s2_ready, 1)

            def clipped(g, m, r):
                b = 2 * m + r
                dve.wait_ge(s2_ready, g + 1)
                wait_count(dve, o_ready, b - 1)
                V.tensor_scalar(qv[r][:, :], y2_all[:, b, :], s2[:, bass.ds(g, 1)], Q_CLIP,
                                ALU.mult, ALU.min).then_inc(qv_ready, 1)
                dve.wait_ge(qv_ready, b + 1)
                V.tensor_scalar(qv[r][:, :], qv[r][:, :], -Q_CLIP, None, ALU.max).then_inc(qc_ready, 1)

            def ffn_pair(m, g=None, scale=False, first=False):
                for r in range(2):
                    split(m, r)
                    if scale and r == 1:
                        group_scale(g - 1)
                    if not (first and r == 0):
                        y2_absmax(2 * m + r - 1)
                    if scale and r == 0:
                        group_max(g - 1)
                    if g is not None:
                        for n in ((), (0, 1))[r] if scale else (r,):
                            clipped(g - 1, m - QB // 2, n)

            ffn_pair(0, first=True)
            with dve.Fori(1, QB // 2) as q:
                ffn_pair(q)
            ffn_pair(QB // 2, g=1, scale=True)
            with dve.Fori(1, QB // 2) as q:
                ffn_pair(QB // 2 + q, g=1)
            with dve.Fori(2, QGROUPS) as g:
                ffn_pair(g * (QB // 2), g=g, scale=True)
                with dve.Fori(1, QB // 2) as q:
                    ffn_pair(g * (QB // 2) + q, g=g)
            y2_absmax(QIMAGES - 1)
            group_max(QGROUPS - 1)
            group_scale(QGROUPS - 1)
            dve.wait_ge(s2_ready, QGROUPS)
            dve.wait_ge(tail_loaded, 16)
            for j in range(QB):
                y2 = y2_all[:, QIMAGES - QB + j, :]
                V.tensor_scalar(y2, y2, s2[:, QGROUPS - 1:QGROUPS], Q_CLIP, ALU.mult, ALU.min).then_inc(tail_clip, 1)
                dve.wait_ge(tail_clip, j + 1)
                V.scalar_tensor_tensor(t2_tail[:, j, :], y2, -Q_CLIP, t2_tail[:, j, :],
                                       ALU.max, ALU.add).then_inc(tail_ready, 1)


_INS = ['x', 'L0_conv_gate_w', 'L0_conv_gate_b', 'L0_conv_w1', 'L0_conv_b1', 'L0_conv_w2', 'L0_conv_b2',
        'L1_attn_qkv_w', 'L1_attn_qkv_b', 'L1_attn_proj_w', 'L1_attn_proj_b', 'L1_attn_lambda_k1',
        'L1_attn_lambda_v1', 'L1_attn_lambda_k2', 'L1_attn_lambda_v2', 'L1_ffn_W1', 'L1_ffn_b1',
        'L1_ffn_W2', 'L1_ffn_b2']


def kernel(**inputs):
    import concourse.bacc as _bacc
    from concourse.bass_utils import run_bass_kernel_spmd as _run

    nc = _bacc.Bacc("TRN2", target_bir_lowering=False, num_devices=1)
    arrays, args = {}, []
    for name in _INS:
        a = np.ascontiguousarray(inputs[name])
        arrays[f"in_{name}"] = a
        args.append(nc.dram_tensor(f"in_{name}", a.shape, mybir.dt.from_np(a.dtype), kind="ExternalInput").ap())
    k = shape_constants()
    arrays["shape_consts"] = k
    args.append(nc.dram_tensor("shape_consts", k.shape, F32, kind="ExternalInput").ap())
    args.append(nc.dram_tensor("out", (BATCH, C, 28, 28), F32, kind="ExternalOutput").ap())
    build(nc, *args)
    r = _run(nc, [arrays], core_ids=[0])
    return r.results[0]["out"]
```
